# Optimizing a Trainium2 kernel written in Bass

```python
import numpy as np
import jax
import jax.numpy as jnp

def _softmax(x, axis=-1):
    return jax.nn.softmax(x, axis=axis)

def _gelu(x):
    return jax.nn.gelu(x, approximate=True)

def _silu(x):
    return jax.nn.silu(x)

def _sigmoid(x):
    return jax.nn.sigmoid(x)

def _layernorm(x, axis=-1, eps=1e-05):
    m = jnp.mean(x, axis=axis, keepdims=True)
    v = jnp.var(x, axis=axis, keepdims=True)
    return (x - m) / jnp.sqrt(v + eps)

def _scatter_add(tgt, idx, src, axis=0):
    return tgt.at[idx].add(src)

def _segment_sum(src, seg, n):
    return jax.ops.segment_sum(src, seg, n)
kernel_name = 'mk_sandwich_d2_jaxref_r8_a190e8'

def setup_inputs(seed: int=0):
    np.random.seed(seed)
    _w = jnp.asarray

    def _L0_attn_setup():
        import jax, jax.numpy as jnp
        import numpy as np
        NUM_HEADS = 1
        LN_EPS = 1e-05
        key = jax.random.key(seed)
        ks = jax.random.split(key, 4)
        B, L, D = (8, 512, 128)
        x = jax.random.normal(ks[0], (B, L, D), dtype=jnp.float32)
        qkv_w = jax.random.normal(ks[1], (3 * D, D), dtype=jnp.float32) * np.float32(np.sqrt(1.0 / D))
        qkv_b = jnp.zeros((3 * D,), dtype=jnp.float32)
        proj_w = jax.random.normal(ks[2], (D, D), dtype=jnp.float32) * np.float32(np.sqrt(1.0 / D))
        proj_b = jnp.zeros((D,), dtype=jnp.float32)
        return {'x': x, 'norm_w': jnp.ones((D,), dtype=jnp.float32), 'norm_b': jnp.zeros((D,), dtype=jnp.float32), 'qkv_w': qkv_w, 'qkv_b': qkv_b, 'proj_w': proj_w, 'proj_b': proj_b}
    _L0_attn_in = _L0_attn_setup()

    def _L0_ffn_setup():
        import jax, jax.numpy as jnp
        import numpy as np
        EPS = 1e-08

        def _ternary_linear(x, w):
            alpha = jnp.mean(jnp.abs(w))
            w_t = jnp.sign(w) * (jnp.abs(w) > 0.5 * alpha).astype(w.dtype)
            w_q = w + jax.lax.stop_gradient(w_t - w)
            d = x.shape[-1]
            rms = jnp.sqrt(jnp.sum(x * x, axis=-1, keepdims=True)) / jnp.sqrt(jnp.asarray(d, x.dtype))
            x_norm = x / (rms + EPS)
            return jnp.einsum('bsd,fd->bsf', x_norm, w_q)
        key = jax.random.key(seed)
        k1, k2, k3 = jax.random.split(key, 3)
        d_model, d_ff = (128, 512)
        B, S = (4, 512)
        x = jax.random.normal(k1, (B, S, d_model), dtype=jnp.float32)
        w_up = jax.random.normal(k2, (d_ff, d_model), dtype=jnp.float32) * 0.02
        w_down = jax.random.normal(k3, (d_model, d_ff), dtype=jnp.float32) * 0.02
        return {'x': x, 'w_up': w_up, 'w_down': w_down}
    _L0_ffn_in = _L0_ffn_setup()

    def _L1_attn_setup():
        import jax, jax.numpy as jnp
        import numpy as np
        HIDDEN = 128
        HEADS = 16
        HEAD_DIM = HIDDEN // HEADS
        ROPE_BASE = 10000.0

        def _rope_cos_sin(seq_len, dim):
            inv_freq = 1.0 / ROPE_BASE ** (jnp.arange(0, dim, 2, dtype=jnp.float32) / dim)
            t = jnp.arange(seq_len, dtype=jnp.float32)
            freqs = jnp.einsum('i,j->ij', t, inv_freq)
            emb = jnp.concatenate([freqs, freqs], axis=-1)
            return (jnp.cos(emb), jnp.sin(emb))

        def _apply_rope(x, cos, sin):
            x1, x2 = (x[..., 0::2], x[..., 1::2])
            c = cos[..., :x1.shape[-1]]
            s = sin[..., :x1.shape[-1]]
            return jnp.concatenate([x1 * c - x2 * s, x1 * s + x2 * c], axis=-1)
        key = jax.random.key(seed)
        ks = jax.random.split(key, 9)
        B, S = (4, 256)
        lim = 1.0 / np.sqrt(HIDDEN)

        def lin(kw, kb):
            W = jax.random.uniform(kw, (HIDDEN, HIDDEN), jnp.float32, -lim, lim)
            b = jax.random.uniform(kb, (HIDDEN,), jnp.float32, -lim, lim)
            return (W, b)
        Wq, bq = lin(ks[0], ks[1])
        Wk, bk = lin(ks[2], ks[3])
        Wv, bv = lin(ks[4], ks[5])
        Wo, bo = lin(ks[6], ks[7])
        x = jax.random.normal(ks[8], (B, S, HIDDEN), jnp.float32)
        return {'x': x, 'Wq': Wq, 'bq': bq, 'Wk': Wk, 'bk': bk, 'Wv': Wv, 'bv': bv, 'Wo': Wo, 'bo': bo}
    _L1_attn_in = _L1_attn_setup()

    def _L1_ffn_setup():
        import math
        import jax, jax.numpy as jnp
        import numpy as np
        E = 24

        def layer_norm(x, w, b, eps=1e-06):
            m = x.mean(-1, keepdims=True)
            v = x.var(-1, keepdims=True)
            return (x - m) / jnp.sqrt(v + eps) * w + b

        def top2_dispatch(x, Wg, C):
            logits = x @ Wg
            gates = jax.nn.softmax(logits, axis=-1)
            idx1 = jnp.argmax(gates, axis=-1)
            m1 = jax.nn.one_hot(idx1, E, dtype=x.dtype)
            masked = jnp.where(m1 > 0, -jnp.inf, logits)
            idx2 = jnp.argmax(masked, axis=-1)
            m2 = jax.nn.one_hot(idx2, E, dtype=x.dtype)
            loc1 = jnp.cumsum(m1, axis=0) - m1
            loc2 = jnp.cumsum(m2, axis=0) - m2 + jnp.sum(m1, axis=0, keepdims=True)
            m1 = m1 * (loc1 < C)
            m2 = m2 * (loc2 < C)
            g1 = jnp.sum(gates * m1, axis=-1)
            g2 = jnp.sum(gates * m2, axis=-1)
            denom = jnp.maximum(g1 + g2, 1e-09)
            g1, g2 = (g1 / denom, g2 / denom)
            p1 = jnp.sum(loc1 * m1, axis=-1).astype(jnp.int32)
            p2 = jnp.sum(loc2 * m2, axis=-1).astype(jnp.int32)
            c1 = g1[:, None, None] * m1[:, :, None] * jax.nn.one_hot(p1, C, dtype=x.dtype)[:, None, :]
            c2 = g2[:, None, None] * m2[:, :, None] * jax.nn.one_hot(p2, C, dtype=x.dtype)[:, None, :]
            combine = c1 + c2
            dispatch = (combine > 0).astype(x.dtype)
            return (combine, dispatch)

        def moe_apply(x, combine, dispatch, W, b):
            disp = jnp.einsum('sec,sd->ecd', dispatch, x)
            h = jnp.einsum('ecd,edf->ecf', disp, W) + b[:, None, :]
            return jnp.einsum('sec,ecf->sf', combine, h)
        b, seq, d_in, d_hid = (4, 256, 128, 512)
        ks = jax.random.split(jax.random.key(seed), 6)
        s = 0.02
        return {'x': jax.random.normal(ks[0], (b, seq, d_in), dtype=jnp.float32), 'Wg': jax.random.normal(ks[1], (d_in, E), dtype=jnp.float32) * s, 'W1': jax.random.normal(ks[2], (E, d_in, d_hid), dtype=jnp.float32) * s, 'b1': jnp.zeros((E, d_hid), dtype=jnp.float32), 'W2': jax.random.normal(ks[3], (E, d_hid, d_in), dtype=jnp.float32) * s, 'b2': jnp.zeros((E, d_in), dtype=jnp.float32), 'ln_hid_w': jnp.ones((4, d_hid), dtype=jnp.float32), 'ln_hid_b': jnp.zeros((4, d_hid), dtype=jnp.float32), 'ln_out_w': jnp.ones((d_in,), dtype=jnp.float32), 'ln_out_b': jnp.zeros((d_in,), dtype=jnp.float32)}
    _L1_ffn_in = _L1_ffn_setup()
    _d = {'L0_attn_x': _L0_attn_in['x'], 'L0_attn_norm_w': _L0_attn_in['norm_w'], 'L0_attn_norm_b': _L0_attn_in['norm_b'], 'L0_attn_qkv_w': _L0_attn_in['qkv_w'], 'L0_attn_qkv_b': _L0_attn_in['qkv_b'], 'L0_attn_proj_w': _L0_attn_in['proj_w'], 'L0_attn_proj_b': _L0_attn_in['proj_b'], 'L0_ffn_w_up': _L0_ffn_in['w_up'], 'L0_ffn_w_down': _L0_ffn_in['w_down'], 'L1_attn_Wq': _L1_attn_in['Wq'], 'L1_attn_bq': _L1_attn_in['bq'], 'L1_attn_Wk': _L1_attn_in['Wk'], 'L1_attn_bk': _L1_attn_in['bk'], 'L1_attn_Wv': _L1_attn_in['Wv'], 'L1_attn_bv': _L1_attn_in['bv'], 'L1_attn_Wo': _L1_attn_in['Wo'], 'L1_attn_bo': _L1_attn_in['bo'], 'L1_ffn_Wg': _L1_ffn_in['Wg'], 'L1_ffn_W1': _L1_ffn_in['W1'], 'L1_ffn_b1': _L1_ffn_in['b1'], 'L1_ffn_W2': _L1_ffn_in['W2'], 'L1_ffn_b2': _L1_ffn_in['b2'], 'L1_ffn_ln_hid_w': _L1_ffn_in['ln_hid_w'], 'L1_ffn_ln_hid_b': _L1_ffn_in['ln_hid_b'], 'L1_ffn_ln_out_w': _L1_ffn_in['ln_out_w'], 'L1_ffn_ln_out_b': _L1_ffn_in['ln_out_b']}
    _x0 = _d['L0_attn_x']
    _d['L0_attn_x'] = jax.random.normal(jax.random.fold_in(jax.random.key(seed), 1), (4, 1024, 128), dtype=_x0.dtype)
    del _x0
    return _d

def reference(L0_attn_x, L0_attn_norm_w, L0_attn_norm_b, L0_attn_qkv_w, L0_attn_qkv_b, L0_attn_proj_w, L0_attn_proj_b, L0_ffn_w_up, L0_ffn_w_down, L1_attn_Wq, L1_attn_bq, L1_attn_Wk, L1_attn_bk, L1_attn_Wv, L1_attn_bv, L1_attn_Wo, L1_attn_bo, L1_ffn_Wg, L1_ffn_W1, L1_ffn_b1, L1_ffn_W2, L1_ffn_b2, L1_ffn_ln_hid_w, L1_ffn_ln_hid_b, L1_ffn_ln_out_w, L1_ffn_ln_out_b):

    def _L0_attn_ref(x, norm_w, norm_b, qkv_w, qkv_b, proj_w, proj_b):
        import jax, jax.numpy as jnp
        import numpy as np
        NUM_HEADS = 1
        LN_EPS = 1e-05
        B, L, D = x.shape
        H = NUM_HEADS
        mu = jnp.mean(x, axis=-1, keepdims=True)
        var = jnp.mean(jnp.square(x - mu), axis=-1, keepdims=True)
        h = (x - mu) / jnp.sqrt(var + LN_EPS) * norm_w + norm_b
        qkv = h @ qkv_w.T + qkv_b
        qkv = qkv.reshape(B * H, L // H, 3, D)
        q, k, v = (qkv[..., 0, :], qkv[..., 1, :], qkv[..., 2, :])
        scale = np.float32(1.0 / np.sqrt(L // H))
        w = jax.nn.softmax(jnp.einsum('ncq,nck->nqk', q, k * scale), axis=2)
        a = jnp.einsum('nqk,nck->ncq', w, v)
        a = a.reshape(B, L, D)
        return a @ proj_w.T + proj_b + x

    def _L0_ffn_ref(x, w_up, w_down):
        import jax, jax.numpy as jnp
        import numpy as np
        EPS = 1e-08

        def _ternary_linear(x, w):
            alpha = jnp.mean(jnp.abs(w))
            w_t = jnp.sign(w) * (jnp.abs(w) > 0.5 * alpha).astype(w.dtype)
            w_q = w + jax.lax.stop_gradient(w_t - w)
            d = x.shape[-1]
            rms = jnp.sqrt(jnp.sum(x * x, axis=-1, keepdims=True)) / jnp.sqrt(jnp.asarray(d, x.dtype))
            x_norm = x / (rms + EPS)
            return jnp.einsum('bsd,fd->bsf', x_norm, w_q)
        h = jax.nn.gelu(_ternary_linear(x, w_up), approximate=False)
        return _ternary_linear(h, w_down)

    def _L1_attn_ref(x, Wq, bq, Wk, bk, Wv, bv, Wo, bo):
        import jax, jax.numpy as jnp
        import numpy as np
        HIDDEN = 128
        HEADS = 16
        HEAD_DIM = HIDDEN // HEADS
        ROPE_BASE = 10000.0

        def _rope_cos_sin(seq_len, dim):
            inv_freq = 1.0 / ROPE_BASE ** (jnp.arange(0, dim, 2, dtype=jnp.float32) / dim)
            t = jnp.arange(seq_len, dtype=jnp.float32)
            freqs = jnp.einsum('i,j->ij', t, inv_freq)
            emb = jnp.concatenate([freqs, freqs], axis=-1)
            return (jnp.cos(emb), jnp.sin(emb))

        def _apply_rope(x, cos, sin):
            x1, x2 = (x[..., 0::2], x[..., 1::2])
            c = cos[..., :x1.shape[-1]]
            s = sin[..., :x1.shape[-1]]
            return jnp.concatenate([x1 * c - x2 * s, x1 * s + x2 * c], axis=-1)
        B, S, _ = x.shape
        scale = HEAD_DIM ** (-0.5)

        def proj(W, b):
            y = jnp.einsum('bsd,ed->bse', x, W) + b
            return y.reshape(B, S, HEADS, HEAD_DIM).transpose(0, 2, 1, 3)
        q = proj(Wq, bq)
        k = proj(Wk, bk)
        v = proj(Wv, bv)
        cos, sin = _rope_cos_sin(S, HEAD_DIM)
        cos = cos[None, None]
        sin = sin[None, None]
        q = _apply_rope(q, cos, sin) * scale
        k = _apply_rope(k, cos, sin)
        attn = jnp.einsum('bhsd,bhtd->bhst', q, k)
        attn = jax.nn.softmax(attn, axis=-1)
        out = jnp.einsum('bhst,bhtd->bhsd', attn, v)
        out = out.transpose(0, 2, 1, 3).reshape(B, S, HIDDEN)
        return jnp.einsum('bsd,ed->bse', out, Wo) + bo

    def _L1_ffn_ref(x, Wg, W1, b1, W2, b2, ln_hid_w, ln_hid_b, ln_out_w, ln_out_b):
        import math
        import jax, jax.numpy as jnp
        import numpy as np
        E = 24

        def layer_norm(x, w, b, eps=1e-06):
            m = x.mean(-1, keepdims=True)
            v = x.var(-1, keepdims=True)
            return (x - m) / jnp.sqrt(v + eps) * w + b

        def top2_dispatch(x, Wg, C):
            logits = x @ Wg
            gates = jax.nn.softmax(logits, axis=-1)
            idx1 = jnp.argmax(gates, axis=-1)
            m1 = jax.nn.one_hot(idx1, E, dtype=x.dtype)
            masked = jnp.where(m1 > 0, -jnp.inf, logits)
            idx2 = jnp.argmax(masked, axis=-1)
            m2 = jax.nn.one_hot(idx2, E, dtype=x.dtype)
            loc1 = jnp.cumsum(m1, axis=0) - m1
            loc2 = jnp.cumsum(m2, axis=0) - m2 + jnp.sum(m1, axis=0, keepdims=True)
            m1 = m1 * (loc1 < C)
            m2 = m2 * (loc2 < C)
            g1 = jnp.sum(gates * m1, axis=-1)
            g2 = jnp.sum(gates * m2, axis=-1)
            denom = jnp.maximum(g1 + g2, 1e-09)
            g1, g2 = (g1 / denom, g2 / denom)
            p1 = jnp.sum(loc1 * m1, axis=-1).astype(jnp.int32)
            p2 = jnp.sum(loc2 * m2, axis=-1).astype(jnp.int32)
            c1 = g1[:, None, None] * m1[:, :, None] * jax.nn.one_hot(p1, C, dtype=x.dtype)[:, None, :]
            c2 = g2[:, None, None] * m2[:, :, None] * jax.nn.one_hot(p2, C, dtype=x.dtype)[:, None, :]
            combine = c1 + c2
            dispatch = (combine > 0).astype(x.dtype)
            return (combine, dispatch)

        def moe_apply(x, combine, dispatch, W, b):
            disp = jnp.einsum('sec,sd->ecd', dispatch, x)
            h = jnp.einsum('ecd,edf->ecf', disp, W) + b[:, None, :]
            return jnp.einsum('sec,ecf->sf', combine, h)
        bsz, seq, d = x.shape
        H = 4
        n = seq // H
        S = bsz * n
        C = math.ceil(2 * S / E)
        xg = x.reshape(bsz, H, n, d).transpose(1, 0, 2, 3).reshape(H, S, d)

        def per_group(xf, lw, lb):
            combine, dispatch = top2_dispatch(xf, Wg, C)
            h = moe_apply(xf, combine, dispatch, W1, b1)
            h = layer_norm(h, lw, lb)
            h = jax.nn.relu(h)
            return moe_apply(h, combine, dispatch, W2, b2)
        out = jax.vmap(per_group)(xg, ln_hid_w, ln_hid_b)
        out = out.reshape(H, bsz, n, d).transpose(1, 0, 2, 3).reshape(bsz, seq, d)
        return layer_norm(out + x, ln_out_w, ln_out_b)
    x = L0_attn_x
    x = x + _layernorm(_L0_attn_ref(_layernorm(x, axis=-1), L0_attn_norm_w, L0_attn_norm_b, L0_attn_qkv_w, L0_attn_qkv_b, L0_attn_proj_w, L0_attn_proj_b), axis=-1)
    x = x + _layernorm(_L0_ffn_ref(_layernorm(x, axis=-1), L0_ffn_w_up, L0_ffn_w_down), axis=-1)
    x = x + _layernorm(_L1_attn_ref(_layernorm(x, axis=-1), L1_attn_Wq, L1_attn_bq, L1_attn_Wk, L1_attn_bk, L1_attn_Wv, L1_attn_bv, L1_attn_Wo, L1_attn_bo), axis=-1)
    x = x + _layernorm(_L1_ffn_ref(_layernorm(x, axis=-1), L1_ffn_Wg, L1_ffn_W1, L1_ffn_b1, L1_ffn_W2, L1_ffn_b2, L1_ffn_ln_hid_w, L1_ffn_ln_hid_b, L1_ffn_ln_out_w, L1_ffn_ln_out_b), axis=-1)
    return x

_drawn_inputs = setup_inputs


def setup_inputs(seed=0):
    import zlib

    import numpy as np

    out = dict(_drawn_inputs(seed))
    spreads = {'L0_attn_norm_w': (1.0, 0.2),
     'L0_attn_norm_b': (0.0, 0.1),
     'L0_attn_qkv_b': (0.0, 0.1),
     'L0_attn_proj_b': (0.0, 0.1),
     'L1_ffn_b1': (0.0, 0.1),
     'L1_ffn_b2': (0.0, 0.332),
     'L1_ffn_ln_hid_w': (1.0, 0.6),
     'L1_ffn_ln_hid_b': (0.0, 0.8),
     'L1_ffn_ln_out_w': (1.0, 0.2),
     'L1_ffn_ln_out_b': (0.0, 0.1)}
    factors = {'L1_attn_bq': 8.0, 'L1_attn_bk': 8.0}
    for name, (base, spread) in spreads.items():
        noise = np.random.default_rng([zlib.crc32(name.encode()), seed]).standard_normal(out[name].shape)
        drawn = base * np.exp(spread * noise) if base else spread * noise
        out[name] = jnp.asarray(drawn.astype(out[name].dtype))
    for name, factor in factors.items():
        out[name] = (out[name] * factor).astype(out[name].dtype)
    return out
```

```python
from contextlib import ExitStack

import numpy as np
import concourse.bass as bass
from concourse import mybir

F32 = mybir.dt.float32
BF16 = mybir.dt.bfloat16
I32 = mybir.dt.int32
ALU = mybir.AluOpType
ACT = mybir.ActivationFunctionType
AX = mybir.AxisListType

P = 128
B, L, D = 4, 1024, 128
T = B * L // P
TB = L // P
FF = 512
FC = FF // P
CH = 512
NCH = B * L // CH
EPS = 1e-5
HEADS, HD = 16, 8
NQ = HEADS // 4


class Chain:

    def __init__(self, engine, sem):
        self.engine, self.sem, self.n = engine, sem, 0

    def mark(self, op):
        op.then_inc(self.sem, 1)
        self.n += 1
        return op

    def wait(self):
        self.engine.wait_ge(self.sem, self.n)

    def run(self, op):
        self.mark(op)
        self.wait()


def stats_of(nc, chain, src, st, nt):
    for t in range(nt):
        chain.mark(nc.vector.bn_stats(st[:, t, :], src[:, t, :]))
    chain.wait()


def finish_stats(nc, chain, st, mean, vn, t1, t2, n=D):
    chain.mark(nc.vector.tensor_tensor(t1, st[:, :, 1], st[:, :, 4], ALU.add))
    chain.mark(nc.vector.tensor_tensor(t2, st[:, :, 1], st[:, :, 4], ALU.subtract))
    chain.run(nc.vector.tensor_tensor(vn, st[:, :, 2], st[:, :, 5], ALU.add))
    chain.mark(nc.vector.tensor_scalar(mean, t1, 0.5, None, ALU.mult))
    chain.run(nc.vector.tensor_tensor(t2, t2, t2, ALU.mult))
    return nc.vector.scalar_tensor_tensor(vn, t2, n / 4.0, vn, ALU.mult, ALU.add)


def clear_after(nc, ctx, used):
    def clear():
        with nc.Block() as block:
            @block.gpsimd
            def _(pool):
                for s in used:
                    pool.sem_clear(s)
    ctx.callback(clear)


def first_attention(nc, R, A):
    with ExitStack() as ctx:
        sb = lambda n, s, d=F32: ctx.enter_context(nc.sbuf_tensor(n, s, d))
        pb = lambda n: ctx.enter_context(nc.psum_tensor(n, [P, 512], F32))
        used = []
        sem = lambda n: used.append(ctx.enter_context(nc.semaphore(n))) or used[-1]
        X, ident, ones = R["X"], R["ident"], R["ones"]
        Y = sb("a_y", [P, T, D])
        Z = sb("a_z", [P, T, D + 4])
        ZT = sb("a_zt", [P, B * L])
        wq, wk, wv, wvt, pj = (sb(f"a_{n}", [P, P]) for n in ("wq", "wk", "wv", "wvt", "pj"))
        wqs, wks = sb("a_wqs", [P, P]), sb("a_wks", [P, P])
        nw, nb, bvc = sb("a_nw", [P, 1]), sb("a_nb", [P, 1]), sb("a_bv", [P, 1])
        rows = sb("a_rows", [1, 3, P])
        rows2 = sb("a_rows2", [1, 2, P])
        bvf = sb("a_bvf", [P, 1])
        st = sb("a_st", [P, T, 6])
        mean, v128, r1, r2, t1, t2 = (sb(f"a_s{i}", [P, T]) for i in range(6))
        Gs = sb("a_g", [P, B, D + 1])
        gr = sb("a_gr", [1, B, P])
        T1 = sb("a_t1", [P, B, P])
        rr = sb("a_rr", [1, B, P])
        W = sb("a_w", [P, B, P])
        nm, den = sb("a_nm", [P, B]), sb("a_den", [P, B])
        Ms, N1 = sb("a_m", [P, B, P]), sb("a_n", [P, B, P])
        bvb = sb("a_bvb", [P, P])
        nmr = sb("a_nmr", [P, T])
        up, dn, pk = sb("a_up", [P, FF]), sb("a_dn", [P, FF]), sb("a_pk", [P, FF])
        ab, thr = sb("a_ab", [P, 2]), sb("a_thr", [P, 4])
        pT = [pb("a_pt0"), pb("a_pt1")]
        pG, pR, pS, pM = pb("a_pg"), pb("a_pr"), pb("a_ps"), pb("a_pm")
        pO = [pb("a_po0"), pb("a_po1")]
        pW = [pG, pS, pO[0], pO[1]]
        pU = [pM, pT[0]]
        x_in = [sem(f"x_in{b}") for b in range(B)]
        w_in = sem("w_in")
        ident_done, ones_done = sem("ident_done"), sem("ones_done")
        var_done, std_done, z_done = sem("var_done"), sem("std_done"), sem("z_done")
        folded, bias_mm = sem("folded"), sem("bias_mm")
        zt_mm, zt_done, g_mm, g_done = sem("zt_mm"), sem("zt_done"), sem("g_mm"), sem("g_done")
        r_mm, r_done, b_read = sem("r_mm"), sem("r_done"), sem("b_read")
        t1_mm, t1_done, s_mm, nm_done, exp_done, w_done = (sem(n) for n in (
            "t1_mm", "t1_done", "s_mm", "nm_done", "exp_done", "w_done"))
        m_mm, m_done, n_mm, n_done = sem("m_mm"), sem("m_done"), sem("n_mm"), sem("n_done")
        o_mm, o_read, abs_done, abs_mm = sem("o_mm"), sem("o_read"), sem("abs_done"), sem("abs_mm")
        r_ready, ln_done, nmr_done, y_done = sem("r_ready"), sem("ln_done"), sem("nmr_done"), sem("y_done")
        vs, ps = sem("a_vec"), sem("a_pool")
        clear_after(nc, ctx, used)
        block = ctx.enter_context(nc.Block())

        @block.sync
        def _(sp):
            for b in range(B):
                sp.dma_start(X[:, b * TB:(b + 1) * TB, :],
                             A["x"][b * L:(b + 1) * L, :].rearrange("(t p) d -> p t d", p=P)).then_inc(x_in[b], 16)

        @block.scalar
        def _(act):
            for dst, src in ((wq, "wq_t"), (wk, "wk_t"), (wv, "wv"), (wvt, "wv_t"), (pj, "proj_t"),
                             (nw, "norm_w"), (nb, "norm_b"), (bvc, "bv")):
                act.dma_start(dst[:], A[src]).then_inc(w_in, 16)
            act.dma_start(rows[:], A["rows"]).then_inc(w_in, 16)
            act.dma_start(up[:], A["w_up"]).then_inc(w_in, 16)
            act.dma_start(dn[:], A["w_down"]).then_inc(w_in, 16)
            for b in range(B):
                tb = slice(b * TB, (b + 1) * TB)
                act.wait_ge(var_done, b + 1)
                nc.scalar.activation(r1[:, tb], v128[:, tb], ACT.Sqrt, bias=R["c_eps"], scale=1.0 / D)
                nc.scalar.activation(r2[:, tb], v128[:, tb], ACT.Sqrt, bias=R["c_eps2"],
                                     scale=(1.0 + EPS) / D).then_inc(std_done, 1)
            for k in range(2 * B):
                act.wait_ge(zt_mm, k + 1)
                nc.scalar.copy(ZT[:, k * CH:(k + 1) * CH], pT[k % 2][:]).then_inc(zt_done, 1)
            for b in range(B):
                act.wait_ge(nm_done, b + 1)
                nc.scalar.activation(W[:, b, :], pW[b][:, 0:P], ACT.Exp, bias=nm[:, b:b + 1],
                                     scale=1.0 / 32.0, accum_out=den[:, b:b + 1]).then_inc(exp_done, 1)
            def std(b):
                tb = slice(b * TB, (b + 1) * TB)
                act.wait_ge(var_done, B + b + 1)
                nc.scalar.activation(r1[:, tb], v128[:, tb], ACT.Sqrt, bias=R["c_eps"],
                                     scale=1.0 / D).then_inc(std_done, 1)

            def normed(b):
                act.wait_ge(nmr_done, b + 1)
                for t in range(b * TB, (b + 1) * TB):
                    y = nc.scalar.activation(Y[:, t, :], Y[:, t, :], ACT.Identity, bias=nmr[:, t:t + 1],
                                             scale=r1[:, t:t + 1])
                y.then_inc(y_done, 1)

            std(0)
            for b in range(B):
                if b + 1 < B:
                    std(b + 1)
                if b < B - 1:
                    normed(b)

        @block.gpsimd
        def _(pool):
            nc.gpsimd.memset(R["c_eps"], EPS).then_inc(ones_done, 1)
            nc.gpsimd.memset(R["c_eps2"], EPS * EPS).then_inc(ones_done, 1)
            nc.gpsimd.memset(ones[:], 1.0).then_inc(ones_done, 1)
            nc.gpsimd.memset(Z[:, :, D:D + 1], 1.0).then_inc(ones_done, 1)
            nc.gpsimd.memset(ident[:], 0.0).then_inc(ps, 1)
            pool.wait_ge(ps, 1)
            nc.gpsimd.affine_select(out=ident[:], in_=ident[:], compare_op=ALU.not_equal, fill=1.0,
                                    base=0, pattern=[[-1, P]], channel_multiplier=1).then_inc(ident_done, 1)
            for b in range(B):
                pool.wait_ge(r_ready, b + 1)
                for t in range(b * TB, (b + 1) * TB):
                    y = nc.gpsimd.tensor_scalar(Y[:, t, :], X[:, t, :], mean[:, t:t + 1], r1[:, t:t + 1],
                                                ALU.subtract, ALU.mult)
                y.then_inc(ln_done, 1)
            for b in range(B - 1):
                tb = slice(b * TB, (b + 1) * TB)
                pool.wait_ge(y_done, b + 1)
                nc.gpsimd.tensor_tensor(X[:, tb, :], X[:, tb, :], Y[:, tb, :], ALU.add).then_inc(ps, 1)
            pool.wait_ge(ps, B)

        @block.vector
        def _(v):
            c = Chain(v, vs)

            def fold_weights():
                v.wait_ge(w_in, 11 * 16)
                c.mark(nc.vector.tensor_scalar(wqs[:], wq[:], nw[:], None, ALU.mult))
                nc.vector.tensor_scalar(wks[:], wk[:], nw[:], None, ALU.mult).then_inc(folded, 1)
                c.mark(nc.vector.tensor_reduce(ab[:, 0:1], up[:], AX.X, ALU.add, apply_absolute_value=True))
                nc.vector.tensor_reduce(ab[:, 1:2], dn[:], AX.X, ALU.add,
                                        apply_absolute_value=True).then_inc(abs_done, 1)
                v.wait_ge(bias_mm, 1)
                c.mark(nc.vector.tensor_tensor(rows2[:], rows[:, 0:2, :],
                                               pM[0:1, 0:2 * P].rearrange("a (r k) -> a r k", r=2), ALU.add))
                nc.vector.tensor_tensor(bvf[:], bvc[:], pM[:, 2 * P:2 * P + 1], ALU.add).then_inc(folded, 1)
                v.wait_ge(folded, 2)
                c.mark(nc.vector.tensor_scalar(bvb[:], ones[:], bvf[:], None, ALU.mult))

            def thresholds():
                v.wait_ge(abs_mm, 1)
                c.mark(nc.vector.tensor_scalar(thr[:, 0:2], pM[:, 0:2], 0.5 / (D * FF), None, ALU.mult))
                c.mark(nc.vector.tensor_scalar(thr[:, 2:4], pM[:, 0:2], -0.5 / (D * FF), None, ALU.mult))

            def ternary():
                for w, out, k in ((up, R["up_t"], 0), (dn, R["down_t"], 1)):
                    c.run(nc.vector.tensor_scalar(pk[:], w[:], thr[:, 2 + k:3 + k], None, ALU.is_lt))
                    c.run(nc.vector.scalar_tensor_tensor(out[:], w[:], thr[:, k:k + 1], pk[:],
                                                         ALU.is_gt, ALU.subtract))

            def stats(b, src):
                tb = slice(b * TB, (b + 1) * TB)
                stats_of(nc, c, src[:, tb, :], st[:, tb, :], TB)
                finish_stats(nc, c, st[:, tb, :], mean[:, tb], v128[:, tb], t1[:, tb],
                             t2[:, tb]).then_inc(var_done, 1)

            def normed(b):
                tb = slice(b * TB, (b + 1) * TB)
                v.wait_ge(std_done, b + 1)
                c.mark(nc.vector.reciprocal(r2[:, tb], r2[:, tb]))
                nc.vector.reciprocal(r1[:, tb], r1[:, tb]).then_inc(r_ready, 1)
                c.wait()
                for t in range(b * TB, (b + 1) * TB):
                    z = nc.vector.tensor_scalar(Z[:, t, 0:D], X[:, t, :], mean[:, t:t + 1], r2[:, t:t + 1],
                                                ALU.subtract, ALU.mult)
                    if t % TB == TB - 1:
                        z.then_inc(z_done, 1)

            def score_max(b):
                v.wait_ge(s_mm, b + 1)
                c.run(nc.vector.tensor_reduce(nm[:, b:b + 1], pW[b][:, 0:P], AX.X, ALU.max, negate=True))
                nc.vector.tensor_scalar(nm[:, b:b + 1], nm[:, b:b + 1], 1.0 / 32.0, None,
                                        ALU.mult).then_inc(nm_done, 1)

            def m_copy(b):
                v.wait_ge(m_mm, b + 1)
                nc.vector.tensor_copy(Ms[:, b, :], pM[:, 0:P]).then_inc(m_done, 1)

            def n_copy(b):
                tb = slice(b * TB, (b + 1) * TB)
                v.wait_ge(n_mm, b + 1)
                nc.vector.tensor_scalar(N1[:, b, :], pM[:, P:2 * P], nw[:], None, ALU.mult).then_inc(n_done, 1)
                v.wait_ge(ln_done, b + 1)
                nc.vector.tensor_tensor(Y[:, tb, :], Y[:, tb, :],
                                        pM[:, 2 * P:3 * P].unsqueeze(1).broadcast_to([P, TB, P]),
                                        ALU.add).then_inc(b_read, 1)

            def add_output(b, k):
                t0 = b * TB + 4 * k
                v.wait_ge(b_read, b + 1)
                v.wait_ge(o_mm, 2 * b + k + 1)
                nc.vector.tensor_tensor(Y[:, t0:t0 + 4, :], Y[:, t0:t0 + 4, :],
                                        pO[k][:].rearrange("p (t d) -> p t d", t=4), ALU.add).then_inc(o_read, 1)

            def scales(b):
                tb = slice(b * TB, (b + 1) * TB)
                v.wait_ge(std_done, B + b + 1)
                c.run(nc.vector.reciprocal(r1[:, tb], r1[:, tb]))
                nc.vector.scalar_tensor_tensor(nmr[:, tb], mean[:, tb], -1.0, r1[:, tb], ALU.mult,
                                               ALU.mult).then_inc(nmr_done, 1)

            v.wait_ge(ones_done, 4)
            v.wait_ge(x_in[0], 16)
            stats(0, X)
            for b in range(B):
                if b + 1 < B:
                    v.wait_ge(x_in[b + 1], 16)
                    stats(b + 1, X)
                normed(b)
                if b == 0:
                    fold_weights()
                if b == 1:
                    thresholds()
            for b in range(B):
                v.wait_ge(g_mm, b + 1)
                nc.vector.tensor_copy(Gs[:, b, :], pW[b][:, 0:D + 1]).then_inc(g_done, 1)
            v.wait_ge(r_mm, 1)
            nc.vector.tensor_copy(gr[:], pR[0:1, :].rearrange("p (b d) -> p b d", b=B)).then_inc(r_done, 1)
            nc.vector.scalar_tensor_tensor(rr[:], rows2[:, 1:2, :].broadcast_to([1, B, P]), float(L),
                                           pT[1][0:1, :].rearrange("p (b d) -> p b d", b=B),
                                           ALU.mult, ALU.add).then_inc(r_done, 1)
            for b in range(B):
                v.wait_ge(t1_mm, b + 1)
                nc.vector.tensor_copy(T1[:, b, :], pU[b % 2][:, 0:P]).then_inc(t1_done, 1)
                if b >= 1:
                    score_max(b - 1)
            score_max(B - 1)
            ternary()
            for b in range(B):
                v.wait_ge(exp_done, b + 1)
                c.run(nc.vector.reciprocal(den[:, b:b + 1], den[:, b:b + 1]))
                nc.vector.tensor_scalar(W[:, b, :], W[:, b, :], den[:, b:b + 1], None, ALU.mult).then_inc(w_done, 1)
                if b == 0:
                    m_copy(0)
            n_copy(0)
            for b in range(B):
                add_output(b, 0)
                if b + 1 < B:
                    m_copy(b + 1)
                add_output(b, 1)
                if b + 1 < B:
                    n_copy(b + 1)
                v.wait_ge(o_read, 2 * b + 2)
                stats(b, Y)
                if b >= 1:
                    scales(b - 1)
            scales(B - 1)
            v.wait_ge(nmr_done, B)
            for t in range(T - TB, T):
                c.mark(nc.vector.tensor_scalar(Y[:, t, :], Y[:, t, :], r1[:, t:t + 1], nmr[:, t:t + 1],
                                               ALU.mult, ALU.add))
            c.wait()
            c.run(nc.vector.tensor_tensor(X[:, T - TB:, :], X[:, T - TB:, :], Y[:, T - TB:, :], ALU.add))

        @block.tensor
        def _(pe):
            mm = nc.tensor.matmul
            pe.wait_ge(folded, 1)
            pe.wait_ge(ones_done, 4)
            pe.wait_ge(ident_done, 1)
            mm(pM[0:1, 0:P], nb[:], wq[:], start=True, stop=True)
            mm(pM[0:1, P:2 * P], nb[:], wk[:], start=True, stop=True)
            mm(pM[:, 2 * P:2 * P + 1], wvt[:], nb[:], start=True, stop=True).then_inc(bias_mm, 1)
            for b in range(B):
                pe.wait_ge(z_done, b + 1)
                for k in range(2):
                    if 2 * b + k >= 2:
                        pe.wait_ge(zt_done, 2 * b + k - 1)
                    for j in range(4):
                        tr = nc.tensor.transpose(pT[k][:, j * P:(j + 1) * P], Z[:, b * TB + 4 * k + j, 0:D], ident[:])
                    tr.then_inc(zt_mm, 1)
                if b == 0:
                    pe.wait_ge(folded, 2)
                    pe.wait_ge(abs_done, 1)
                    mm(pM[:, 0:2], ones[:], ab[:], start=True, stop=True).then_inc(abs_mm, 1)
                for t in range(b * TB, (b + 1) * TB):
                    g = mm(pW[b][:, 0:D + 1], Z[:, t, 0:D], Z[:, t, 0:D + 1], start=t % TB == 0, stop=t % TB == TB - 1)
                g.then_inc(g_mm, 1)
            for b in range(B):
                pe.wait_ge(g_done, b + 1)
                if b == 0:
                    pe.wait_ge(zt_done, 8)
                mm(pR[0:1, b * P:(b + 1) * P], Gs[:, b, D:D + 1], ident[:], start=True, stop=True)
                s_wk = mm(pT[1][0:1, b * P:(b + 1) * P], Gs[:, b, D:D + 1], wks[:], start=True, stop=True)
            s_wk.then_inc(r_mm, 1)
            pe.wait_ge(r_done, 2)

            def t1(b):
                if b >= 2:
                    pe.wait_ge(t1_done, b - 1)
                mm(pU[b % 2][:, 0:P], Gs[:, b, 0:D], wks[:], start=True, stop=False)
                mm(pU[b % 2][:, 0:P], gr[:, b, :], rows2[:, 1, :], start=False, stop=True).then_inc(t1_mm, 1)

            def score(b):
                pe.wait_ge(t1_done, b + 1)
                mm(pW[b][:, 0:P], wqs[:], T1[:, b, :], start=True, stop=False)
                mm(pW[b][:, 0:P], rows2[:, 0, :], rr[:, b, :], start=False, stop=True).then_inc(s_mm, 1)

            def m(b):
                pe.wait_ge(w_done, b + 1)
                if b == 0:
                    pe.wait_ge(t1_done, B)
                else:
                    pe.wait_ge(b_read, b)
                mm(pM[:, 0:P], W[:, b, :], pj[:], start=True, stop=True).then_inc(m_mm, 1)

            def n(b):
                pe.wait_ge(m_done, b + 1)
                mm(pM[:, P:2 * P], wv[:], Ms[:, b, :], start=True, stop=True)
                mm(pM[:, 2 * P:3 * P], bvb[:], Ms[:, b, :], start=True, stop=False)
                mm(pM[:, 2 * P:3 * P], ones[0:1, :], rows[:, 2, :], start=False, stop=True).then_inc(n_mm, 1)

            def output(b, k):
                if b >= 1:
                    pe.wait_ge(o_read, 2 * b + k - 1)
                for j in range(4):
                    t = b * TB + 4 * k + j
                    last = mm(pO[k][:, j * P:(j + 1) * P], ZT[:, t * P:(t + 1) * P], N1[:, b, :], start=True, stop=True)
                last.then_inc(o_mm, 1)

            t1(0)
            for b in range(B):
                if b + 1 < B:
                    t1(b + 1)
                score(b)
            m(0)
            n(0)
            pe.wait_ge(exp_done, B)
            for b in range(B):
                pe.wait_ge(n_done, b + 1)
                output(b, 0)
                if b + 1 < B:
                    m(b + 1)
                output(b, 1)
                if b + 1 < B:
                    n(b + 1)


def feed_forward(nc, R, A):
    with ExitStack() as ctx:
        sb = lambda n, s, d=F32: ctx.enter_context(nc.sbuf_tensor(n, s, d))
        pb = lambda n: ctx.enter_context(nc.psum_tensor(n, [P, 512], F32))
        used = []
        sem = lambda n: used.append(ctx.enter_context(nc.semaphore(n))) or used[-1]
        X, ident, ones = R["X"], R["ident"], R["ones"]
        Z = sb("f_z", [P, T, D])
        ZT = sb("f_zt", [P, B * L])
        H = sb("f_h", [P, 2, FC, CH])
        SQ = sb("f_sq", [P, 3, FC, CH])
        O = sb("f_o", [P, T, D])
        st = sb("f_st", [P, T, 6])
        mean, v128, r1, r2, t1, t2, ssq, mean2, q1, q2, nmr = (sb(f"f_s{i}", [P, T]) for i in range(11))
        PARTS = (slice(0, 3 * TB), slice(3 * TB, T))
        pT = [pb("f_pt0"), pb("f_pt1")]
        pU = [pb("f_pu0"), pb("f_pu1")]
        pD = [pb("f_pd0"), pb("f_pd1")]
        pQ = [pb("f_pq0"), pb("f_pq1")]
        var_done, std_done, z_done, zt_mm, zt_done = (sem(n) for n in (
            "var_done", "std_done", "z_done", "zt_mm", "zt_done"))
        up_mm, h_done, sq_done, down_mm, o_read = (sem(n) for n in (
            "up_mm", "h_done", "sq_done", "down_mm", "o_read"))
        s_done, rms_done, u_done = sem("s_done"), sem("rms_done"), sem("u_done")
        sqs_done, sum_mm, q_read, scale_done, u2_done = (sem(n) for n in (
            "sqs_done", "sum_mm", "q_read", "scale_done", "u2_done"))
        vs, ps = sem("f_vec"), sem("f_pool")
        clear_after(nc, ctx, used)
        block = ctx.enter_context(nc.Block())

        @block.scalar
        def _(act):
            def std(b):
                tb = slice(b * TB, (b + 1) * TB)
                act.wait_ge(var_done, b + 1)
                nc.scalar.activation(r1[:, tb], v128[:, tb], ACT.Sqrt, bias=R["c_eps"], scale=1.0 / D)
                nc.scalar.activation(r2[:, tb], v128[:, tb], ACT.Sqrt, scale=1.0 / D).then_inc(std_done, 1)

            def zt(k):
                act.wait_ge(zt_mm, k + 1)
                nc.scalar.copy(ZT[:, k * CH:(k + 1) * CH], pT[k % 2][:]).then_inc(zt_done, 1)

            def deviations(part, ts):
                act.wait_ge(s_done, 2 * part + 1)
                nc.scalar.activation(q1[:, ts], ssq[:, ts], ACT.Sqrt, scale=1.0 / FF).then_inc(rms_done, 1)
                act.wait_ge(s_done, 2 * part + 2)
                nc.scalar.activation(q2[:, ts], v128[:, ts], ACT.Sqrt, bias=R["c_eps"], scale=1.0 / D).then_inc(rms_done, 1)

            std(0)
            zt(0)
            for b in range(1, B):
                std(b)
            for k in range(NCH):
                if k + 1 < NCH:
                    zt(k + 1)
                if k == NCH - 1:
                    deviations(0, PARTS[0])
                if k >= 2:
                    act.wait_ge(down_mm, k - 1)
                    act.wait_ge(sq_done, FC * (k - 1))
                for f in range(FC):
                    act.wait_ge(up_mm, FC * k + f + 1)
                    nc.scalar.activation(H[:, k % 2, f, :], pU[f % 2][:], ACT.Gelu).then_inc(h_done, 1)
            act.wait_ge(scale_done, 1)
            for t in range(2 * TB):
                u = nc.scalar.activation(Z[:, t, :], O[:, t, :], ACT.Identity, bias=nmr[:, t:t + 1],
                                         scale=q1[:, t:t + 1])
                if t % TB == TB - 1:
                    u.then_inc(u_done, 1)
            deviations(1, PARTS[1])

        @block.gpsimd
        def _(pool):
            for k in range(NCH):
                pool.wait_ge(sq_done, FC * (k + 1))
                nc.gpsimd.tensor_tensor(SQ[:, k % 3, 0:2, :], SQ[:, k % 3, 0:2, :], SQ[:, k % 3, 2:4, :], ALU.add
                                        ).then_inc(ps, 1)
                pool.wait_ge(ps, k + 1)
                nc.gpsimd.tensor_tensor(SQ[:, k % 3, 0, :], SQ[:, k % 3, 0, :], SQ[:, k % 3, 1, :], ALU.add
                                        ).then_inc(sqs_done, 1)
            pool.wait_ge(u2_done, 1)
            nc.gpsimd.tensor_tensor(X[:, 2 * TB:3 * TB, :], X[:, 2 * TB:3 * TB, :], Z[:, 2 * TB:3 * TB, :], ALU.add
                                    ).then_inc(ps, 1)
            for b in range(2):
                tb = slice(b * TB, (b + 1) * TB)
                pool.wait_ge(u_done, b + 1)
                nc.gpsimd.tensor_tensor(X[:, tb, :], X[:, tb, :], Z[:, tb, :], ALU.add).then_inc(ps, 1)
            pool.wait_ge(ps, NCH + 3)

        @block.vector
        def _(v):
            c = Chain(v, vs)

            def stats(b):
                tb = slice(b * TB, (b + 1) * TB)
                stats_of(nc, c, X[:, tb, :], st[:, tb, :], TB)
                finish_stats(nc, c, st[:, tb, :], mean[:, tb], v128[:, tb], t1[:, tb],
                             t2[:, tb]).then_inc(var_done, 1)

            def normed(b):
                tb = slice(b * TB, (b + 1) * TB)
                v.wait_ge(std_done, b + 1)
                c.run(nc.vector.reciprocal(r1[:, tb], r1[:, tb]))
                c.run(nc.vector.tensor_tensor(r2[:, tb], r2[:, tb], r1[:, tb], ALU.mult))
                c.run(nc.vector.tensor_scalar(r2[:, tb], r2[:, tb], 1e-8, None, ALU.add))
                c.run(nc.vector.reciprocal(r2[:, tb], r2[:, tb]))
                c.run(nc.vector.tensor_tensor(r1[:, tb], r2[:, tb], r1[:, tb], ALU.mult))
                for t in range(b * TB, (b + 1) * TB):
                    z = nc.vector.tensor_scalar(Z[:, t, :], X[:, t, :], mean[:, t:t + 1], r1[:, t:t + 1],
                                                ALU.subtract, ALU.mult)
                    if t % TB == TB - 1:
                        z.then_inc(z_done, 1)

            def squares(k):
                for f in range(FC):
                    v.wait_ge(h_done, FC * k + f + 1)
                    if k >= 3 and f == 0:
                        v.wait_ge(sum_mm, k - 2)
                    nc.vector.tensor_tensor(SQ[:, k % 3, f, :], H[:, k % 2, f, :], H[:, k % 2, f, :],
                                            ALU.mult).then_inc(sq_done, 1)

            def outputs(k):
                ts = slice(4 * k, 4 * k + 4)
                v.wait_ge(down_mm, k + 1)
                nc.vector.tensor_copy(O[:, ts, :], pD[k % 2][:].rearrange("p (t d) -> p t d", t=4)).then_inc(o_read, 1)
                v.wait_ge(sum_mm, k + 1)
                nc.vector.tensor_copy(ssq[:, ts], pQ[k % 2][:, 0:4]).then_inc(q_read, 1)
                v.wait_ge(o_read, k + 1)
                for t in range(4 * k, 4 * k + 4):
                    c.mark(nc.vector.bn_stats(st[:, t, :], O[:, t, :]))

            def scales(part, ts):
                c.wait()
                v.wait_ge(q_read, (NCH - 2, NCH)[part])
                finish_stats(nc, c, st[:, ts], mean2[:, ts], v128[:, ts], t1[:, ts], t2[:, ts]).then_inc(s_done, 1)
                v.wait_ge(rms_done, 2 * part + 1)
                c.run(nc.vector.tensor_scalar(q1[:, ts], q1[:, ts], 1e-8, None, ALU.add))
                c.run(nc.vector.reciprocal(q1[:, ts], q1[:, ts]))
                c.run(nc.vector.tensor_tensor(t1[:, ts], q1[:, ts], q1[:, ts], ALU.mult))
                v.wait_ge(s_done, 2 * part + 1)
                nc.vector.tensor_tensor(v128[:, ts], v128[:, ts], t1[:, ts], ALU.mult).then_inc(s_done, 1)
                v.wait_ge(rms_done, 2 * part + 2)
                c.run(nc.vector.reciprocal(q2[:, ts], q2[:, ts]))
                c.run(nc.vector.tensor_tensor(q1[:, ts], q1[:, ts], q2[:, ts], ALU.mult))
                nc.vector.scalar_tensor_tensor(nmr[:, ts], mean2[:, ts], -1.0, q1[:, ts], ALU.mult,
                                               ALU.mult).then_inc(scale_done, 1)

            def output_normed(b):
                for t in range(b * TB, (b + 1) * TB):
                    u = nc.vector.tensor_scalar(Z[:, t, :], O[:, t, :], mean2[:, t:t + 1], q1[:, t:t + 1],
                                                ALU.subtract, ALU.mult)
                return u

            stats(0)
            normed(0)
            for b in range(1, B):
                stats(b)
            for k in range(NCH):
                if k % 2 == 0 and k // 2 + 1 < B:
                    normed(k // 2 + 1)
                squares(k)
                if 2 <= k < NCH - 1:
                    outputs(k - 2)
                if k == NCH - 2:
                    outputs(NCH - 3)
                    scales(0, PARTS[0])
            output_normed(2).then_inc(u2_done, 1)
            outputs(NCH - 2)
            outputs(NCH - 1)
            scales(1, PARTS[1])
            c.run(output_normed(3))
            c.run(nc.vector.tensor_tensor(X[:, T - TB:, :], X[:, T - TB:, :], Z[:, T - TB:, :], ALU.add))

        @block.tensor
        def _(pe):
            mm = nc.tensor.matmul

            def transposes(k):
                pe.wait_ge(z_done, k // 2 + 1)
                if k >= 2:
                    pe.wait_ge(zt_done, k - 1)
                for j in range(4):
                    tr = nc.tensor.transpose(pT[k % 2][:, j * P:(j + 1) * P], Z[:, 4 * k + j, :], ident[:])
                tr.then_inc(zt_mm, 1)

            def up(k):
                pe.wait_ge(zt_done, k + 1)
                for f in range(FC):
                    n = FC * k + f
                    if n >= 2:
                        pe.wait_ge(h_done, n - 1)
                    mm(pU[f % 2][:], R["up_t"][:, f * P:(f + 1) * P], ZT[:, k * CH:(k + 1) * CH],
                       start=True, stop=True).then_inc(up_mm, 1)

            def down(k):
                pe.wait_ge(h_done, FC * (k + 1))
                if k >= 2:
                    pe.wait_ge(o_read, k - 1)
                for j in range(4):
                    for f in range(FC):
                        last = mm(pD[k % 2][:, j * P:(j + 1) * P], H[:, k % 2, f, j * P:(j + 1) * P],
                                  R["down_t"][:, f * P:(f + 1) * P], start=f == 0, stop=f == FC - 1)
                last.then_inc(down_mm, 1)

            def sums(k):
                pe.wait_ge(sqs_done, k + 1)
                if k >= 2:
                    pe.wait_ge(q_read, k - 1)
                for j in range(4):
                    last = mm(pQ[k % 2][:, j:j + 1], SQ[:, k % 3, 0, j * P:(j + 1) * P], ones[:, 0:1],
                              start=True, stop=True)
                last.then_inc(sum_mm, 1)

            transposes(0)
            for k in range(NCH):
                if k + 1 < NCH:
                    transposes(k + 1)
                up(k)
                if k >= 1:
                    down(k - 1)
                if 2 <= k < NCH - 1:
                    sums(k - 2)
                if k == NCH - 2:
                    sums(NCH - 3)
            down(NCH - 1)
            sums(NCH - 2)
            sums(NCH - 1)


SCALE = float(HD) ** -0.5
MAX_SHIFT = 20.0
SPLIT_Q = (0, 0, 0, 1, 1, 2)
SPLIT_K = (0, 1, 2, 0, 1, 0)
RUNS = ((0, 3), (3, 2), (5, 1))
ROW_SHIFT = 8 * len(SPLIT_Q)
UNITS = B * NQ


def second_projections(nc, R, A, S):
    with ExitStack() as ctx:
        sb = lambda n, s, d=F32: ctx.enter_context(nc.sbuf_tensor(n, s, d))
        pb = lambda n: ctx.enter_context(nc.psum_tensor(n, [P, 512], F32))
        used = []
        sem = lambda n: used.append(ctx.enter_context(nc.semaphore(n))) or used[-1]
        X, ident = R["X"], R["ident"]
        Z = sb("b_z", [P, T, D])
        ZT = sb("b_zt", [P, B * L])
        wab = sb("b_wab", [P, 4, P])
        wv = sb("b_wv", [P, P])
        bab = sb("b_bab", [P, 4])
        bv = sb("b_bv", [P, P])
        cs = sb("b_cs", [P, 2, L])
        blk = sb("b_blk", [P, HEADS])
        ta, tb_, q, r = (sb(f"b_{n}", [P, 2, CH]) for n in ("ta", "tb", "q", "r"))
        sq = sb("b_sq", [P, 2, CH])
        parts = sb("b_parts", [P, 4, 3, CH], BF16)
        N2 = sb("b_n2", [HEADS, 2, B * L])
        m2 = sb("b_m2", [HEADS, L])
        sh = sb("b_sh", [HEADS, B, L], BF16)
        kmax, mmax = sb("b_kmax", [HEADS, B]), sb("b_mmax", [HEADS, B])
        ok = sb("b_ok", [HEADS, 2])
        pad = sb("b_pad", [32, 2 * L], BF16)
        st = sb("b_st", [P, T, 6])
        mean, v128, r1, t1, t2 = (sb(f"b_s{i}", [P, T]) for i in range(5))
        pT = [pb("b_pt0"), pb("b_pt1")]
        pA = [pb("b_pa0"), pb("b_pa1")]
        pB = [pb("b_pb0"), pb("b_pb1")]
        pN, pV = pb("b_pn"), pb("b_pv")
        (w_in, var_done, std_done, z_done, zt_mm, zt_done, ab_mm, ab_read, q_done, hi_done, r_done, mid_done,
         lo_done, sq_done, n_mm, n_read, v_mm, v_read, m2_done, sh_done, m_done, pad_done, pad_out, pad_in, sh_out,
         ok_done, ok_mm) = (sem("b_" + n) for n in (
             "w_in", "var_done", "std_done", "z_done", "zt_mm", "zt_done", "ab_mm", "ab_read", "q_done", "hi_done",
             "r_done", "mid_done", "lo_done", "sq_done", "n_mm", "n_read", "v_mm", "v_read", "m2_done", "sh_done",
             "m_done", "pad_done", "pad_out", "pad_in", "sh_out", "ok_done", "ok_mm"))
        part_out = [sem(f"b_part_out{i}") for i in range(4)]
        vs = sem("b_vec")
        clear_after(nc, ctx, used)
        block = ctx.enter_context(nc.Block())

        @block.sync
        def _(sp):
            for dst, src in ((wab, "w_ab"), (wv, "wv1_t"), (bab, "b_ab"), (cs, "cos_sin"), (blk, "head_sum")):
                sp.dma_start(dst[:], A[src]).then_inc(w_in, 16)
            sp.dma_start(bv[:], A["bv1"].partition_broadcast(P)).then_inc(w_in, 16)
            sp.wait_ge(pad_in, 16)
            for b in range(B):
                for a in range(2):
                    r0 = 64 * a + ROW_SHIFT
                    for w in range(2):
                        sp.dma_start(S["qk"[w]][b, r0:r0 + 16].rearrange("r n h t -> r n (h t)"),
                                     pad[16 * w:16 * w + 16, :].unsqueeze(1).broadcast_to([16, NQ, 2 * L])
                                     ).then_inc(pad_out, 16)
            for i in range(2 * NCH):
                k, w = i // 2, i % 2
                b, t0 = k // 2, (k % 2) * CH
                sp.wait_ge(lo_done, i + 1)
                sp.wait_ge(mid_done, i + 1)
                for run, (g, count) in enumerate(RUNS):
                    for a in range(2):
                        rows = slice(64 * a, 64 * a + 64)
                        dst = S["qk"[w]][b, 64 * a + 8 * g:64 * a + 8 * (g + count), :, :, t0:t0 + CH]
                        if w == 0:
                            src = parts[rows, i % 4, run:run + 1, :].broadcast_to([64, count, CH])
                        else:
                            src = parts[rows, i % 4, 0:count, :]
                        sp.dma_start(dst.rearrange("(g r) n h t -> (r n h) g t", g=count), src
                                     ).then_inc(part_out[i % 4], 16)
            sp.wait_ge(pad_out, 64 * B)
            for b in range(B):
                sp.wait_ge(sh_done, b + 1)
                for a in range(2):
                    sp.dma_start(S["q"][b, 64 * a + ROW_SHIFT, :, :, :].rearrange("n h t -> (n h) t"),
                                 sh[8 * a:8 * a + 8, b, :]).then_inc(sh_out, 16)
            sp.wait_ge(sh_out, B * 2 * 16)
            for i in range(4):
                sp.wait_ge(part_out[i], 2 * NCH // 4 * 6 * 16)

        @block.scalar
        def _(act):
            def std(b):
                tb = slice(b * TB, (b + 1) * TB)
                act.wait_ge(var_done, b + 1)
                nc.scalar.activation(r1[:, tb], v128[:, tb], ACT.Sqrt, bias=R["c_eps"],
                                     scale=1.0 / D).then_inc(std_done, 1)

            def zt(k):
                act.wait_ge(zt_mm, k + 1)
                nc.scalar.copy(ZT[:, k * CH:(k + 1) * CH], pT[k % 2][:]).then_inc(zt_done, 1)

            def shift(b):
                act.wait_ge(m2_done, b + 1)
                nc.scalar.activation(m2[:], m2[:], ACT.Sqrt).then_inc(m_done, 1)

            def mid(i):
                act.wait_ge(r_done, i + 1)
                nc.scalar.copy(parts[:, i % 4, 1, :], r[:, i % 2, :]).then_inc(mid_done, 1)

            std(0)
            zt(0)
            for k in range(NCH):
                if k % 2 == 0 and k // 2 + 1 < B:
                    std(k // 2 + 1)
                if k + 1 < NCH:
                    zt(k + 1)
                for w in range(2):
                    i = 2 * k + w
                    act.wait_ge(q_done, i + 1)
                    if i >= 4:
                        act.wait_ge(part_out[i % 4], (i // 4) * 6 * 16)
                    nc.scalar.copy(parts[:, i % 4, 0, :], q[:, i % 2, :]).then_inc(hi_done, 1)
                    if i >= 1:
                        mid(i - 1)
                    if i >= 2:
                        act.wait_ge(n_mm, i - 1)
                    nc.scalar.square(sq[:, i % 2, :], q[:, i % 2, :]).then_inc(sq_done, 1)
                    if i % 4 == 1 and i >= 5:
                        shift(i // 4 - 1)
            mid(2 * NCH - 1)
            shift(B - 1)

        @block.gpsimd
        def _(pool):
            nc.gpsimd.memset(pad[:], 0.0).then_inc(pad_done, 1)
            pool.wait_ge(pad_done, 1)
            pool.dma_start(pad[16:19, :], A["ones_row"]).then_inc(pad_in, 16)
            for i in range(2 * NCH):
                pool.wait_ge(ab_read, 2 * i + 2)
                if i >= 2:
                    pool.wait_ge(sq_done, i - 1)
                    pool.wait_ge(r_done, i - 1)
                nc.gpsimd.tensor_tensor(q[:, i % 2, :], ta[:, i % 2, :], tb_[:, i % 2, :], ALU.add).then_inc(q_done, 1)

        @block.vector
        def _(v):
            c = Chain(v, vs)

            def stats(b):
                tb = slice(b * TB, (b + 1) * TB)
                stats_of(nc, c, X[:, tb, :], st[:, tb, :], TB)
                finish_stats(nc, c, st[:, tb, :], mean[:, tb], v128[:, tb], t1[:, tb],
                             t2[:, tb]).then_inc(var_done, 1)

            def normed(b):
                tb = slice(b * TB, (b + 1) * TB)
                v.wait_ge(std_done, b + 1)
                c.run(nc.vector.reciprocal(r1[:, tb], r1[:, tb]))
                for t in range(b * TB, (b + 1) * TB):
                    z = nc.vector.tensor_scalar(Z[:, t, :], X[:, t, :], mean[:, t:t + 1], r1[:, t:t + 1],
                                                ALU.subtract, ALU.mult)
                    if t % TB == TB - 1:
                        z.then_inc(z_done, 1)

            def rotate(i):
                k, w = i // 2, i % 2
                t0 = (k % 2) * CH
                if i >= 2:
                    v.wait_ge(q_done, i - 1)
                v.wait_ge(ab_mm, i + 1)
                nc.vector.scalar_tensor_tensor(ta[:, i % 2, :], pA[i % 2][:], bab[:, 2 * w:2 * w + 1],
                                               cs[:, 0, t0:t0 + CH], ALU.add, ALU.mult).then_inc(ab_read, 1)
                nc.vector.scalar_tensor_tensor(tb_[:, i % 2, :], pB[i % 2][:], bab[:, 2 * w + 1:2 * w + 2],
                                               cs[:, 1, t0:t0 + CH], ALU.add, ALU.mult).then_inc(ab_read, 1)

            def value(k):
                v.wait_ge(v_mm, k + 1)
                nc.vector.tensor_tensor(
                    R["V"][:, (k // 2) * NQ:(k // 2 + 1) * NQ, 4 * (k % 2):4 * (k % 2) + 4, :],
                    pV[:].rearrange("p (t n e) -> p n t e", t=4, n=NQ),
                    bv[:].rearrange("p (n e) -> p n e", n=NQ).unsqueeze(2).broadcast_to([P, NQ, 4, 32]),
                    ALU.add).then_inc(v_read, 1)

            def remainder(i):
                v.wait_ge(hi_done, i + 1)
                if i >= 2:
                    v.wait_ge(mid_done, i - 1)
                    v.wait_ge(lo_done, i - 1)
                nc.vector.tensor_tensor(r[:, i % 2, :], q[:, i % 2, :], parts[:, i % 4, 0, :],
                                        ALU.subtract).then_inc(r_done, 1)

            def last_part(i):
                v.wait_ge(mid_done, i + 1)
                nc.vector.tensor_tensor(parts[:, i % 4, 2, :], r[:, i % 2, :], parts[:, i % 4, 1, :],
                                        ALU.subtract).then_inc(lo_done, 1)

            def norms(i):
                k, w = i // 2, i % 2
                v.wait_ge(n_mm, i + 1)
                nc.vector.tensor_copy(N2[:, w, k * CH:(k + 1) * CH], pN[32 * w:32 * w + HEADS, :]).then_inc(n_read, 1)

            def bounds(b):
                tb = slice(b * L, (b + 1) * L)
                v.wait_ge(n_read, 4 * b + 4)
                c.run(nc.vector.tensor_reduce(kmax[:, b:b + 1], N2[:, 1, tb], AX.X, ALU.max))
                if b >= 1:
                    v.wait_ge(sh_done, b)
                nc.vector.tensor_scalar(m2[:], N2[:, 0, tb], kmax[:, b:b + 1], None, ALU.mult).then_inc(m2_done, 1)

            def shifts(b):
                v.wait_ge(m_done, b + 1)
                c.mark(nc.vector.tensor_reduce(mmax[:, b:b + 1], m2[:], AX.X, ALU.max))
                nc.vector.tensor_scalar(sh[:, b, :], m2[:], -1.0, None, ALU.mult).then_inc(sh_done, 1)

            v.wait_ge(w_in, 6 * 16)
            stats(0)
            normed(0)
            rotate(0)
            value(0)
            for i in range(2 * NCH):
                b = i // 4 + 1
                if i % 4 == 0 and b < B:
                    stats(b)
                if i + 1 < 2 * NCH:
                    rotate(i + 1)
                    if i % 2 == 1:
                        value((i + 1) // 2)
                remainder(i)
                if i % 4 == 1 and b < B:
                    normed(b)
                if i >= 1:
                    last_part(i - 1)
                if i >= 2:
                    norms(i - 2)
                if i % 4 == 1 and i >= 5:
                    bounds(i // 4 - 1)
                if i % 4 == 2 and i >= 6:
                    shifts(i // 4 - 1)
            last_part(2 * NCH - 1)
            norms(2 * NCH - 2)
            norms(2 * NCH - 1)
            bounds(B - 1)
            shifts(B - 1)
            c.wait()
            c.run(nc.vector.tensor_reduce(ok[:, 0:1], mmax[:], AX.X, ALU.max))
            nc.vector.tensor_scalar(ok[:, 1:2], ok[:, 0:1], MAX_SHIFT / SCALE, None, ALU.is_le).then_inc(ok_done, 1)
            v.wait_ge(ok_mm, 1)
            c.run(nc.vector.tensor_scalar(R["flag"], pN[0:1, 0:1], HEADS - 0.5, None, ALU.is_lt))

        @block.tensor
        def _(pe):
            mm = nc.tensor.matmul

            def transposes(k):
                pe.wait_ge(z_done, k // 2 + 1)
                if k >= 2:
                    pe.wait_ge(zt_done, k - 1)
                for j in range(4):
                    tr = nc.tensor.transpose(pT[k % 2][:, j * P:(j + 1) * P], Z[:, 4 * k + j, :], ident[:])
                tr.then_inc(zt_mm, 1)

            def norms(i):
                q0 = 32 * (i % 2)
                if i >= 2:
                    pe.wait_ge(n_read, i - 1)
                pe.wait_ge(sq_done, i + 1)
                mm(pN[q0:q0 + HEADS, :], blk[:], sq[:, i % 2, :], start=True, stop=True).then_inc(n_mm, 1)

            pe.wait_ge(w_in, 6 * 16)
            transposes(0)
            for k in range(NCH):
                pe.wait_ge(zt_done, k + 1)
                for w in range(2):
                    i = 2 * k + w
                    if i >= 2:
                        pe.wait_ge(ab_read, 2 * i - 2)
                    zt = ZT[:, k * CH:(k + 1) * CH]
                    mm(pA[i % 2][:], wab[:, 2 * w, :], zt, start=True, stop=True)
                    mm(pB[i % 2][:], wab[:, 2 * w + 1, :], zt, start=True, stop=True).then_inc(ab_mm, 1)
                    if w == 0:
                        if k >= 1:
                            pe.wait_ge(v_read, k)
                        for j in range(4):
                            last = mm(pV[:, j * P:(j + 1) * P], ZT[:, (4 * k + j) * P:(4 * k + j + 1) * P], wv[:],
                                      start=True, stop=True)
                        last.then_inc(v_mm, 1)
                    if w == 1 and k + 1 < NCH:
                        transposes(k + 1)
                    if i >= 2:
                        norms(i - 2)
            norms(2 * NCH - 2)
            norms(2 * NCH - 1)
            pe.wait_ge(n_read, 2 * NCH)
            pe.wait_ge(ok_done, 1)
            mm(pN[0:1, 0:1], ok[:, 1:2], R["ones"][0:HEADS, 0:1], start=True, stop=True).then_inc(ok_mm, 1)


def exact_maxima(nc, R, S):
    with ExitStack() as ctx:
        sb = lambda n, s, d=F32: ctx.enter_context(nc.sbuf_tensor(n, s, d))
        sem = lambda n: ctx.enter_context(nc.semaphore(n))
        Q, K = sb("m_q", [P, 2, L], BF16), sb("m_k", [P, 2, L], BF16)
        mt = sb("m_mt", [P, TB, 4])
        neg, rest = sb("m_neg", [4, L]), sb("m_rest", [4, L])
        parts = sb("m_parts", [4, 3, L], BF16)
        pS = [ctx.enter_context(nc.psum_tensor(f"m_ps{i}", [P, 1024], F32)) for i in range(2)]
        pT = ctx.enter_context(nc.psum_tensor("m_pt", [P, 1024], F32))
        qk_in, s_mm, max_done, t_mm, parts_done, shift_out, vs = (sem("m_" + n) for n in (
            "qk_in", "s_mm", "max_done", "t_mm", "parts_done", "shift_out", "vec"))
        block = ctx.enter_context(nc.Block())
        NS = TB * 4

        @block.sync
        def _(sp):
            slow = sp.value_load(R["flag"], min_val=0, max_val=1)
            with sp.If(slow > 0):
                for u in range(UNITS):
                    b, n = u // NQ, u % NQ
                    sp.dma_start(Q[:], S["q"][b, :, n, :, :]).then_inc(qk_in, 16)
                    sp.dma_start(K[:], S["k"][b, :, n, :, :]).then_inc(qk_in, 16)
                    sp.wait_ge(parts_done, u + 1)
                    for h in range(4):
                        r0 = 64 * (h % 2) + ROW_SHIFT
                        sp.dma_start(S["q"][b, r0:r0 + 3, n, h // 2, :], parts[h:h + 1, :, :]).then_inc(shift_out, 16)
                    sp.wait_ge(shift_out, 64 * (u + 1))

        @block.vector
        def _(v):
            slow = v.value_load(R["flag"], min_val=0, max_val=1)
            with v.If(slow > 0):
                with v.Fori(0, UNITS) as n:
                    for i in range(NS):
                        v.wait_ge(s_mm, n * NS + (i + 1))
                        nc.vector.tensor_reduce(mt[:, i // 4, i % 4:i % 4 + 1], pS[i % 2][:], AX.X,
                                                ALU.max, negate=True).then_inc(max_done, 1)
                    v.wait_ge(t_mm, n + 1)
                    nc.vector.tensor_copy(neg[:], pT[0:4, :]).then_inc(vs, 1)
                    v.wait_ge(vs, n * 5 + 1)
                    nc.vector.tensor_copy(parts[:, 0, :], neg[:]).then_inc(vs, 1)
                    v.wait_ge(vs, n * 5 + 2)
                    nc.vector.tensor_tensor(rest[:], neg[:], parts[:, 0, :], ALU.subtract).then_inc(vs, 1)
                    v.wait_ge(vs, n * 5 + 3)
                    nc.vector.tensor_copy(parts[:, 1, :], rest[:]).then_inc(vs, 1)
                    v.wait_ge(vs, n * 5 + 4)
                    nc.vector.tensor_tensor(rest[:], rest[:], parts[:, 1, :], ALU.subtract).then_inc(vs, 1)
                    v.wait_ge(vs, n * 5 + 5)
                    nc.vector.tensor_copy(parts[:, 2, :], rest[:]).then_inc(parts_done, 1)
                    v.wait_ge(parts_done, n + 1)

        @block.tensor
        def _(pe):
            slow = pe.value_load(R["flag"], min_val=0, max_val=1)
            with pe.If(slow > 0):
                with pe.Fori(0, UNITS) as n:
                    pe.wait_ge(qk_in, n * 32 + 32)
                    for i in range(NS):
                        st, h = i // 4, i % 4
                        pair, a = h // 2, h % 2
                        rows = slice(64 * a, 64 * a + ROW_SHIFT)
                        if i >= 2:
                            pe.wait_ge(max_done, n * NS + (i - 1))
                        for half in range(2):
                            last = nc.tensor.matmul(pS[i % 2][:, half * CH:(half + 1) * CH],
                                                    Q[rows, pair, st * P:(st + 1) * P],
                                                    K[rows, pair, half * CH:(half + 1) * CH], start=True, stop=True)
                        last.then_inc(s_mm, 1)
                    pe.wait_ge(max_done, n * NS + NS)
                    for st in range(TB):
                        last = nc.tensor.transpose(pT[0:4, st * P:(st + 1) * P], mt[:, st, :], R["ident"][:])
                    last.then_inc(t_mm, 1)


def second_scores(nc, R, A, S):
    with ExitStack() as ctx:
        sb = lambda n, s, d=F32: ctx.enter_context(nc.sbuf_tensor(n, s, d))
        sem = lambda n: ctx.enter_context(nc.semaphore(n))
        Q = [sb(f"s_q{i}", [P, 2, L], BF16) for i in range(2)]
        K = [sb(f"s_k{i}", [P, 2, L], BF16) for i in range(2)]
        V4 = [sb(f"s_v{i}", [P, TB, 4, 32]) for i in range(2)]
        E = [sb(f"s_e{i}", [P, 4, CH]) for i in range(4)]
        AS = [sb(f"s_as{i}", [P, CH]) for i in range(2)]
        rec = sb("s_rec", [P, 4, 4])
        zero = sb("s_zero", [P, NE * ROWS * D // P // 4])
        pS = [ctx.enter_context(nc.psum_tensor(f"s_ps{i}", [P, 1024], F32)) for i in range(2)]
        acc = [ctx.enter_context(nc.psum_tensor(f"s_acc{i}", [P, CH], F32)) for i in range(2)]
        pX = [ctx.enter_context(nc.psum_tensor(f"s_px{i}", [P, CH], F32)) for i in range(2)]
        qk_in = [sem(f"qk_in{i}") for i in range(2)]
        scores, exp_done, av_done, v_staged, acc_read, tr_mm, o_done, rec_done = (sem("s_" + n) for n in (
            "scores", "exp_done", "av_done", "v_staged", "acc_read", "tr_mm", "o_done", "rec_done"))
        v_zero = sem("s_v_zero")
        block = ctx.enter_context(nc.Block())
        STEPS = 2 * TB
        G = NQ * STEPS
        HU = 2 * NQ

        def over_batches(engine, batch):
            batch(0, True)
            with engine.Fori(1, B) as b:
                batch(b, False)

        @block.sync
        def _(sp):
            def load(b, c):
                for sb_, s in ((Q, "q"), (K, "k")):
                    sp.dma_start(sb_[c % 2][:], S[s][b, :, c, :, :]).then_inc(qk_in[c % 2], 16)

            for n in range(UNITS):
                if n >= 2:
                    sp.wait_ge(scores, 2 * STEPS * (n - 1))
                load(n // NQ, n % NQ)
                if n == 1:
                    sp.dma_start(R["W1"][:], A["w1"].rearrange("e d f -> d e f")).then_inc(R["w_in"], 16)
                    sp.dma_start(R["W2"][:].rearrange("p e c d -> p (e c) d"), A["w2"].rearrange("e (c p) d -> p (e c) d", p=P)
                                 ).then_inc(R["w_in"], 16)
                    sp.wait_ge(v_zero, 5)
                    for h in range(GR):
                        for e in range(0, NE, 6):
                            sp.dma_start(R["x_rows"][h][e:e + 6].rearrange("e r d -> (e r d)").rearrange(
                                "(p q) -> p q", p=P), zero[:]).then_inc(R["zero_out"], 16)

        @block.scalar
        def _(act):
            def batch(b, first):
                for g in range(G):
                    for pair in range(2):
                        act.wait_ge(scores, b * (2 * G) + (2 * g + pair + 1))
                        if pair == 0 and (g >= 4 or not first):
                            act.wait_ge(av_done, b * G + (g - 3))
                        nc.scalar.activation(E[g % 4][:, 2 * pair:2 * pair + 2, :],
                                             pS[pair][:].rearrange("p (a s) -> p a s", a=2),
                                             ACT.Exp, scale=SCALE).then_inc(exp_done, 1)

            over_batches(act, batch)

        @block.gpsimd
        def _(pool):
            for i in range(2):
                nc.gpsimd.memset(V4[i][:], 0.0).then_inc(v_zero, 1)
            nc.gpsimd.memset(zero[:], 0.0).then_inc(v_zero, 1)
            pool.wait_ge(v_zero, 3)
            for i in range(2):
                nc.gpsimd.memset(V4[i][:, :, :, HD:HD + 1], 1.0).then_inc(v_zero, 1)

        @block.vector
        def _(v):
            v.wait_ge(v_zero, 5)

            def stage(n, c):
                nc.vector.tensor_copy(V4[c % 2][:, :, :, 0:HD],
                                      R["V"][:, bass.ds(n, 1), :, :].rearrange("p n t (h e) -> p (n t) h e", h=4)
                                      ).then_inc(v_staged, 1)

            def batch(b, last):
                for hu in range(HU):
                    v.wait_ge(av_done, b * G + TB * (hu + 1))
                    nc.vector.tensor_copy(AS[hu % 2][:], acc[hu % 2][:]).then_inc(acc_read, 1)
                    if hu % 2 == 1 and not (last and hu // 2 + 2 >= NQ):
                        stage(b * NQ + (hu // 2 + 2), hu // 2)
                    v.wait_ge(tr_mm, b * HU + (hu + 1))
                    o = pX[hu % 2][:].rearrange("p (t h e) -> p t h e", t=4, h=4)
                    nc.vector.reciprocal(rec[:], o[:, :, :, HD]).then_inc(rec_done, 1)
                    v.wait_ge(rec_done, b * HU + (hu + 1))
                    t0 = 4 * (hu % 2)
                    c = hu // 2
                    dst = R["O"][:, bass.ds(b * TB + t0, 4), 32 * c:32 * c + 32]
                    nc.vector.tensor_tensor(dst.rearrange("p t (h e) -> p t h e", h=4), o[:, :, :, 0:HD],
                                            rec[:].unsqueeze(3).broadcast_to([P, 4, 4, HD]),
                                            ALU.mult).then_inc(o_done, 1)

            stage(0, 0)
            stage(1, 1)
            with v.Fori(0, B - 1) as b:
                batch(b, False)
            batch(B - 1, True)

        @block.tensor
        def _(pe):
            def score(b, first, g, pair):
                c, half, j = g // STEPS, (g // TB) % 2, g % TB
                if g % STEPS == 0 and pair == 0:
                    pe.wait_ge(qk_in[c % 2], b * 64 + 32 * (c // 2 + 1))
                if g >= 1 or not first:
                    pe.wait_ge(exp_done, b * (2 * G) + (2 * g - 1 + pair))
                for a in range(2):
                    rows = slice(64 * a, 64 * a + 64)
                    last = nc.tensor.matmul(pS[pair][:, a * CH:(a + 1) * CH],
                                            K[c % 2][rows, pair, j * P:(j + 1) * P],
                                            Q[c % 2][rows, pair, half * CH:(half + 1) * CH], start=True, stop=True)
                last.then_inc(scores, 1)

            def av(b, first, g):
                c, hu, j = g // STEPS, g // TB, g % TB
                if g % STEPS == 0:
                    pe.wait_ge(v_staged, b * NQ + (c + 1))
                if j == 0 and (hu >= 2 or not first):
                    pe.wait_ge(acc_read, b * HU + (hu - 1))
                pe.wait_ge(exp_done, b * (2 * G) + (2 * g + 2))
                for h in range(4):
                    last = nc.tensor.matmul(acc[hu % 2][32 * h:32 * h + 32, :], V4[c % 2][:, j, h, :],
                                            E[g % 4][:, h, :], start=j == 0, stop=j == TB - 1)
                last.then_inc(av_done, 1)

            def transposes(b, first, hu):
                pe.wait_ge(acc_read, b * HU + (hu + 1))
                if hu >= 2 or not first:
                    pe.wait_ge(o_done, b * HU + (hu - 1))
                for t in range(4):
                    last = nc.tensor.transpose(pX[hu % 2][:, t * P:(t + 1) * P],
                                               AS[hu % 2][:, t * P:(t + 1) * P], R["ident"][:])
                last.then_inc(tr_mm, 1)

            def batch(b, first):
                for g in range(G):
                    score(b, first, g, 0)
                    if g >= 2 or not first:
                        av(b, first, g - 2)
                    score(b, first, g, 1)
                    if g % TB == 4 and (g > TB or not first):
                        transposes(b, first, g // TB - 1)

            over_batches(pe, batch)
            av(B - 1, False, G - 2)
            av(B - 1, False, G - 1)
            transposes(B - 1, False, HU - 1)


def second_output(nc, R, A):
    with ExitStack() as ctx:
        sb = lambda n, s, d=F32: ctx.enter_context(nc.sbuf_tensor(n, s, d))
        pb = lambda n: ctx.enter_context(nc.psum_tensor(n, [P, 512], F32))
        sem = lambda n: ctx.enter_context(nc.semaphore(n))
        X = R["X"]
        OT = sb("o_ot", [P, 2, CH])
        Y = sb("o_y", [P, T, D])
        wo, bo = sb("o_wo", [P, P]), sb("o_bo", [P, P])
        st = sb("o_st", [P, T, 6])
        mean, v128, r1, t1, t2 = (sb(f"o_s{i}", [P, T]) for i in range(5))
        pT = [pb("o_pt0"), pb("o_pt1")]
        pO = [pb("o_po0"), pb("o_po1")]
        w_in, ot_mm, ot_done, o_mm, o_read, var_done, std_done, u_done = (sem("o_" + n) for n in (
            "w_in", "ot_mm", "ot_done", "o_mm", "o_read", "var_done", "std_done", "u_done"))
        vs, ps = sem("o_vec"), sem("o_pool")
        block = ctx.enter_context(nc.Block())

        @block.sync
        def _(sp):
            sp.dma_start(wo[:], A["wo_t"]).then_inc(w_in, 16)
            sp.dma_start(bo[:], A["bo"].partition_broadcast(P)).then_inc(w_in, 16)

        def std(act, b):
            tb = slice(b * TB, (b + 1) * TB)
            act.wait_ge(var_done, b + 1)
            nc.scalar.activation(r1[:, tb], v128[:, tb], ACT.Sqrt, bias=R["c_eps"],
                                 scale=1.0 / D).then_inc(std_done, 1)

        @block.scalar
        def _(act):
            for k in range(NCH):
                act.wait_ge(ot_mm, k + 1)
                if k >= 2:
                    act.wait_ge(o_mm, k - 1)
                nc.scalar.copy(OT[:, k % 2, :], pT[k % 2][:]).then_inc(ot_done, 1)
                if k % 2 == 1 and k >= 3:
                    std(act, k // 2 - 1)
            std(act, B - 1)

        @block.gpsimd
        def _(pool):
            for b in range(B):
                tb = slice(b * TB, (b + 1) * TB)
                pool.wait_ge(u_done, b + 1)
                nc.gpsimd.tensor_tensor(X[:, tb, :], X[:, tb, :], Y[:, tb, :], ALU.add).then_inc(ps, 1)
            pool.wait_ge(ps, B)

        @block.vector
        def _(v):
            c = Chain(v, vs)
            v.wait_ge(w_in, 32)

            def normed(b):
                tb = slice(b * TB, (b + 1) * TB)
                v.wait_ge(std_done, b + 1)
                c.run(nc.vector.reciprocal(r1[:, tb], r1[:, tb]))
                for t in range(b * TB, (b + 1) * TB):
                    y = nc.vector.tensor_scalar(Y[:, t, :], Y[:, t, :], mean[:, t:t + 1], r1[:, t:t + 1],
                                                ALU.subtract, ALU.mult)
                    if t % TB == TB - 1:
                        y.then_inc(u_done, 1)

            for k in range(NCH):
                v.wait_ge(o_mm, k + 1)
                nc.vector.tensor_tensor(Y[:, 4 * k:4 * k + 4, :], pO[k % 2][:].rearrange("p (t d) -> p t d", t=4),
                                        bo[:].unsqueeze(1).broadcast_to([P, 4, D]), ALU.add).then_inc(o_read, 1)
                if k % 2 == 1:
                    b = k // 2
                    tb = slice(b * TB, (b + 1) * TB)
                    v.wait_ge(o_read, k + 1)
                    stats_of(nc, c, Y[:, tb, :], st[:, tb, :], TB)
                    finish_stats(nc, c, st[:, tb, :], mean[:, tb], v128[:, tb], t1[:, tb],
                                 t2[:, tb]).then_inc(var_done, 1)
                    if b >= 1:
                        normed(b - 1)
            normed(B - 1)

        @block.tensor
        def _(pe):
            pe.wait_ge(w_in, 32)

            def transposes(k):
                if k >= 2:
                    pe.wait_ge(ot_done, k - 1)
                for j in range(4):
                    tr = nc.tensor.transpose(pT[k % 2][:, j * P:(j + 1) * P],
                                             R["O"][:, 4 * k + j, :], R["ident"][:])
                tr.then_inc(ot_mm, 1)

            transposes(0)
            for k in range(NCH):
                if k + 1 < NCH:
                    transposes(k + 1)
                pe.wait_ge(ot_done, k + 1)
                if k >= 2:
                    pe.wait_ge(o_read, k - 1)
                for j in range(4):
                    last = nc.tensor.matmul(pO[k % 2][:, j * P:(j + 1) * P], OT[:, k % 2, j * P:(j + 1) * P], wo[:],
                                            start=True, stop=True)
                last.then_inc(o_mm, 1)


GR = 4
GT = T // GR
NE = 24
CAP = -(-2 * GT * P // NE)
ROWS = 96
EB = 4
NB = NE // EB
BIG = 100000.0
LN_EPS = 1e-6


def tile_of(h, i):
    return (i // 2) * TB + 2 * h + i % 2


def routing(nc, R, A):
    with ExitStack() as ctx:
        sb = lambda n, s, d=F32: ctx.enter_context(nc.sbuf_tensor(n, s, d))
        pb = lambda n: ctx.enter_context(nc.psum_tensor(n, [P, 512], F32))
        sem = lambda n: ctx.enter_context(nc.semaphore(n))
        X, Yn, ident = R["X"], R["Yn"], R["ident"]
        YT = sb("r_yt", [P, 2, CH])
        wg = sb("r_wg", [P, NE])
        LG = sb("r_lg", [P, T, NE])
        top, ix = sb("r_top", [P, T, 8]), sb("r_ix", [P, T, 8], mybir.dt.uint32)
        eidx = sb("r_eidx", [P, T, 2])
        iota_i, iota = sb("r_iota_i", [P, NE], I32), sb("r_iota", [P, NE])
        M = sb("r_m", [P, T, 2, NE], BF16)
        PF = sb("r_pf", [P, GR, GT + 1, 2 * NE], BF16)
        before, onesb = sb("r_before", [P, P], BF16), sb("r_onesb", [P, P], BF16)
        LP = sb("r_lp", [P, T, 2, NE])
        p2, valid = sb("r_p2", [P, T, 2]), sb("r_valid", [P, T, 2])
        sl, s2 = sb("r_slot", [P, T, 2]), sb("r_away", [P, T, 2])
        EX = sb("r_ex", [P, T, NE + 1])
        zs, g, gs = sb("r_zs", [P, T]), sb("r_g", [P, T, 2]), sb("r_gs", [P, T])
        st = sb("r_st", [P, T, 6])
        mean, v128, r1, t1, t2 = (sb(f"r_s{i}", [P, T]) for i in range(5))
        pT = [pb("r_pt0"), pb("r_pt1")]
        pL = [pb("r_pl0"), pb("r_pl1")]
        pP = [pb("r_pp0"), pb("r_pp1")]
        (w_in, var_done, std_done, z_done, zt_mm, zt_done, lg_mm, lg_done, consts, pf_done, pos_mm, pos_read,
         ex_in, ex_done) = (sem("r_" + n) for n in (
             "w_in", "var_done", "std_done", "z_done", "zt_mm", "zt_done", "lg_mm", "lg_done", "consts", "pf_done",
             "pos_mm", "pos_read", "ex_in", "ex_done"))
        vs, ps = sem("r_vec"), sem("r_pool")
        block = ctx.enter_context(nc.Block())

        @block.sync
        def _(sp):
            sp.dma_start(wg[:], A["w_gate"]).then_inc(w_in, 16)

        @block.gpsimd
        def _(pool):
            nc.gpsimd.iota(iota_i[:], pattern=[[1, NE]], base=0, channel_multiplier=0).then_inc(ps, 1)
            nc.gpsimd.memset(onesb[:], 1.0).then_inc(ps, 1)
            pool.wait_ge(ps, 2)
            nc.gpsimd.tensor_copy(iota[:], iota_i[:]).then_inc(consts, 1)
            nc.gpsimd.affine_select(out=before[:], in_=onesb[:], compare_op=ALU.is_gt, fill=0.0,
                                    base=0, pattern=[[1, P]], channel_multiplier=-1).then_inc(consts, 1)

        @block.scalar
        def _(act):
            for b in range(B):
                tb = slice(b * TB, (b + 1) * TB)
                act.wait_ge(var_done, b + 1)
                nc.scalar.activation(r1[:, tb], v128[:, tb], ACT.Sqrt, bias=R["c_eps"],
                                     scale=1.0 / D).then_inc(std_done, 1)
            for k in range(NCH):
                act.wait_ge(zt_mm, k + 1)
                if k >= 2:
                    act.wait_ge(lg_mm, k - 1)
                nc.scalar.copy(YT[:, k % 2, :], pT[k % 2][:]).then_inc(zt_done, 1)
            act.wait_ge(ex_in, 1)
            nc.scalar.activation(EX[:], EX[:], ACT.Exp).then_inc(ex_done, 1)

        @block.vector
        def _(v):
            c = Chain(v, vs)

            def stats(b):
                tb = slice(b * TB, (b + 1) * TB)
                stats_of(nc, c, X[:, tb, :], st[:, tb, :], TB)
                finish_stats(nc, c, st[:, tb, :], mean[:, tb], v128[:, tb], t1[:, tb],
                             t2[:, tb]).then_inc(var_done, 1)

            def normed(b):
                tb = slice(b * TB, (b + 1) * TB)
                v.wait_ge(std_done, b + 1)
                c.run(nc.vector.reciprocal(r1[:, tb], r1[:, tb]))
                for t in range(b * TB, (b + 1) * TB):
                    z = nc.vector.tensor_scalar(Yn[:, t, :], X[:, t, :], mean[:, t:t + 1], r1[:, t:t + 1],
                                                ALU.subtract, ALU.mult)
                    if t % TB == TB - 1:
                        z.then_inc(z_done, 1)

            stats(0)
            for b in range(B):
                if b + 1 < B:
                    stats(b + 1)
                normed(b)
            for k in range(NCH):
                ts = slice(4 * k, 4 * k + 4)
                v.wait_ge(lg_mm, k + 1)
                c.run(nc.vector.tensor_copy(LG[:, ts, :], pL[k % 2][:, 0:4 * NE].rearrange("p (t e) -> p t e", t=4)))
                for t in range(4 * k, 4 * k + 4):
                    c.mark(nc.vector.max(top[:, t, :], LG[:, t, :]))
                c.wait()
                for t in range(4 * k, 4 * k + 4):
                    c.mark(nc.vector.max_index(ix[:, t, :], top[:, t, :], LG[:, t, :]))
                nc.vector.tensor_tensor(EX[:, ts, 0:NE], LG[:, ts, :], top[:, ts, 0:1].broadcast_to([P, 4, NE]),
                                        ALU.subtract).then_inc(lg_done, 1)
            c.wait()
            nc.vector.tensor_tensor(EX[:, :, NE], top[:, :, 1], top[:, :, 0], ALU.subtract).then_inc(ex_in, 1)
            c.run(nc.vector.tensor_copy(eidx[:], ix[:, :, 0:2]))
            v.wait_ge(consts, 2)
            for k in range(2):
                c.mark(nc.vector.tensor_tensor(M[:, :, k, :], iota[:].unsqueeze(1).broadcast_to([P, T, NE]),
                                               eidx[:, :, k:k + 1].broadcast_to([P, T, NE]), ALU.is_equal))
            c.wait()
            Mt = M[:].rearrange("p (b h r) k e -> p b h r (k e)", b=B, h=GR)
            c.run(nc.vector.memset(PF[:, :, 0, :], 0.0))
            for i in range(GT):
                add = nc.vector.tensor_tensor(PF[:, :, i + 1, :], PF[:, :, i, :], Mt[:, i // 2, :, i % 2, :], ALU.add)
                if i < GT - 1:
                    c.run(add)
                else:
                    add.then_inc(pf_done, 1)
            for h in range(GR):
                v.wait_ge(pos_mm, h + 1)
                src = pP[h % 2][:, 0:GT * 2 * NE].rearrange("p (b r k e) -> p b r (k e)", b=B, r=2, k=2)
                dst = LP[:].rearrange("p (b h r) k e -> p b h r (k e)", b=B, h=GR)[:, :, h, :, :]
                nc.vector.tensor_tensor(dst, src, Mt[:, :, h, :, :], ALU.mult).then_inc(pos_read, 1)
            v.wait_ge(pos_read, GR)
            c.run(nc.vector.tensor_reduce(p2[:], LP[:], AX.X, ALU.add))
            c.mark(nc.vector.tensor_scalar(valid[:], p2[:], CAP - 0.5, None, ALU.is_lt))
            c.run(nc.vector.tensor_scalar(p2[:], p2[:], float(CAP), None, ALU.min))
            c.run(nc.vector.scalar_tensor_tensor(sl[:], eidx[:], float(ROWS), p2[:], ALU.mult, ALU.add))
            c.mark(nc.vector.tensor_copy(R["take"], sl[:]))
            c.run(nc.vector.tensor_scalar(s2[:], valid[:], -BIG, BIG, ALU.mult, ALU.add))
            c.run(nc.vector.tensor_tensor(R["send"], sl[:], s2[:], ALU.add))
            v.wait_ge(ex_done, 1)
            c.run(nc.vector.tensor_reduce(zs[:], EX[:, :, 0:NE], AX.X, ALU.add))
            c.run(nc.vector.reciprocal(zs[:], zs[:]))
            c.mark(nc.vector.tensor_copy(g[:, :, 0], zs[:]))
            c.run(nc.vector.tensor_tensor(g[:, :, 1], zs[:], EX[:, :, NE], ALU.mult))
            c.run(nc.vector.tensor_tensor(g[:], g[:], valid[:], ALU.mult))
            c.run(nc.vector.tensor_tensor(gs[:], g[:, :, 0], g[:, :, 1], ALU.add))
            c.run(nc.vector.tensor_scalar(gs[:], gs[:], 1e-9, None, ALU.max))
            c.run(nc.vector.reciprocal(gs[:], gs[:]))
            c.run(nc.vector.tensor_tensor(R["gate"], g[:], gs[:].unsqueeze(2).broadcast_to([P, T, 2]), ALU.mult))
            c.run(nc.vector.tensor_tensor(LP[:], M[:], R["gate"].unsqueeze(3).broadcast_to([P, T, 2, NE]), ALU.mult))
            c.run(nc.vector.tensor_tensor(R["GD"][:], LP[:, :, 0, :], LP[:, :, 1, :], ALU.add))

        @block.tensor
        def _(pe):
            mm = nc.tensor.matmul
            pe.wait_ge(w_in, 16)

            def transposes(k):
                pe.wait_ge(z_done, k // 2 + 1)
                if k >= 2:
                    pe.wait_ge(zt_done, k - 1)
                for j in range(4):
                    tr = nc.tensor.transpose(pT[k % 2][:, j * P:(j + 1) * P], Yn[:, 4 * k + j, :], ident[:])
                tr.then_inc(zt_mm, 1)

            transposes(0)
            for k in range(NCH):
                if k + 1 < NCH:
                    transposes(k + 1)
                pe.wait_ge(zt_done, k + 1)
                if k >= 2:
                    pe.wait_ge(lg_done, k - 1)
                for j in range(4):
                    last = mm(pL[k % 2][:, j * NE:(j + 1) * NE], YT[:, k % 2, j * P:(j + 1) * P], wg[:],
                              start=True, stop=True)
                last.then_inc(lg_mm, 1)
            pe.wait_ge(pf_done, 1)
            for h in range(GR):
                if h >= 2:
                    pe.wait_ge(pos_read, h - 1)
                for i in range(GT):
                    o = pP[h % 2][:, i * 2 * NE:(i + 1) * 2 * NE]
                    mm(o, before[:], M[:, tile_of(h, i), :, :].rearrange("p k e -> p (k e)"), start=True, stop=False)
                    mm(o, onesb[:], PF[:, h, i, :], start=False, stop=False)
                    last = mm(o[:, NE:2 * NE], onesb[:], PF[:, h, GT, 0:NE], start=False, stop=True)
                last.then_inc(pos_mm, 1)


def rsqrt(nc, chain, v, y, t, scale, eps):
    chain.run(nc.vector.tensor_scalar(v, v, scale, eps, ALU.mult, ALU.add))
    chain.run(nc.vector.tensor_scalar(t.bitcast(I32), v.bitcast(I32), 1, None, ALU.logical_shift_right))
    chain.run(nc.vector.tensor_scalar(y.bitcast(I32), t.bitcast(I32), -1.0, float(0x5f3759df), ALU.mult, ALU.add))
    for _ in range(3):
        chain.run(nc.vector.tensor_tensor(t, y, y, ALU.mult))
        chain.run(nc.vector.scalar_tensor_tensor(t, t, -0.5, v, ALU.mult, ALU.mult))
        chain.run(nc.vector.scalar_tensor_tensor(y, t, 1.5, y, ALU.add, ALU.mult))


def expert_layers(nc, R, A, DR):
    with ExitStack() as ctx:
        sb = lambda n, s, d=F32: ctx.enter_context(nc.sbuf_tensor(n, s, d))
        pb = lambda n: ctx.enter_context(nc.psum_tensor(n, [P, 512], F32))
        sem = lambda n: ctx.enter_context(nc.semaphore(n))
        X, Yn, ident, W1, W2, GD = R["X"], R["Yn"], R["ident"], R["W1"], R["W2"], R["GD"]
        gate, take, send = R["gate"], R["take"], R["send"]
        XS = [sb(f"e_xs{i}", [ROWS, EB, D]) for i in range(2)]
        XT = [sb(f"e_xt{i}", [P, EB * ROWS]) for i in range(2)]
        HS = [sb(f"e_hs{i}", [ROWS, FF]) for i in range(3)]
        HL = [sb(f"e_hl{i}", [ROWS, 2, FF]) for i in range(3)]
        GA = [[sb(f"e_g{k}{i}", [P, FF]) for k in range(2)] for i in range(2)]
        TT = sb("e_t", [P, GT, FF])
        HT = [sb(f"e_ht{c}", [P, EB * ROWS]) for c in range(FC)]
        YS = [sb(f"e_ys{i}", [ROWS, EB, D]) for i in range(2)]
        YA = [[sb(f"e_ya{k}{i}", [P, D]) for k in range(2)] for i in range(2)]
        GTT = sb("e_gt", [NE, GT * P])
        b1, b2 = sb("e_b1", [NE, FF]), sb("e_b2", [NE, D])
        lnh, lno = sb("e_lnh", [P, 2, GR, FC]), sb("e_lno", [P, 2, D])
        st = sb("e_st", [P, GT, 6])
        mean, v128, r1, t1, t2 = (sb(f"e_s{i}", [P, GT]) for i in range(5))
        pX, pH, pN = pb("e_px"), [pb("e_ph0"), pb("e_ph1")], [pb("e_pn0"), pb("e_pn1")]
        pY, pG = pb("e_py"), [pb("e_pg0"), pb("e_pg1")]
        w_in = sem("e_w_in")
        (xt_mm, xt_done, h_mm, hs_done, t_bias, gt_mm, gt_done, b2_mm, b2_read, c_read, n_done, hn_mm, ht_done,
         y_mm, ys_done, y_read, o_done) = (sem("e_" + n) for n in (
             "xt_mm", "xt_done", "h_mm", "hs_done", "t_bias", "gt_mm", "gt_done", "b2_mm", "b2_read", "c_read",
             "n_done", "hn_mm", "ht_done", "y_mm", "ys_done", "y_read", "o_done"))
        sent = [sem(f"e_sent{h}") for h in range(GR)]
        hs_out = [sem(f"e_hs_out{i}") for i in range(3)]
        n_sent = [sem(f"e_n_sent{h}") for h in range(GR)]
        ys_out = [sem(f"e_ys_out{i}") for i in range(2)]
        xs_in = [sem(f"e_xs_in{i}") for i in range(2)]
        ga_in = [sem(f"e_ga_in{i}") for i in range(2)]
        hl_in = [sem(f"e_hl_in{i}") for i in range(3)]
        ya_in = [sem(f"e_ya_in{i}") for i in range(2)]
        out_done = sem("e_out_done")
        vs = sem("e_vec")
        block = ctx.enter_context(nc.Block())
        XD, HD_, YD = DR["x"], DR["h"], DR["y"]
        ORDER = [("u", 0), ("b", 0), ("u", 1), ("b", 1), ("w", 0), ("u", 2), ("b", 2), ("w", 1), ("u", 3), ("b", 3),
                 ("w", 2), ("w", 3)]
        ring = {}
        for s, h in ORDER:
            if s != "w":
                for j in range(NE if s == "u" else GT):
                    ring[s, h, j] = len(ring)

        def h_wait(pe, n):
            s, h, j = list(ring)[n]
            pe.wait_ge(hs_done if s == "u" else t_bias, h * (NE if s == "u" else GT) + j + 1)

        @block.sync
        def _(sp):
            sp.dma_start(b1[:], A["b1"]).then_inc(w_in, 16)
            sp.dma_start(b2[:], A["b2"]).then_inc(w_in, 16)
            sp.dma_start(lnh[:], A["ln_hid"]).then_inc(w_in, 16)
            sp.dma_start(lno[:], A["ln_out"].partition_broadcast(P)).then_inc(w_in, 16)

            def x_load(n):
                h, eb = n // NB, n % NB
                if eb == 0:
                    sp.wait_ge(sent[h], 2 * GT * 16)
                if n >= 2:
                    sp.wait_ge(xt_mm, n - 1)
                sp.dma_start(XS[n % 2][:], XD[h][eb * EB:(eb + 1) * EB, :, :].rearrange("e r d -> r e d")
                             ).then_inc(xs_in[n % 2], 16)

            def h_store(m):
                h, e = m // NE, m % NE
                sp.wait_ge(hs_done, m + 1)
                sp.dma_start(HD_[h][e, :, :], HS[m % 3][:]).then_inc(hs_out[m % 3], 16)

            def h_load(m):
                h, pr = m // (NE // 2), m % (NE // 2)
                if pr == 0:
                    sp.wait_ge(n_sent[h], 2 * GT * 16)
                if m >= 3:
                    sp.wait_ge(hn_mm, FC * ((m - 3) // 2 + 1))
                sp.dma_start(HL[m % 3][:], HD_[h][2 * pr:2 * pr + 2, :, :].rearrange("e r d -> r e d")
                             ).then_inc(hl_in[m % 3], 16)

            def y_store(n):
                h, eb = n // NB, n % NB
                sp.wait_ge(ys_done, n + 1)
                sp.dma_start(YD[h][eb * EB:(eb + 1) * EB, :, :].rearrange("e r d -> r e d"), YS[n % 2][:]
                             ).then_inc(ys_out[n % 2], 16)

            for s, h in ORDER:
                if s == "u":
                    x_load(h * NB)
                    for eb in range(NB):
                        if eb + 1 < NB:
                            x_load(h * NB + eb + 1)
                        for e in range(EB):
                            h_store(h * NE + eb * EB + e)
                if s == "w":
                    h_load(h * 2 * NB)
                    h_load(h * 2 * NB + 1)
                    h_load(h * 2 * NB + 2)
                    for eb in range(NB):
                        for j in range(3 + 2 * eb, min(5 + 2 * eb, 2 * NB)):
                            h_load(h * 2 * NB + j)
                        y_store(h * NB + eb)
            for h in range(GR):
                sp.wait_ge(o_done, h + 1)
                for b in range(B):
                    t = b * TB + 2 * h
                    sp.dma_start(DR["out"][t * P:(t + 2) * P, :].rearrange("(t p) d -> p t d", p=P),
                                 X[:, t:t + 2, :]).then_inc(out_done, 16)
            sp.wait_ge(out_done, 16 * GR * B)

        @block.gpsimd
        def _(pool):
            idx = lambda ap, t, k: bass.IndirectOffsetOnAxis(ap=ap[:, t, k:k + 1], axis=0)
            flat = lambda ap, h: ap[h].rearrange("e r d -> (e r) d")
            last_row = NE * ROWS - 1

            def scatter_x(h):
                for i in range(GT):
                    t = tile_of(h, i)
                    for k in range(2):
                        nc.gpsimd.indirect_dma_start(flat(XD, h), idx(send, t, k), Yn[:, t, :], None,
                                                     bounds_check=last_row, oob_is_err=False).then_inc(sent[h], 16)

            def gather_h(h):
                for i in range(3):
                    pool.wait_ge(hs_out[i], (h + 1) * NE // 3 * 16)
                for i in range(GT):
                    t, n = tile_of(h, i), h * GT + i
                    if n >= 2:
                        pool.wait_ge(c_read, n - 1)
                    for k in range(2):
                        nc.gpsimd.indirect_dma_start(GA[n % 2][k][:], None, flat(HD_, h), idx(take, t, k)
                                                     ).then_inc(ga_in[n % 2], 16)

            def scatter_n(h):
                for i in range(GT):
                    t = tile_of(h, i)
                    pool.wait_ge(n_done, h * GT + i + 1)
                    for k in range(2):
                        nc.gpsimd.indirect_dma_start(flat(HD_, h), idx(send, t, k), TT[:, i, :], None,
                                                     bounds_check=last_row, oob_is_err=False).then_inc(n_sent[h], 16)

            def gather_y(h):
                for i in range(2):
                    pool.wait_ge(ys_out[i], (h + 1) * NB // 2 * 16)
                for i in range(GT):
                    t, n = tile_of(h, i), h * GT + i
                    if n >= 2:
                        pool.wait_ge(y_read, n - 1)
                    for k in range(2):
                        nc.gpsimd.indirect_dma_start(YA[n % 2][k][:], None, flat(YD, h), idx(take, t, k)
                                                     ).then_inc(ya_in[n % 2], 16)

            pool.wait_ge(R["zero_out"], 16 * GR * 4)
            for stage, h in ((scatter_x, 0), (scatter_x, 1), (gather_h, 0), (scatter_n, 0), (scatter_x, 2),
                             (gather_h, 1), (scatter_n, 1), (gather_y, 0), (scatter_x, 3), (gather_h, 2),
                             (scatter_n, 2), (gather_y, 1), (gather_h, 3), (scatter_n, 3), (gather_y, 2),
                             (gather_y, 3)):
                stage(h)

        @block.tensor
        def _(pe):
            mm = nc.tensor.matmul
            pe.wait_ge(w_in, 64)
            pe.wait_ge(R["w_in"], 32)

            def x_transposes(n):
                pe.wait_ge(xs_in[n % 2], 16 * (n // 2 + 1))
                if n >= 1:
                    pe.wait_ge(xt_done, n)
                for e in range(EB):
                    tr = nc.tensor.transpose(pX[:, e * ROWS:(e + 1) * ROWS], XS[n % 2][:, e, :], ident[0:ROWS, 0:ROWS])
                tr.then_inc(xt_mm, 1)

            def h_free(key):
                n = ring[key]
                if n >= 2:
                    h_wait(pe, n - 2)
                return pH[n % 2]

            def y_block(n):
                h, eb = n // NB, n % NB
                for c in range(FC):
                    m = FC * n + c
                    if m >= 2:
                        pe.wait_ge(ht_done, m - 1)
                    for e in range(EB):
                        l = 2 * n + e // 2
                        if c == 0 and e % 2 == 0:
                            pe.wait_ge(hl_in[l % 3], 16 * (l // 3 + 1))
                        tr = nc.tensor.transpose(pN[m % 2][:, e * ROWS:(e + 1) * ROWS],
                                                 HL[l % 3][:, e % 2, c * P:(c + 1) * P], ident[0:ROWS, 0:ROWS])
                    tr.then_inc(hn_mm, 1)
                if n >= 1:
                    pe.wait_ge(ys_done, n)
                for c in range(FC):
                    pe.wait_ge(ht_done, FC * n + c + 1)
                    for e in range(EB):
                        last = mm(pY[0:ROWS, e * D:(e + 1) * D], HT[c][:, e * ROWS:(e + 1) * ROWS],
                                  W2[:, eb * EB + e, c, :], start=c == 0 and e == 0, stop=c == FC - 1,
                                  skip_group_check=True)
                    last.then_inc(y_mm, 1)

            for s, h in ORDER:
                if s == "u":
                    x_transposes(h * NB)
                    for eb in range(NB):
                        n = h * NB + eb
                        if eb + 1 < NB:
                            x_transposes(n + 1)
                        pe.wait_ge(xt_done, n + 1)
                        for e in range(EB):
                            mm(h_free(("u", h, eb * EB + e))[0:ROWS, :], XT[n % 2][:, e * ROWS:(e + 1) * ROWS],
                               W1[:, eb * EB + e, :], start=True, stop=True).then_inc(h_mm, 1)
                if s == "b":
                    for half in range(2):
                        if h >= 1:
                            pe.wait_ge(b2_read, 2 * h)
                        for j in range(4):
                            tr = nc.tensor.transpose(pG[half][0:NE, j * P:(j + 1) * P],
                                                     GD[:, tile_of(h, 4 * half + j), :], ident[:])
                        tr.then_inc(gt_mm, 1)
                    pe.wait_ge(gt_done, 2 * h + 2)
                    for half in range(2):
                        for j in range(4):
                            i = 4 * half + j
                            last = mm(pG[half][:, j * P:(j + 1) * P], GTT[:, i * P:(i + 1) * P], b2[:],
                                      start=True, stop=True)
                        last.then_inc(b2_mm, 1)
                    for i in range(GT):
                        mm(h_free(("b", h, i))[:], GTT[:, i * P:(i + 1) * P], b1[:],
                           start=True, stop=True).then_inc(h_mm, 1)
                if s == "w":
                    for eb in range(NB):
                        y_block(h * NB + eb)

        @block.scalar
        def _(act):
            def xt(n):
                act.wait_ge(xt_mm, n + 1)
                if n >= 2:
                    act.wait_ge(h_mm, ring["u", (n - 2) // NB, (n - 2) % NB * EB + EB - 1] + 1)
                nc.scalar.copy(XT[n % 2][:], pX[:, 0:EB * ROWS]).then_inc(xt_done, 1)

            act.wait_ge(w_in, 64)
            for s, h in ORDER:
                if s == "u":
                    xt(h * NB)
                    for eb in range(NB):
                        if eb + 1 < NB:
                            xt(h * NB + eb + 1)
                        for e in range(EB):
                            m = h * NE + eb * EB + e
                            r = ring["u", h, eb * EB + e]
                            act.wait_ge(h_mm, r + 1)
                            if m >= 3:
                                act.wait_ge(hs_out[m % 3], 16 * (m // 3))
                            nc.scalar.copy(HS[m % 3][:], pH[r % 2][0:ROWS, :]).then_inc(hs_done, 1)
                if s == "b":
                    for half in range(2):
                        act.wait_ge(gt_mm, 2 * h + half + 1)
                        nc.scalar.copy(GTT[:, half * CH:(half + 1) * CH], pG[half][0:NE, :]).then_inc(gt_done, 1)
                    if h >= 1:
                        act.wait_ge(n_sent[h - 1], 2 * GT * 16)
                    for i in range(GT):
                        r = ring["b", h, i]
                        act.wait_ge(h_mm, r + 1)
                        nc.scalar.copy(TT[:, i, :], pH[r % 2][:]).then_inc(t_bias, 1)
                if s == "w":
                    for eb in range(NB):
                        n = h * NB + eb
                        for c in range(FC):
                            m = FC * n + c
                            act.wait_ge(hn_mm, m + 1)
                            if n >= 1:
                                act.wait_ge(y_mm, FC * (n - 1) + c + 1)
                            nc.scalar.activation(HT[c][:], pN[m % 2][:, 0:EB * ROWS], ACT.Relu,
                                                 bias=lnh[:, 1, h, c:c + 1], scale=lnh[:, 0, h, c:c + 1]
                                                 ).then_inc(ht_done, 1)
                        act.wait_ge(y_mm, FC * n + FC)
                        if n >= 2:
                            act.wait_ge(ys_out[n % 2], 16 * (n // 2))
                        nc.scalar.copy(YS[n % 2][:], pY[0:ROWS, :].rearrange("p (e d) -> p e d", e=EB)
                                       ).then_inc(ys_done, 1)

        @block.vector
        def _(v):
            c = Chain(v, vs)
            group = lambda ap, h: ap.rearrange("p (b h r) d -> p b h r d", b=B, h=GR)[:, :, h, :, :]

            def combine(h):
                v.wait_ge(sent[h], 2 * GT * 16)
                for half in range(2):
                    v.wait_ge(b2_mm, 2 * h + half + 1)
                    y = Yn.rearrange("p (b h r) d -> p b h (r d)", b=B, h=GR)[:, 2 * half:2 * half + 2, h, :]
                    nc.vector.tensor_tensor(y, y, pG[half][:].rearrange("p (b q) -> p b q", b=2),
                                            ALU.add).then_inc(b2_read, 1)
                for i in range(GT):
                    t, n = tile_of(h, i), h * GT + i
                    v.wait_ge(t_bias, n + 1)
                    v.wait_ge(ga_in[n % 2], 32 * (n // 2 + 1))
                    c.run(nc.vector.scalar_tensor_tensor(TT[:, i, :], GA[n % 2][0][:], gate[:, t, 0:1], TT[:, i, :],
                                                         ALU.mult, ALU.add))
                    nc.vector.scalar_tensor_tensor(TT[:, i, :], GA[n % 2][1][:], gate[:, t, 1:2], TT[:, i, :],
                                                   ALU.mult, ALU.add).then_inc(c_read, 1)
                    v.wait_ge(c_read, n + 1)
                    c.mark(nc.vector.bn_stats(st[:, i, :], TT[:, i, :]))
                c.wait()
                c.run(finish_stats(nc, c, st[:], mean[:], v128[:], t1[:], t2[:], FF))
                rsqrt(nc, c, v128[:], r1[:], t1[:], 1.0 / FF, LN_EPS)
                for i in range(GT):
                    nc.vector.tensor_scalar(TT[:, i, :], TT[:, i, :], mean[:, i:i + 1], r1[:, i:i + 1],
                                            ALU.subtract, ALU.mult).then_inc(n_done, 1)

            def normalise(h, eps):
                for i in range(GT):
                    c.mark(nc.vector.bn_stats(st[:, i, :], Yn[:, tile_of(h, i), :]))
                c.wait()
                c.run(finish_stats(nc, c, st[:], mean[:], v128[:], t1[:], t2[:], D))
                rsqrt(nc, c, v128[:], r1[:], t1[:], 1.0 / D, eps)
                for i in range(GT):
                    y = Yn[:, tile_of(h, i), :]
                    c.mark(nc.vector.tensor_scalar(y, y, mean[:, i:i + 1], r1[:, i:i + 1], ALU.subtract, ALU.mult))
                c.wait()

            def output(h):
                for i in range(GT):
                    t, n = tile_of(h, i), h * GT + i
                    v.wait_ge(ya_in[n % 2], 32 * (n // 2 + 1))
                    c.run(nc.vector.scalar_tensor_tensor(Yn[:, t, :], YA[n % 2][0][:], gate[:, t, 0:1], Yn[:, t, :],
                                                         ALU.mult, ALU.add))
                    nc.vector.scalar_tensor_tensor(Yn[:, t, :], YA[n % 2][1][:], gate[:, t, 1:2], Yn[:, t, :],
                                                   ALU.mult, ALU.add).then_inc(y_read, 1)
                v.wait_ge(y_read, (h + 1) * GT)
                normalise(h, LN_EPS)
                for k, op in ((0, ALU.mult), (1, ALU.add)):
                    for b in range(B):
                        y = Yn[:, b * TB + 2 * h:b * TB + 2 * h + 2, :]
                        c.mark(nc.vector.tensor_tensor(y, y, lno[:, k:k + 1, :].broadcast_to([P, 2, D]), op))
                    c.wait()
                normalise(h, EPS)
                x = group(X[:], h).rearrange("p b r d -> p b (r d)")
                nc.vector.tensor_tensor(x, x, group(Yn, h).rearrange("p b r d -> p b (r d)"), ALU.add
                                        ).then_inc(o_done, 1)

            v.wait_ge(w_in, 64)
            for stage, h in ((combine, 0), (combine, 1), (output, 0), (combine, 2), (output, 1), (combine, 3),
                             (output, 2), (output, 3)):
                stage(h)


def experts(nc, R, A, out):
    with ExitStack() as ctx:
        sb = lambda n, s, d=F32: ctx.enter_context(nc.sbuf_tensor(n, s, d))
        R["GD"] = sb("gates_dense", [P, T, NE])
        R["gate"] = sb("gate", [P, T, 2])[:]
        R["take"], R["send"] = sb("take", [P, T, 2], I32)[:], sb("send", [P, T, 2], I32)[:]
        DR = {"x": R["x_rows"], "out": out,
              "h": [nc.dram_tensor(f"h_rows{h}", (NE, ROWS, FF), F32, kind="Internal").ap() for h in range(GR)],
              "y": [nc.dram_tensor(f"y_rows{h}", (NE, ROWS, D), F32, kind="Internal").ap() for h in range(GR)]}
        routing(nc, R, A)
        expert_layers(nc, R, A, DR)


def build(nc, A, out):
    with ExitStack() as ctx:
        sb = lambda n, s, d=F32: ctx.enter_context(nc.sbuf_tensor(n, s, d))
        consts = sb("consts", [P, 8])
        R = {
            "X": sb("x_res", [P, T, D]), "ident": sb("ident", [P, P]), "ones": sb("ones", [P, P]),
            "c_eps": consts[:, 0:1], "c_eps2": consts[:, 1:2],
        }
        with nc.sbuf_tensor("up_t", [P, FF], F32) as R["up_t"], nc.sbuf_tensor("down_t", [P, FF], F32) as R["down_t"]:
            first_attention(nc, R, A)
            feed_forward(nc, R, A)
        flag = sb("flag", [1, 8], I32)
        R["flag"] = flag[0:1, 0:1]
        R["V"] = sb("v_all", [P, UNITS, TB, 32])
        S = {n: nc.dram_tensor(f"stack_{n}", (B, P, NQ, 2, L), BF16, kind="Internal").ap() for n in "qk"}
        second_projections(nc, R, A, S)
        exact_maxima(nc, R, S)
        R["w_in"], R["zero_out"] = (ctx.enter_context(nc.semaphore(n)) for n in ("experts_in", "zero_out"))
        R["W1"], R["W2"] = sb("w_1", [P, NE, FF]), sb("w_2", [P, NE, FC, D])
        R["x_rows"] = [nc.dram_tensor(f"x_rows{h}", (NE, ROWS, D), F32, kind="Internal").ap() for h in range(GR)]
        with nc.sbuf_tensor("o_all", [P, T, D], F32) as R["O"]:
            second_scores(nc, R, A, S)
            second_output(nc, R, A)
        R["Yn"] = R["V"][:].rearrange("p n t e -> p (n t e)").rearrange("p (t d) -> p t d", d=D)
        experts(nc, R, A, out)


def layout(inputs):
    a = {k: np.asarray(v) for k, v in inputs.items()}
    f = lambda z: np.ascontiguousarray(z, dtype=np.float32)
    w, bq = a["L0_attn_qkv_w"], a["L0_attn_qkv_b"]
    got = {
        "x": f(a["L0_attn_x"].reshape(B * L, D)),
        "wq_t": f(w[0:D].T), "wk_t": f(w[D:2 * D].T), "wv": f(w[2 * D:]), "wv_t": f(w[2 * D:].T),
        "proj_t": f(a["L0_attn_proj_w"].T),
        "norm_w": f(a["L0_attn_norm_w"][:, None]), "norm_b": f(a["L0_attn_norm_b"][:, None]),
        "bv": f(bq[2 * D:, None]),
        "rows": f(np.stack([bq[0:D], bq[D:2 * D], a["L0_attn_proj_b"]])[None]),
        "w_up": f(a["L0_ffn_w_up"].T),
        "w_down": f(a["L0_ffn_w_down"].T.reshape(FC, P, D).transpose(1, 0, 2).reshape(P, FF)),
    }
    a2, dim, n, pair = np.meshgrid(range(2), range(8), range(4), range(2), indexing="ij")
    head = (4 * n + 2 * pair + a2).ravel()
    dim = dim.ravel()
    rows_a = 8 * head + 2 * (dim % 4) + dim // 4
    rows_b = 8 * head + 2 * (dim % 4) + 1 - dim // 4
    order = [("Wq", "bq", rows_a), ("Wq", "bq", rows_b), ("Wk", "bk", rows_a), ("Wk", "bk", rows_b)]
    got["w_ab"] = f(np.stack([a["L1_attn_" + w][r].T for w, _, r in order], axis=1))
    got["b_ab"] = f(np.stack([a["L1_attn_" + c][r] for _, c, r in order], axis=1))
    inv = (np.float32(1) / np.power(np.float32(10000), np.arange(0, HD, 2, dtype=np.float32) / np.float32(HD)))
    angle = np.outer(np.arange(L, dtype=np.float32), inv).astype(np.float32)
    sign = np.where(dim < 4, -1, 1).astype(np.float32)[:, None]
    got["cos_sin"] = f(np.stack([np.cos(angle)[:, dim % 4].T, sign * np.sin(angle)[:, dim % 4].T], axis=1))
    got["head_sum"] = f(((8 * a2 + 2 * n + pair).reshape(P, 1) == np.arange(HEADS)))
    got["ones_row"] = np.ones((3, 2 * L), mybir.dt.np(BF16))
    got["wv1_t"] = f(a["L1_attn_Wv"].T)
    got["bv1"] = f(a["L1_attn_bv"])
    got["wo_t"] = f(a["L1_attn_Wo"].T)
    got["bo"] = f(a["L1_attn_bo"])
    got["w_gate"] = f(a["L1_ffn_Wg"])
    got["w1"] = f(a["L1_ffn_W1"])
    got["w2"] = f(a["L1_ffn_W2"])
    got["b1"], got["b2"] = f(a["L1_ffn_b1"]), f(a["L1_ffn_b2"])
    ln = np.stack([a["L1_ffn_ln_hid_w"], a["L1_ffn_ln_hid_b"]])
    got["ln_hid"] = f(ln.reshape(2, GR, FC, P).transpose(3, 0, 1, 2))
    got["ln_out"] = f(np.stack([a["L1_ffn_ln_out_w"], a["L1_ffn_ln_out_b"]]))
    return got


def kernel(**inputs):
    import concourse.bacc as bacc
    from concourse.bass_utils import run_bass_kernel_spmd as run

    nc = bacc.Bacc("TRN2", target_bir_lowering=False, num_devices=1)
    arrays = layout(inputs)
    A = {k: nc.dram_tensor(f"in_{k}", z.shape, mybir.dt.from_np(z.dtype), kind="ExternalInput").ap()
         for k, z in arrays.items()}
    out = nc.dram_tensor("out_x", (B * L, D), F32, kind="ExternalOutput").ap()
    build(nc, A, out)
    r = run(nc, [{f"in_{k}": z for k, z in arrays.items()}], core_ids=[0])
    return r.results[0]["out_x"].reshape(B, L, D)
```

```python
from contextlib import ExitStack

import numpy as np
import concourse.bass as bass
from concourse import mybir

F32 = mybir.dt.float32
BF16 = mybir.dt.bfloat16
I32 = mybir.dt.int32
ALU = mybir.AluOpType
ACT = mybir.ActivationFunctionType
AX = mybir.AxisListType

P = 128
B, L, D = 4, 1024, 128
T = B * L // P
TB = L // P
FF = 512
FC = FF // P
CH = 512
NCH = B * L // CH
EPS = 1e-5
LN_EPS = 1e-6
HEADS, HD = 16, 8
NQ = HEADS // 4


class Chain:

    def __init__(self, engine, sem):
        self.engine, self.sem, self.n = engine, sem, 0

    def mark(self, op):
        op.then_inc(self.sem, 1)
        self.n += 1
        return op

    def wait(self):
        self.engine.wait_ge(self.sem, self.n)

    def run(self, op):
        self.mark(op)
        self.wait()


def stats_of(nc, chain, src, st, nt):
    for t in range(nt):
        chain.mark(nc.vector.bn_stats(st[:, t, :], src[:, t, :]))
    chain.wait()


def finish_stats(nc, chain, st, mean, vn, t1, t2, n=D):
    chain.mark(nc.vector.tensor_tensor(t1, st[:, :, 1], st[:, :, 4], ALU.add))
    chain.mark(nc.vector.tensor_tensor(t2, st[:, :, 1], st[:, :, 4], ALU.subtract))
    chain.run(nc.vector.tensor_tensor(vn, st[:, :, 2], st[:, :, 5], ALU.add))
    chain.mark(nc.vector.tensor_scalar(mean, t1, 0.5, None, ALU.mult))
    chain.run(nc.vector.tensor_tensor(t2, t2, t2, ALU.mult))
    return nc.vector.scalar_tensor_tensor(vn, t2, n / 4.0, vn, ALU.mult, ALU.add)


def clear_semaphores(pool, R):
    for s in R.pop("used", ()):
        pool.sem_clear(s)


def rsqrt(nc, chain, v, y, t, scale, eps):
    chain.run(nc.vector.tensor_scalar(v, v, scale, eps, ALU.mult, ALU.add))
    chain.run(nc.vector.tensor_scalar(t.bitcast(I32), v.bitcast(I32), 1, None, ALU.logical_shift_right))
    chain.run(nc.vector.tensor_scalar(y.bitcast(I32), t.bitcast(I32), -1.0, float(0x5f3759df), ALU.mult, ALU.add))
    for _ in range(3):
        chain.run(nc.vector.tensor_tensor(t, y, y, ALU.mult))
        chain.run(nc.vector.scalar_tensor_tensor(t, t, -0.5, v, ALU.mult, ALU.mult))
        chain.run(nc.vector.scalar_tensor_tensor(y, t, 1.5, y, ALU.add, ALU.mult))


def first_attention(nc, R, A):
    with ExitStack() as ctx:
        sb = lambda n, s, d=F32: ctx.enter_context(nc.sbuf_tensor(n, s, d))
        pb = lambda n: ctx.enter_context(nc.psum_tensor(n, [P, 512], F32))
        used = []
        sem = lambda n: used.append(ctx.enter_context(nc.semaphore(n))) or used[-1]
        X, ident, ones = R["X"], R["ident"], R["ones"]
        Y = sb("a_y", [P, T, D])
        Z = sb("a_z", [P, T, D + 4])
        ZT = sb("a_zt", [P, B * L])
        wq, wk, wv, wvt, pj = (sb(f"a_{n}", [P, P]) for n in ("wq", "wk", "wv", "wvt", "pj"))
        wqs, wks = sb("a_wqs", [P, P]), sb("a_wks", [P, P])
        nw, nb, bvc = sb("a_nw", [P, 1]), sb("a_nb", [P, 1]), sb("a_bv", [P, 1])
        rows = sb("a_rows", [1, 3, P])
        rows2 = sb("a_rows2", [1, 2, P])
        bvf = sb("a_bvf", [P, 1])
        st = sb("a_st", [P, T, 6])
        mean, v128, r1, r2, t1, t2 = (sb(f"a_s{i}", [P, T]) for i in range(6))
        Gs = sb("a_g", [P, B, D + 1])
        gr = sb("a_gr", [1, B, P])
        T1 = sb("a_t1", [P, B, P])
        rr = sb("a_rr", [1, B, P])
        W = sb("a_w", [P, B, P])
        nm, den = sb("a_nm", [P, B]), sb("a_den", [P, B])
        Ms, N1 = sb("a_m", [P, B, P]), sb("a_n", [P, B, P])
        bvb = sb("a_bvb", [P, P])
        nmr = sb("a_nmr", [P, T])
        up, dn, pk = sb("a_up", [P, FF]), sb("a_dn", [P, FF]), sb("a_pk", [P, FF])
        ab, thr = sb("a_ab", [P, 2]), sb("a_thr", [P, 4])
        pT = [pb("a_pt0"), pb("a_pt1")]
        pG, pR, pS, pM = pb("a_pg"), pb("a_pr"), pb("a_ps"), pb("a_pm")
        pO = [pb("a_po0"), pb("a_po1")]
        pW = [pG, pS, pO[0], pO[1]]
        pU = [pM, pT[0]]
        x_in = [sem(f"x_in{b}") for b in range(B)]
        w_in = sem("w_in")
        ident_done, ones_done = sem("ident_done"), sem("ones_done")
        var_done, std_done, z_done = sem("var_done"), sem("std_done"), sem("z_done")
        folded, bias_mm = sem("folded"), sem("bias_mm")
        zt_mm, zt_done, g_mm, g_done = sem("zt_mm"), sem("zt_done"), sem("g_mm"), sem("g_done")
        r_mm, r_done, b_read = sem("r_mm"), sem("r_done"), sem("b_read")
        t1_mm, t1_done, s_mm, nm_done, exp_done, w_done = (sem(n) for n in (
            "t1_mm", "t1_done", "s_mm", "nm_done", "exp_done", "w_done"))
        m_mm, m_done, n_mm, n_done = sem("m_mm"), sem("m_done"), sem("n_mm"), sem("n_done")
        o_mm, o_read, abs_done, abs_mm = sem("o_mm"), sem("o_read"), sem("abs_done"), sem("abs_mm")
        r_ready, ln_done, nmr_done, y_done = sem("r_ready"), sem("ln_done"), sem("nmr_done"), sem("y_done")
        vs, ps = sem("a_vec"), sem("a_pool")
        block = ctx.enter_context(nc.Block())

        @block.sync
        def _(sp):
            for b in range(B):
                sp.dma_start(X[:, b * TB:(b + 1) * TB, :],
                             A["x"][b * L:(b + 1) * L, :].rearrange("(t p) d -> p t d", p=P)).then_inc(x_in[b], 16)

        @block.scalar
        def _(act):
            for dst, src in ((wq, "wq_t"), (wk, "wk_t"), (wv, "wv"), (wvt, "wv_t"), (pj, "proj_t"),
                             (nw, "norm_w"), (nb, "norm_b"), (bvc, "bv")):
                act.dma_start(dst[:], A[src]).then_inc(w_in, 16)
            act.dma_start(rows[:], A["rows"]).then_inc(w_in, 16)
            act.dma_start(up[:], A["w_up"]).then_inc(w_in, 16)
            act.dma_start(dn[:], A["w_down"]).then_inc(w_in, 16)
            for b in range(B):
                tb = slice(b * TB, (b + 1) * TB)
                act.wait_ge(var_done, b + 1)
                nc.scalar.activation(r1[:, tb], v128[:, tb], ACT.Sqrt, bias=R["c_eps"], scale=1.0 / D)
                nc.scalar.activation(r2[:, tb], v128[:, tb], ACT.Sqrt, bias=R["c_eps2"],
                                     scale=(1.0 + EPS) / D).then_inc(std_done, 1)
            for k in range(2 * B):
                act.wait_ge(zt_mm, k + 1)
                nc.scalar.copy(ZT[:, k * CH:(k + 1) * CH], pT[k % 2][:]).then_inc(zt_done, 1)
            for b in range(B):
                act.wait_ge(nm_done, b + 1)
                nc.scalar.activation(W[:, b, :], pW[b][:, 0:P], ACT.Exp, bias=nm[:, b:b + 1],
                                     scale=1.0 / 32.0, accum_out=den[:, b:b + 1]).then_inc(exp_done, 1)
            def std(b):
                tb = slice(b * TB, (b + 1) * TB)
                act.wait_ge(var_done, B + b + 1)
                nc.scalar.activation(r1[:, tb], v128[:, tb], ACT.Sqrt, bias=R["c_eps"],
                                     scale=1.0 / D).then_inc(std_done, 1)

            def normed(b):
                act.wait_ge(nmr_done, b + 1)
                for t in range(b * TB, (b + 1) * TB):
                    y = nc.scalar.activation(Y[:, t, :], Y[:, t, :], ACT.Identity, bias=nmr[:, t:t + 1],
                                             scale=r1[:, t:t + 1])
                y.then_inc(y_done, 1)

            std(0)
            for b in range(B):
                if b + 1 < B:
                    std(b + 1)
                if b < B - 1:
                    normed(b)

        @block.gpsimd
        def _(pool):
            nc.gpsimd.memset(R["c_eps"], EPS).then_inc(ones_done, 1)
            nc.gpsimd.memset(R["c_eps2"], EPS * EPS).then_inc(ones_done, 1)
            nc.gpsimd.memset(R["c_ln_eps"], LN_EPS).then_inc(ones_done, 1)
            nc.gpsimd.memset(ones[:], 1.0).then_inc(ones_done, 1)
            nc.gpsimd.memset(Z[:, :, D:D + 1], 1.0).then_inc(ones_done, 1)
            nc.gpsimd.memset(ident[:], 0.0).then_inc(ps, 1)
            pool.wait_ge(ps, 1)
            nc.gpsimd.affine_select(out=ident[:], in_=ident[:], compare_op=ALU.not_equal, fill=1.0,
                                    base=0, pattern=[[-1, P]], channel_multiplier=1).then_inc(ident_done, 1)
            for b in range(B):
                pool.wait_ge(r_ready, b + 1)
                for t in range(b * TB, (b + 1) * TB):
                    y = nc.gpsimd.tensor_scalar(Y[:, t, :], X[:, t, :], mean[:, t:t + 1], r1[:, t:t + 1],
                                                ALU.subtract, ALU.mult)
                y.then_inc(ln_done, 1)
            for b in range(B - 1):
                tb = slice(b * TB, (b + 1) * TB)
                pool.wait_ge(y_done, b + 1)
                nc.gpsimd.tensor_tensor(X[:, tb, :], X[:, tb, :], Y[:, tb, :], ALU.add).then_inc(ps, 1)
            pool.wait_ge(ps, B)

        @block.vector
        def _(v):
            c = Chain(v, vs)

            def fold_weights():
                v.wait_ge(w_in, 11 * 16)
                c.mark(nc.vector.tensor_scalar(wqs[:], wq[:], nw[:], None, ALU.mult))
                nc.vector.tensor_scalar(wks[:], wk[:], nw[:], None, ALU.mult).then_inc(folded, 1)
                c.mark(nc.vector.tensor_reduce(ab[:, 0:1], up[:], AX.X, ALU.add, apply_absolute_value=True))
                nc.vector.tensor_reduce(ab[:, 1:2], dn[:], AX.X, ALU.add,
                                        apply_absolute_value=True).then_inc(abs_done, 1)
                v.wait_ge(bias_mm, 1)
                c.mark(nc.vector.tensor_tensor(rows2[:], rows[:, 0:2, :],
                                               pM[0:1, 0:2 * P].rearrange("a (r k) -> a r k", r=2), ALU.add))
                nc.vector.tensor_tensor(bvf[:], bvc[:], pM[:, 2 * P:2 * P + 1], ALU.add).then_inc(folded, 1)
                v.wait_ge(folded, 2)
                c.mark(nc.vector.tensor_scalar(bvb[:], ones[:], bvf[:], None, ALU.mult))

            def thresholds():
                v.wait_ge(abs_mm, 1)
                c.mark(nc.vector.tensor_scalar(thr[:, 0:2], pM[:, 0:2], 0.5 / (D * FF), None, ALU.mult))
                c.mark(nc.vector.tensor_scalar(thr[:, 2:4], pM[:, 0:2], -0.5 / (D * FF), None, ALU.mult))

            def ternary():
                for w, out, k in ((up, R["up_t"], 0), (dn, R["down_t"], 1)):
                    c.run(nc.vector.tensor_scalar(pk[:], w[:], thr[:, 2 + k:3 + k], None, ALU.is_lt))
                    c.run(nc.vector.scalar_tensor_tensor(out[:], w[:], thr[:, k:k + 1], pk[:],
                                                         ALU.is_gt, ALU.subtract))

            def stats(b, src):
                tb = slice(b * TB, (b + 1) * TB)
                stats_of(nc, c, src[:, tb, :], st[:, tb, :], TB)
                finish_stats(nc, c, st[:, tb, :], mean[:, tb], v128[:, tb], t1[:, tb],
                             t2[:, tb]).then_inc(var_done, 1)

            def normed(b):
                tb = slice(b * TB, (b + 1) * TB)
                v.wait_ge(std_done, b + 1)
                c.mark(nc.vector.reciprocal(r2[:, tb], r2[:, tb]))
                nc.vector.reciprocal(r1[:, tb], r1[:, tb]).then_inc(r_ready, 1)
                c.wait()
                for t in range(b * TB, (b + 1) * TB):
                    z = nc.vector.tensor_scalar(Z[:, t, 0:D], X[:, t, :], mean[:, t:t + 1], r2[:, t:t + 1],
                                                ALU.subtract, ALU.mult)
                    if t % TB == TB - 1:
                        z.then_inc(z_done, 1)

            def score_max(b):
                v.wait_ge(s_mm, b + 1)
                c.run(nc.vector.tensor_reduce(nm[:, b:b + 1], pW[b][:, 0:P], AX.X, ALU.max, negate=True))
                nc.vector.tensor_scalar(nm[:, b:b + 1], nm[:, b:b + 1], 1.0 / 32.0, None,
                                        ALU.mult).then_inc(nm_done, 1)

            def m_copy(b):
                v.wait_ge(m_mm, b + 1)
                nc.vector.tensor_copy(Ms[:, b, :], pM[:, 0:P]).then_inc(m_done, 1)

            def n_copy(b):
                tb = slice(b * TB, (b + 1) * TB)
                v.wait_ge(n_mm, b + 1)
                nc.vector.tensor_scalar(N1[:, b, :], pM[:, P:2 * P], nw[:], None, ALU.mult).then_inc(n_done, 1)
                v.wait_ge(ln_done, b + 1)
                nc.vector.tensor_tensor(Y[:, tb, :], Y[:, tb, :],
                                        pM[:, 2 * P:3 * P].unsqueeze(1).broadcast_to([P, TB, P]),
                                        ALU.add).then_inc(b_read, 1)

            def add_output(b, k):
                t0 = b * TB + 4 * k
                v.wait_ge(b_read, b + 1)
                v.wait_ge(o_mm, 2 * b + k + 1)
                nc.vector.tensor_tensor(Y[:, t0:t0 + 4, :], Y[:, t0:t0 + 4, :],
                                        pO[k][:].rearrange("p (t d) -> p t d", t=4), ALU.add).then_inc(o_read, 1)

            def scales(b):
                tb = slice(b * TB, (b + 1) * TB)
                v.wait_ge(std_done, B + b + 1)
                c.run(nc.vector.reciprocal(r1[:, tb], r1[:, tb]))
                nc.vector.scalar_tensor_tensor(nmr[:, tb], mean[:, tb], -1.0, r1[:, tb], ALU.mult,
                                               ALU.mult).then_inc(nmr_done, 1)

            v.wait_ge(ones_done, 5)
            v.wait_ge(x_in[0], 16)
            stats(0, X)
            for b in range(B):
                if b + 1 < B:
                    v.wait_ge(x_in[b + 1], 16)
                    stats(b + 1, X)
                normed(b)
                if b == 0:
                    fold_weights()
                if b == 1:
                    thresholds()
            for b in range(B):
                v.wait_ge(g_mm, b + 1)
                nc.vector.tensor_copy(Gs[:, b, :], pW[b][:, 0:D + 1]).then_inc(g_done, 1)
            v.wait_ge(r_mm, 1)
            nc.vector.tensor_copy(gr[:], pR[0:1, :].rearrange("p (b d) -> p b d", b=B)).then_inc(r_done, 1)
            nc.vector.scalar_tensor_tensor(rr[:], rows2[:, 1:2, :].broadcast_to([1, B, P]), float(L),
                                           pT[1][0:1, :].rearrange("p (b d) -> p b d", b=B),
                                           ALU.mult, ALU.add).then_inc(r_done, 1)
            for b in range(B):
                v.wait_ge(t1_mm, b + 1)
                nc.vector.tensor_copy(T1[:, b, :], pU[b % 2][:, 0:P]).then_inc(t1_done, 1)
                if b >= 1:
                    score_max(b - 1)
            score_max(B - 1)
            ternary()
            for b in range(B):
                v.wait_ge(exp_done, b + 1)
                c.run(nc.vector.reciprocal(den[:, b:b + 1], den[:, b:b + 1]))
                nc.vector.tensor_scalar(W[:, b, :], W[:, b, :], den[:, b:b + 1], None, ALU.mult).then_inc(w_done, 1)
                if b == 0:
                    m_copy(0)
            n_copy(0)
            for b in range(B):
                add_output(b, 0)
                if b + 1 < B:
                    m_copy(b + 1)
                add_output(b, 1)
                if b + 1 < B:
                    n_copy(b + 1)
                v.wait_ge(o_read, 2 * b + 2)
                stats(b, Y)
                if b >= 1:
                    scales(b - 1)
            scales(B - 1)
            v.wait_ge(nmr_done, B)
            for t in range(T - TB, T):
                c.mark(nc.vector.tensor_scalar(Y[:, t, :], Y[:, t, :], r1[:, t:t + 1], nmr[:, t:t + 1],
                                               ALU.mult, ALU.add))
            c.wait()
            c.run(nc.vector.tensor_tensor(X[:, T - TB:, :], X[:, T - TB:, :], Y[:, T - TB:, :], ALU.add))

        @block.tensor
        def _(pe):
            mm = nc.tensor.matmul
            pe.wait_ge(folded, 1)
            pe.wait_ge(ones_done, 5)
            pe.wait_ge(ident_done, 1)
            mm(pM[0:1, 0:P], nb[:], wq[:], start=True, stop=True)
            mm(pM[0:1, P:2 * P], nb[:], wk[:], start=True, stop=True)
            mm(pM[:, 2 * P:2 * P + 1], wvt[:], nb[:], start=True, stop=True).then_inc(bias_mm, 1)
            for b in range(B):
                pe.wait_ge(z_done, b + 1)
                for k in range(2):
                    if 2 * b + k >= 2:
                        pe.wait_ge(zt_done, 2 * b + k - 1)
                    for j in range(4):
                        tr = nc.tensor.transpose(pT[k][:, j * P:(j + 1) * P], Z[:, b * TB + 4 * k + j, 0:D], ident[:])
                    tr.then_inc(zt_mm, 1)
                if b == 0:
                    pe.wait_ge(folded, 2)
                    pe.wait_ge(abs_done, 1)
                    mm(pM[:, 0:2], ones[:], ab[:], start=True, stop=True).then_inc(abs_mm, 1)
                for t in range(b * TB, (b + 1) * TB):
                    g = mm(pW[b][:, 0:D + 1], Z[:, t, 0:D], Z[:, t, 0:D + 1], start=t % TB == 0, stop=t % TB == TB - 1)
                g.then_inc(g_mm, 1)
            for b in range(B):
                pe.wait_ge(g_done, b + 1)
                if b == 0:
                    pe.wait_ge(zt_done, 8)
                mm(pR[0:1, b * P:(b + 1) * P], Gs[:, b, D:D + 1], ident[:], start=True, stop=True)
                s_wk = mm(pT[1][0:1, b * P:(b + 1) * P], Gs[:, b, D:D + 1], wks[:], start=True, stop=True)
            s_wk.then_inc(r_mm, 1)
            pe.wait_ge(r_done, 2)

            def t1(b):
                if b >= 2:
                    pe.wait_ge(t1_done, b - 1)
                mm(pU[b % 2][:, 0:P], Gs[:, b, 0:D], wks[:], start=True, stop=False)
                mm(pU[b % 2][:, 0:P], gr[:, b, :], rows2[:, 1, :], start=False, stop=True).then_inc(t1_mm, 1)

            def score(b):
                pe.wait_ge(t1_done, b + 1)
                mm(pW[b][:, 0:P], wqs[:], T1[:, b, :], start=True, stop=False)
                mm(pW[b][:, 0:P], rows2[:, 0, :], rr[:, b, :], start=False, stop=True).then_inc(s_mm, 1)

            def m(b):
                pe.wait_ge(w_done, b + 1)
                if b == 0:
                    pe.wait_ge(t1_done, B)
                else:
                    pe.wait_ge(b_read, b)
                mm(pM[:, 0:P], W[:, b, :], pj[:], start=True, stop=True).then_inc(m_mm, 1)

            def n(b):
                pe.wait_ge(m_done, b + 1)
                mm(pM[:, P:2 * P], wv[:], Ms[:, b, :], start=True, stop=True)
                mm(pM[:, 2 * P:3 * P], bvb[:], Ms[:, b, :], start=True, stop=False)
                mm(pM[:, 2 * P:3 * P], ones[0:1, :], rows[:, 2, :], start=False, stop=True).then_inc(n_mm, 1)

            def output(b, k):
                if b >= 1:
                    pe.wait_ge(o_read, 2 * b + k - 1)
                for j in range(4):
                    t = b * TB + 4 * k + j
                    last = mm(pO[k][:, j * P:(j + 1) * P], ZT[:, t * P:(t + 1) * P], N1[:, b, :], start=True, stop=True)
                last.then_inc(o_mm, 1)

            t1(0)
            for b in range(B):
                if b + 1 < B:
                    t1(b + 1)
                score(b)
            m(0)
            n(0)
            pe.wait_ge(exp_done, B)
            for b in range(B):
                pe.wait_ge(n_done, b + 1)
                output(b, 0)
                if b + 1 < B:
                    m(b + 1)
                output(b, 1)
                if b + 1 < B:
                    n(b + 1)
        R["used"] = used


def feed_forward(nc, R, A):
    with ExitStack() as ctx:
        sb = lambda n, s, d=F32: ctx.enter_context(nc.sbuf_tensor(n, s, d))
        pb = lambda n: ctx.enter_context(nc.psum_tensor(n, [P, 512], F32))
        used = []
        sem = lambda n: used.append(ctx.enter_context(nc.semaphore(n))) or used[-1]
        X, ident, ones = R["X"], R["ident"], R["ones"]
        Z = sb("f_z", [P, T, D])
        ZT = sb("f_zt", [P, B * L])
        H = sb("f_h", [P, 2, FC, CH])
        SQ = sb("f_sq", [P, 3, FC, CH])
        O = sb("f_o", [P, T, D])
        st = sb("f_st", [P, T, 6])
        mean, v128, r1, r2, t1, t2, ssq, mean2, q1, q2, nmr = (sb(f"f_s{i}", [P, T]) for i in range(11))
        PARTS = (slice(0, 3 * TB), slice(3 * TB, T))
        pT = [pb("f_pt0"), pb("f_pt1")]
        pU = [pb("f_pu0"), pb("f_pu1")]
        pD = [pb("f_pd0"), pb("f_pd1")]
        pQ = [pb("f_pq0"), pb("f_pq1")]
        var_done, std_done, z_done, zt_mm, zt_done = (sem(n) for n in (
            "var_done", "std_done", "z_done", "zt_mm", "zt_done"))
        up_mm, h_done, sq_done, down_mm, o_read = (sem(n) for n in (
            "up_mm", "h_done", "sq_done", "down_mm", "o_read"))
        s_done, rms_done, u_done = sem("s_done"), sem("rms_done"), sem("u_done")
        sqs_done, sum_mm, q_read, scale_done, u2_done = (sem(n) for n in (
            "sqs_done", "sum_mm", "q_read", "scale_done", "u2_done"))
        vs, ps = sem("f_vec"), sem("f_pool")
        block = ctx.enter_context(nc.Block())

        @block.scalar
        def _(act):
            def std(b):
                tb = slice(b * TB, (b + 1) * TB)
                act.wait_ge(var_done, b + 1)
                nc.scalar.activation(r1[:, tb], v128[:, tb], ACT.Sqrt, bias=R["c_eps"], scale=1.0 / D)
                nc.scalar.activation(r2[:, tb], v128[:, tb], ACT.Sqrt, scale=1.0 / D).then_inc(std_done, 1)

            def zt(k):
                act.wait_ge(zt_mm, k + 1)
                nc.scalar.copy(ZT[:, k * CH:(k + 1) * CH], pT[k % 2][:]).then_inc(zt_done, 1)

            def deviations(part, ts):
                act.wait_ge(s_done, 2 * part + 1)
                nc.scalar.activation(q1[:, ts], ssq[:, ts], ACT.Sqrt, scale=1.0 / FF).then_inc(rms_done, 1)
                act.wait_ge(s_done, 2 * part + 2)
                nc.scalar.activation(q2[:, ts], v128[:, ts], ACT.Sqrt, bias=R["c_eps"],
                                     scale=1.0 / D).then_inc(rms_done, 1)

            std(0)
            zt(0)
            for b in range(1, B):
                std(b)
            for k in range(NCH):
                if k + 1 < NCH:
                    zt(k + 1)
                if k == NCH - 1:
                    deviations(0, PARTS[0])
                if k >= 2:
                    act.wait_ge(down_mm, k - 1)
                    act.wait_ge(sq_done, FC * (k - 1))
                for f in range(FC):
                    act.wait_ge(up_mm, FC * k + f + 1)
                    nc.scalar.activation(H[:, k % 2, f, :], pU[f % 2][:], ACT.Gelu).then_inc(h_done, 1)
            act.wait_ge(scale_done, 1)
            for t in range(2 * TB):
                u = nc.scalar.activation(Z[:, t, :], O[:, t, :], ACT.Identity, bias=nmr[:, t:t + 1],
                                         scale=q1[:, t:t + 1])
                if t % TB == TB - 1:
                    u.then_inc(u_done, 1)
            deviations(1, PARTS[1])

        @block.gpsimd
        def _(pool):
            clear_semaphores(pool, R)
            for k in range(NCH):
                pool.wait_ge(sq_done, FC * (k + 1))
                nc.gpsimd.tensor_tensor(SQ[:, k % 3, 0:2, :], SQ[:, k % 3, 0:2, :], SQ[:, k % 3, 2:4, :], ALU.add
                                        ).then_inc(ps, 1)
                pool.wait_ge(ps, k + 1)
                nc.gpsimd.tensor_tensor(SQ[:, k % 3, 0, :], SQ[:, k % 3, 0, :], SQ[:, k % 3, 1, :], ALU.add
                                        ).then_inc(sqs_done, 1)
            pool.wait_ge(u2_done, 1)
            nc.gpsimd.tensor_tensor(X[:, 2 * TB:3 * TB, :], X[:, 2 * TB:3 * TB, :], Z[:, 2 * TB:3 * TB, :], ALU.add
                                    ).then_inc(ps, 1)
            for b in range(2):
                tb = slice(b * TB, (b + 1) * TB)
                pool.wait_ge(u_done, b + 1)
                nc.gpsimd.tensor_tensor(X[:, tb, :], X[:, tb, :], Z[:, tb, :], ALU.add).then_inc(ps, 1)
            pool.wait_ge(ps, NCH + 3)

        @block.vector
        def _(v):
            c = Chain(v, vs)

            def stats(b):
                tb = slice(b * TB, (b + 1) * TB)
                stats_of(nc, c, X[:, tb, :], st[:, tb, :], TB)
                finish_stats(nc, c, st[:, tb, :], mean[:, tb], v128[:, tb], t1[:, tb],
                             t2[:, tb]).then_inc(var_done, 1)

            def normed(b):
                tb = slice(b * TB, (b + 1) * TB)
                v.wait_ge(std_done, b + 1)
                c.run(nc.vector.reciprocal(r1[:, tb], r1[:, tb]))
                c.run(nc.vector.tensor_tensor(r2[:, tb], r2[:, tb], r1[:, tb], ALU.mult))
                c.run(nc.vector.tensor_scalar(r2[:, tb], r2[:, tb], 1e-8, None, ALU.add))
                c.run(nc.vector.reciprocal(r2[:, tb], r2[:, tb]))
                c.run(nc.vector.tensor_tensor(r1[:, tb], r2[:, tb], r1[:, tb], ALU.mult))
                for t in range(b * TB, (b + 1) * TB):
                    z = nc.vector.tensor_scalar(Z[:, t, :], X[:, t, :], mean[:, t:t + 1], r1[:, t:t + 1],
                                                ALU.subtract, ALU.mult)
                    if t % TB == TB - 1:
                        z.then_inc(z_done, 1)

            def squares(k):
                for f in range(FC):
                    v.wait_ge(h_done, FC * k + f + 1)
                    if k >= 3 and f == 0:
                        v.wait_ge(sum_mm, k - 2)
                    nc.vector.tensor_tensor(SQ[:, k % 3, f, :], H[:, k % 2, f, :], H[:, k % 2, f, :],
                                            ALU.mult).then_inc(sq_done, 1)

            def outputs(k):
                ts = slice(4 * k, 4 * k + 4)
                v.wait_ge(down_mm, k + 1)
                nc.vector.tensor_copy(O[:, ts, :], pD[k % 2][:].rearrange("p (t d) -> p t d", t=4)).then_inc(o_read, 1)
                v.wait_ge(sum_mm, k + 1)
                nc.vector.tensor_copy(ssq[:, ts], pQ[k % 2][:, 0:4]).then_inc(q_read, 1)
                v.wait_ge(o_read, k + 1)
                for t in range(4 * k, 4 * k + 4):
                    c.mark(nc.vector.bn_stats(st[:, t, :], O[:, t, :]))

            def scales(part, ts):
                c.wait()
                v.wait_ge(q_read, (NCH - 2, NCH)[part])
                finish_stats(nc, c, st[:, ts], mean2[:, ts], v128[:, ts], t1[:, ts], t2[:, ts]).then_inc(s_done, 1)
                v.wait_ge(rms_done, 2 * part + 1)
                c.run(nc.vector.tensor_scalar(q1[:, ts], q1[:, ts], 1e-8, None, ALU.add))
                c.run(nc.vector.reciprocal(q1[:, ts], q1[:, ts]))
                c.run(nc.vector.tensor_tensor(t1[:, ts], q1[:, ts], q1[:, ts], ALU.mult))
                v.wait_ge(s_done, 2 * part + 1)
                nc.vector.tensor_tensor(v128[:, ts], v128[:, ts], t1[:, ts], ALU.mult).then_inc(s_done, 1)
                v.wait_ge(rms_done, 2 * part + 2)
                c.run(nc.vector.reciprocal(q2[:, ts], q2[:, ts]))
                c.run(nc.vector.tensor_tensor(q1[:, ts], q1[:, ts], q2[:, ts], ALU.mult))
                nc.vector.scalar_tensor_tensor(nmr[:, ts], mean2[:, ts], -1.0, q1[:, ts], ALU.mult,
                                               ALU.mult).then_inc(scale_done, 1)

            def output_normed(b):
                for t in range(b * TB, (b + 1) * TB):
                    u = nc.vector.tensor_scalar(Z[:, t, :], O[:, t, :], mean2[:, t:t + 1], q1[:, t:t + 1],
                                                ALU.subtract, ALU.mult)
                return u

            stats(0)
            normed(0)
            for b in range(1, B):
                stats(b)
            for k in range(NCH):
                if k % 2 == 0 and k // 2 + 1 < B:
                    normed(k // 2 + 1)
                squares(k)
                if 2 <= k < NCH - 1:
                    outputs(k - 2)
                if k == NCH - 2:
                    outputs(NCH - 3)
                    scales(0, PARTS[0])
            output_normed(2).then_inc(u2_done, 1)
            outputs(NCH - 2)
            outputs(NCH - 1)
            scales(1, PARTS[1])
            c.run(output_normed(3))
            c.run(nc.vector.tensor_tensor(X[:, T - TB:, :], X[:, T - TB:, :], Z[:, T - TB:, :], ALU.add))

        @block.tensor
        def _(pe):
            mm = nc.tensor.matmul

            def transposes(k):
                pe.wait_ge(z_done, k // 2 + 1)
                if k >= 2:
                    pe.wait_ge(zt_done, k - 1)
                for j in range(4):
                    tr = nc.tensor.transpose(pT[k % 2][:, j * P:(j + 1) * P], Z[:, 4 * k + j, :], ident[:])
                tr.then_inc(zt_mm, 1)

            def up(k):
                pe.wait_ge(zt_done, k + 1)
                for f in range(FC):
                    n = FC * k + f
                    if n >= 2:
                        pe.wait_ge(h_done, n - 1)
                    mm(pU[f % 2][:], R["up_t"][:, f * P:(f + 1) * P], ZT[:, k * CH:(k + 1) * CH],
                       start=True, stop=True).then_inc(up_mm, 1)

            def down(k):
                pe.wait_ge(h_done, FC * (k + 1))
                if k >= 2:
                    pe.wait_ge(o_read, k - 1)
                for j in range(4):
                    for f in range(FC):
                        last = mm(pD[k % 2][:, j * P:(j + 1) * P], H[:, k % 2, f, j * P:(j + 1) * P],
                                  R["down_t"][:, f * P:(f + 1) * P], start=f == 0, stop=f == FC - 1)
                last.then_inc(down_mm, 1)

            def sums(k):
                pe.wait_ge(sqs_done, k + 1)
                if k >= 2:
                    pe.wait_ge(q_read, k - 1)
                for j in range(4):
                    last = mm(pQ[k % 2][:, j:j + 1], SQ[:, k % 3, 0, j * P:(j + 1) * P], ones[:, 0:1],
                              start=True, stop=True)
                last.then_inc(sum_mm, 1)

            transposes(0)
            for k in range(NCH):
                if k + 1 < NCH:
                    transposes(k + 1)
                up(k)
                if k >= 1:
                    down(k - 1)
                if 2 <= k < NCH - 1:
                    sums(k - 2)
                if k == NCH - 2:
                    sums(NCH - 3)
            down(NCH - 1)
            sums(NCH - 2)
            sums(NCH - 1)
        R["used"] = used


SCALE = float(HD) ** -0.5
MAX_SHIFT = 20.0
SPLIT_Q = (0, 0, 0, 1, 1, 2)
SPLIT_K = (0, 1, 2, 0, 1, 0)
RUNS = ((0, 3), (3, 2), (5, 1))
ROW_SHIFT = 8 * len(SPLIT_Q)
UNITS = B * NQ


def second_projections(nc, R, A, S):
    with ExitStack() as ctx:
        sb = lambda n, s, d=F32: ctx.enter_context(nc.sbuf_tensor(n, s, d))
        pb = lambda n: ctx.enter_context(nc.psum_tensor(n, [P, 512], F32))
        used = []
        sem = lambda n: used.append(ctx.enter_context(nc.semaphore(n))) or used[-1]
        X, ident = R["X"], R["ident"]
        Z = sb("b_z", [P, T, D])
        ZT = sb("b_zt", [P, B * L])
        wab = sb("b_wab", [P, 4, P])
        wv = sb("b_wv", [P, P])
        bab = sb("b_bab", [P, 4])
        bv = sb("b_bv", [P, P])
        cs = sb("b_cs", [P, 2, L])
        blk = sb("b_blk", [P, HEADS], BF16)
        ta, tb_, q, r = (sb(f"b_{n}", [P, 2, CH]) for n in ("ta", "tb", "q", "r"))
        sq = sb("b_sq", [P, 2, CH], BF16)
        parts = sb("b_parts", [P, 4, 3, L], BF16)
        N2 = sb("b_n2", [HEADS, 2, B * L])
        m2 = sb("b_m2", [HEADS, L])
        sh = sb("b_sh", [HEADS, B, L], BF16)
        kmax, mmax = sb("b_kmax", [HEADS, B]), sb("b_mmax", [HEADS, B])
        ok = sb("b_ok", [HEADS, 2])
        pad = sb("b_pad", [32, 2 * L], BF16)
        st = sb("b_st", [P, T, 6])
        mean, v128, r1, t1, t2 = (sb(f"b_s{i}", [P, T]) for i in range(5))
        pT = [pb("b_pt0"), pb("b_pt1")]
        pA = [pb("b_pa0"), pb("b_pa1")]
        pB = [pb("b_pb0"), pb("b_pb1")]
        pN, pV = pb("b_pn"), pb("b_pv")
        (w_in, var_done, std_done, z_done, zt_mm, zt_done, ab_mm, ab_read, q_done, hi_done, r_done, mid_done,
         lo_done, sq_done, n_mm, n_read, v_mm, v_read, m2_done, sh_done, m_done, pad_done, pad_out, pad_in, sh_out,
         ok_done, ok_mm) = (sem("b_" + n) for n in (
             "w_in", "var_done", "std_done", "z_done", "zt_mm", "zt_done", "ab_mm", "ab_read", "q_done", "hi_done",
             "r_done", "mid_done", "lo_done", "sq_done", "n_mm", "n_read", "v_mm", "v_read", "m2_done", "sh_done",
             "m_done", "pad_done", "pad_out", "pad_in", "sh_out", "ok_done", "ok_mm"))
        part_out = [sem(f"b_part_out{i}") for i in range(4)]
        vs = sem("b_vec")
        slot = lambda i: 2 * (i // 4 % 2) + i % 2
        part = lambda i, n: parts[:, slot(i), n, (i // 2 % 2) * CH:(i // 2 % 2 + 1) * CH]
        block = ctx.enter_context(nc.Block())

        @block.sync
        def _(sp):
            for dst, src in ((wab, "w_ab"), (wv, "wv1_t"), (bab, "b_ab"), (cs, "cos_sin"), (blk, "head_sum")):
                sp.dma_start(dst[:], A[src]).then_inc(w_in, 16)
            sp.dma_start(bv[:], A["bv1"].partition_broadcast(P)).then_inc(w_in, 16)
            sp.wait_ge(pad_in, 16)
            for b in range(B):
                for a in range(2):
                    r0 = 64 * a + ROW_SHIFT
                    for w in range(2):
                        sp.dma_start(S["qk"[w]][b, r0:r0 + 16].rearrange("r n h t -> r n (h t)"),
                                     pad[16 * w:16 * w + 16, :].unsqueeze(1).broadcast_to([16, NQ, 2 * L])
                                     ).then_inc(pad_out, 16)

            def stack(i, t0, nt):
                b, w = i // 4, i % 2
                sp.wait_ge(lo_done, i + 1)
                sp.wait_ge(mid_done, i + 1)
                for run, (g, count) in enumerate(RUNS):
                    for half in range(2):
                        rows = slice(64 * half, 64 * half + 64)
                        dst = S["qk"[w]][b, 64 * half + 8 * g:64 * half + 8 * (g + count), :, :, t0:t0 + nt]
                        if w == 0:
                            src = parts[rows, slot(i), run:run + 1, t0:t0 + nt].broadcast_to([64, count, nt])
                        else:
                            src = parts[rows, slot(i), 0:count, t0:t0 + nt]
                        sp.dma_start(dst.rearrange("(g r) n h t -> (r n h) g t", g=count), src
                                     ).then_inc(part_out[slot(i)], 16)

            def shift_row(b):
                if b == 0:
                    sp.wait_ge(pad_out, 64 * B)
                sp.wait_ge(sh_done, b + 1)
                for a in range(2):
                    sp.dma_start(S["q"][b, 64 * a + ROW_SHIFT, :, :, :].rearrange("n h t -> (n h) t"),
                                 sh[8 * a:8 * a + 8, b, :]).then_inc(sh_out, 16)

            for b in range(B - 1):
                stack(4 * b + 2, 0, L)
                stack(4 * b + 3, 0, L)
                if b >= 1:
                    shift_row(b - 1)
            stack(4 * B - 3, 0, CH)
            stack(4 * B - 2, 0, L)
            shift_row(B - 2)
            stack(4 * B - 1, CH, CH)
            shift_row(B - 1)
            sp.wait_ge(sh_out, B * 2 * 16)
            for i in range(4):
                sp.wait_ge(part_out[i], (B // 2 + i // 3) * 6 * 16)

        @block.scalar
        def _(act):
            def std(b):
                tb = slice(b * TB, (b + 1) * TB)
                act.wait_ge(var_done, b + 1)
                nc.scalar.activation(r1[:, tb], v128[:, tb], ACT.Sqrt, bias=R["c_eps"],
                                     scale=1.0 / D).then_inc(std_done, 1)

            def zt(k):
                act.wait_ge(zt_mm, k + 1)
                nc.scalar.copy(ZT[:, k * CH:(k + 1) * CH], pT[k % 2][:]).then_inc(zt_done, 1)

            def shift(b):
                act.wait_ge(m2_done, b + 1)
                nc.scalar.activation(m2[:], m2[:], ACT.Sqrt).then_inc(m_done, 1)

            def norms(i):
                k, w = i // 2, i % 2
                act.wait_ge(n_mm, i + 1)
                nc.scalar.copy(N2[:, w, k * CH:(k + 1) * CH], pN[32 * w:32 * w + HEADS, :]).then_inc(n_read, 1)

            def mid(i):
                act.wait_ge(r_done, i + 1)
                nc.scalar.copy(part(i, 1), r[:, i % 2, :]).then_inc(mid_done, 1)

            std(0)
            zt(0)
            for k in range(NCH):
                if k % 2 == 0 and k // 2 + 1 < B:
                    std(k // 2 + 1)
                if k + 1 < NCH:
                    zt(k + 1)
                for w in range(2):
                    i = 2 * k + w
                    act.wait_ge(q_done, i + 1)
                    if i >= 8 and i % 4 < 2:
                        act.wait_ge(part_out[slot(i)], (i // 8) * 6 * 16)
                    nc.scalar.copy(part(i, 0), q[:, i % 2, :]).then_inc(hi_done, 1)
                    if i >= 1:
                        mid(i - 1)
                    if i >= 2:
                        act.wait_ge(n_mm, i - 1)
                    nc.scalar.square(sq[:, i % 2, :], q[:, i % 2, :]).then_inc(sq_done, 1)
                    if i >= 2:
                        norms(i - 2)
                    if i % 4 == 2 and i >= 6:
                        shift(i // 4 - 1)
            mid(2 * NCH - 1)
            norms(2 * NCH - 2)
            norms(2 * NCH - 1)
            shift(B - 1)

        @block.gpsimd
        def _(pool):
            clear_semaphores(pool, R)
            nc.gpsimd.memset(pad[:], 0.0).then_inc(pad_done, 1)
            pool.wait_ge(pad_done, 1)
            pool.dma_start(pad[16:19, :], A["ones_row"]).then_inc(pad_in, 16)
            def last_part(i):
                pool.wait_ge(mid_done, i + 1)
                nc.gpsimd.tensor_tensor(part(i, 2), r[:, i % 2, :], part(i, 1),
                                        ALU.subtract).then_inc(lo_done, 1)

            for i in range(2 * NCH):
                pool.wait_ge(ab_read, 2 * i + 2)
                if i >= 2:
                    pool.wait_ge(sq_done, i - 1)
                    pool.wait_ge(r_done, i - 1)
                nc.gpsimd.tensor_tensor(q[:, i % 2, :], ta[:, i % 2, :], tb_[:, i % 2, :], ALU.add).then_inc(q_done, 1)
                if i >= 2:
                    last_part(i - 2)
            last_part(2 * NCH - 2)
            last_part(2 * NCH - 1)

        @block.vector
        def _(v):
            c = Chain(v, vs)

            def stats(b):
                tb = slice(b * TB, (b + 1) * TB)
                stats_of(nc, c, X[:, tb, :], st[:, tb, :], TB)
                finish_stats(nc, c, st[:, tb, :], mean[:, tb], v128[:, tb], t1[:, tb],
                             t2[:, tb]).then_inc(var_done, 1)

            def normed(b):
                tb = slice(b * TB, (b + 1) * TB)
                v.wait_ge(std_done, b + 1)
                c.run(nc.vector.reciprocal(r1[:, tb], r1[:, tb]))
                for t in range(b * TB, (b + 1) * TB):
                    z = nc.vector.tensor_scalar(Z[:, t, :], X[:, t, :], mean[:, t:t + 1], r1[:, t:t + 1],
                                                ALU.subtract, ALU.mult)
                    if t % TB == TB - 1:
                        z.then_inc(z_done, 1)

            def rotate(i):
                k, w = i // 2, i % 2
                t0 = (k % 2) * CH
                if i >= 2:
                    v.wait_ge(q_done, i - 1)
                v.wait_ge(ab_mm, i + 1)
                nc.vector.scalar_tensor_tensor(ta[:, i % 2, :], pA[i % 2][:], bab[:, 2 * w:2 * w + 1],
                                               cs[:, 0, t0:t0 + CH], ALU.add, ALU.mult).then_inc(ab_read, 1)
                nc.vector.scalar_tensor_tensor(tb_[:, i % 2, :], pB[i % 2][:], bab[:, 2 * w + 1:2 * w + 2],
                                               cs[:, 1, t0:t0 + CH], ALU.add, ALU.mult).then_inc(ab_read, 1)

            def value(k):
                v.wait_ge(v_mm, k + 1)
                nc.vector.tensor_tensor(
                    R["V"][:, (k // 2) * NQ:(k // 2 + 1) * NQ, 4 * (k % 2):4 * (k % 2) + 4, :],
                    pV[:].rearrange("p (t n e) -> p n t e", t=4, n=NQ),
                    bv[:].rearrange("p (n e) -> p n e", n=NQ).unsqueeze(2).broadcast_to([P, NQ, 4, 32]),
                    ALU.add).then_inc(v_read, 1)

            def remainder(i):
                v.wait_ge(hi_done, i + 1)
                if i >= 2:
                    v.wait_ge(mid_done, i - 1)
                    v.wait_ge(lo_done, i - 1)
                nc.vector.tensor_tensor(r[:, i % 2, :], q[:, i % 2, :], part(i, 0),
                                        ALU.subtract).then_inc(r_done, 1)

            def bounds(b):
                tb = slice(b * L, (b + 1) * L)
                v.wait_ge(n_read, 4 * b + 4)
                c.run(nc.vector.tensor_reduce(kmax[:, b:b + 1], N2[:, 1, tb], AX.X, ALU.max))
                if b >= 1:
                    v.wait_ge(sh_done, b)
                nc.vector.tensor_scalar(m2[:], N2[:, 0, tb], kmax[:, b:b + 1], None, ALU.mult).then_inc(m2_done, 1)

            def shifts(b):
                v.wait_ge(m_done, b + 1)
                c.mark(nc.vector.tensor_reduce(mmax[:, b:b + 1], m2[:], AX.X, ALU.max))
                nc.vector.tensor_scalar(sh[:, b, :], m2[:], -1.0, None, ALU.mult).then_inc(sh_done, 1)

            stats(0)
            normed(0)
            v.wait_ge(w_in, 6 * 16)
            rotate(0)
            value(0)
            for i in range(2 * NCH):
                b = i // 4 + 1
                if i % 4 == 0 and b < B:
                    stats(b)
                if i + 1 < 2 * NCH:
                    rotate(i + 1)
                    if i % 2 == 1:
                        value((i + 1) // 2)
                remainder(i)
                if i % 4 == 1 and b < B:
                    normed(b)
                if i % 4 == 2 and i >= 6:
                    bounds(i // 4 - 1)
                if i % 4 == 3 and i >= 7:
                    shifts(i // 4 - 1)
            bounds(B - 1)
            shifts(B - 1)
            c.wait()
            c.run(nc.vector.tensor_reduce(ok[:, 0:1], mmax[:], AX.X, ALU.max))
            nc.vector.tensor_scalar(ok[:, 1:2], ok[:, 0:1], MAX_SHIFT / SCALE, None, ALU.is_le).then_inc(ok_done, 1)
            v.wait_ge(ok_mm, 1)
            c.run(nc.vector.tensor_scalar(R["flag"], pN[0:1, 0:1], HEADS - 0.5, None, ALU.is_lt))

        @block.tensor
        def _(pe):
            mm = nc.tensor.matmul

            def transposes(k):
                pe.wait_ge(z_done, k // 2 + 1)
                if k >= 2:
                    pe.wait_ge(zt_done, k - 1)
                for j in range(4):
                    tr = nc.tensor.transpose(pT[k % 2][:, j * P:(j + 1) * P], Z[:, 4 * k + j, :], ident[:])
                tr.then_inc(zt_mm, 1)

            def norms(i):
                q0 = 32 * (i % 2)
                if i >= 2:
                    pe.wait_ge(n_read, i - 1)
                pe.wait_ge(sq_done, i + 1)
                mm(pN[q0:q0 + HEADS, :], blk[:], sq[:, i % 2, :], start=True, stop=True).then_inc(n_mm, 1)

            transposes(0)
            pe.wait_ge(w_in, 6 * 16)
            for k in range(NCH):
                pe.wait_ge(zt_done, k + 1)
                for w in range(2):
                    i = 2 * k + w
                    if i >= 2:
                        pe.wait_ge(ab_read, 2 * i - 2)
                    zt = ZT[:, k * CH:(k + 1) * CH]
                    mm(pA[i % 2][:], wab[:, 2 * w, :], zt, start=True, stop=True)
                    mm(pB[i % 2][:], wab[:, 2 * w + 1, :], zt, start=True, stop=True).then_inc(ab_mm, 1)
                    if w == 0:
                        if k >= 1:
                            pe.wait_ge(v_read, k)
                        for j in range(4):
                            last = mm(pV[:, j * P:(j + 1) * P], ZT[:, (4 * k + j) * P:(4 * k + j + 1) * P], wv[:],
                                      start=True, stop=True)
                        last.then_inc(v_mm, 1)
                    if w == 1 and k + 1 < NCH:
                        transposes(k + 1)
                    if i >= 2:
                        norms(i - 2)
            norms(2 * NCH - 2)
            norms(2 * NCH - 1)
            pe.wait_ge(n_read, 2 * NCH)
            pe.wait_ge(ok_done, 1)
            mm(pN[0:1, 0:1], ok[:, 1:2], R["ones"][0:HEADS, 0:1], start=True, stop=True).then_inc(ok_mm, 1)
        R["used"] = used


def exact_maxima(nc, R, S):
    with ExitStack() as ctx:
        sb = lambda n, s, d=F32: ctx.enter_context(nc.sbuf_tensor(n, s, d))
        sem = lambda n: ctx.enter_context(nc.semaphore(n))
        Q, K = sb("m_q", [P, 2, L], BF16), sb("m_k", [P, 2, L], BF16)
        mt = sb("m_mt", [P, TB, 4])
        neg, rest = sb("m_neg", [4, L]), sb("m_rest", [4, L])
        parts = sb("m_parts", [4, 3, L], BF16)
        pS = [ctx.enter_context(nc.psum_tensor(f"m_ps{i}", [P, 1024], F32)) for i in range(2)]
        pT = ctx.enter_context(nc.psum_tensor("m_pt", [P, 1024], F32))
        qk_in, s_mm, max_done, t_mm, parts_done, shift_out, vs = (sem("m_" + n) for n in (
            "qk_in", "s_mm", "max_done", "t_mm", "parts_done", "shift_out", "vec"))
        block = ctx.enter_context(nc.Block())
        NS = TB * 4

        @block.gpsimd
        def _(pool):
            clear_semaphores(pool, R)

        @block.sync
        def _(sp):
            slow = sp.value_load(R["flag"], min_val=0, max_val=1)
            with sp.If(slow > 0):
                for u in range(UNITS):
                    b, n = u // NQ, u % NQ
                    sp.dma_start(Q[:], S["q"][b, :, n, :, :]).then_inc(qk_in, 16)
                    sp.dma_start(K[:], S["k"][b, :, n, :, :]).then_inc(qk_in, 16)
                    sp.wait_ge(parts_done, u + 1)
                    for h in range(4):
                        r0 = 64 * (h % 2) + ROW_SHIFT
                        sp.dma_start(S["q"][b, r0:r0 + 3, n, h // 2, :], parts[h:h + 1, :, :]).then_inc(shift_out, 16)
                    sp.wait_ge(shift_out, 64 * (u + 1))

        @block.vector
        def _(v):
            slow = v.value_load(R["flag"], min_val=0, max_val=1)
            with v.If(slow > 0):
                with v.Fori(0, UNITS) as n:
                    for i in range(NS):
                        v.wait_ge(s_mm, n * NS + (i + 1))
                        nc.vector.tensor_reduce(mt[:, i // 4, i % 4:i % 4 + 1], pS[i % 2][:], AX.X,
                                                ALU.max, negate=True).then_inc(max_done, 1)
                    v.wait_ge(t_mm, n + 1)
                    nc.vector.tensor_copy(neg[:], pT[0:4, :]).then_inc(vs, 1)
                    v.wait_ge(vs, n * 5 + 1)
                    nc.vector.tensor_copy(parts[:, 0, :], neg[:]).then_inc(vs, 1)
                    v.wait_ge(vs, n * 5 + 2)
                    nc.vector.tensor_tensor(rest[:], neg[:], parts[:, 0, :], ALU.subtract).then_inc(vs, 1)
                    v.wait_ge(vs, n * 5 + 3)
                    nc.vector.tensor_copy(parts[:, 1, :], rest[:]).then_inc(vs, 1)
                    v.wait_ge(vs, n * 5 + 4)
                    nc.vector.tensor_tensor(rest[:], rest[:], parts[:, 1, :], ALU.subtract).then_inc(vs, 1)
                    v.wait_ge(vs, n * 5 + 5)
                    nc.vector.tensor_copy(parts[:, 2, :], rest[:]).then_inc(parts_done, 1)
                    v.wait_ge(parts_done, n + 1)

        @block.tensor
        def _(pe):
            slow = pe.value_load(R["flag"], min_val=0, max_val=1)
            with pe.If(slow > 0):
                with pe.Fori(0, UNITS) as n:
                    pe.wait_ge(qk_in, n * 32 + 32)
                    for i in range(NS):
                        st, h = i // 4, i % 4
                        pair, a = h // 2, h % 2
                        rows = slice(64 * a, 64 * a + ROW_SHIFT)
                        if i >= 2:
                            pe.wait_ge(max_done, n * NS + (i - 1))
                        for half in range(2):
                            last = nc.tensor.matmul(pS[i % 2][:, half * CH:(half + 1) * CH],
                                                    Q[rows, pair, st * P:(st + 1) * P],
                                                    K[rows, pair, half * CH:(half + 1) * CH], start=True, stop=True)
                        last.then_inc(s_mm, 1)
                    pe.wait_ge(max_done, n * NS + NS)
                    for st in range(TB):
                        last = nc.tensor.transpose(pT[0:4, st * P:(st + 1) * P], mt[:, st, :], R["ident"][:])
                    last.then_inc(t_mm, 1)


LATE = ((6, 0, -1), (9, 1, 0), (16, 0, 1), (17, 1, 0), (46, 1, 4), (48, 0, 5), (56, 1, 6))
NX = len(LATE)
LATE_BEFORE = {0: 1, 1: 4, 5: 5, 6: 6}


def second_scores(nc, R, A, S):
    with ExitStack() as ctx:
        sb = lambda n, s, d=F32: ctx.enter_context(nc.sbuf_tensor(n, s, d))
        sem = lambda n: ctx.enter_context(nc.semaphore(n))
        Q = [sb(f"s_q{i}", [P, 2, L], BF16) for i in range(2)]
        K = [sb(f"s_k{i}", [P, 2, L], BF16) for i in range(2)]
        V4 = [sb(f"s_v{i}", [P, TB, 4, 32]) for i in range(2)]
        E = [sb(f"s_e{i}", [P, 4, CH]) for i in range(4)]
        AS = [sb(f"s_as{i}", [P, CH]) for i in range(2)]
        rec = sb("s_rec", [P, 4, 4])
        O = sb("s_o", [P, TB, D])
        OT = YT = sb("s_ot", [P, 2, CH])
        SO = YB = sb("s_so", [P, TB, D])
        wo, bo, wg = sb("s_wo", [P, P]), sb("s_bo", [P, P]), sb("s_wg", [P, NE])
        LG = sb("s_lg", [P, TB, NE])
        st = sb("s_st", [P, TB, 6])
        mean, v128, r1, t1, t2 = (sb(f"s_s{i}", [P, TB]) for i in range(5))
        zero = sb("s_zero", [P, ROWS])
        pS = [ctx.enter_context(nc.psum_tensor(f"s_ps{i}", [P, 1024], F32)) for i in range(2)]
        acc = [ctx.enter_context(nc.psum_tensor(f"s_acc{i}", [P, CH], F32)) for i in range(2)]
        pX = [ctx.enter_context(nc.psum_tensor(f"s_px{i}", [P, CH], F32)) for i in range(2)]
        qk_in = [sem(f"qk_in{i}") for i in range(2)]
        scores, exp_done, av_done, v_staged, acc_read, tr_mm, o_done, rec_done = (sem("s_" + n) for n in (
            "scores", "exp_done", "av_done", "v_staged", "acc_read", "tr_mm", "o_done", "rec_done"))
        v_zero, w_in, late_mm, late_read, yb_done, yn_done = (sem("s_" + n) for n in (
            "v_zero", "w_in", "late_mm", "late_read", "yb_done", "yn_done"))
        var_done, std_done, vs = sem("s_var_done"), sem("s_std_done"), sem("s_vec")
        X, top, ix = R["X"], sb("s_top", [P, TB, 8]), sb("s_ix", [P, TB, 8], mybir.dt.uint32)
        block = ctx.enter_context(nc.Block())
        STEPS = 2 * TB
        G = NQ * STEPS
        HU = 2 * NQ

        def over_batches(engine, batch):
            batch(0, True)
            with engine.Fori(1, B) as b:
                batch(b, False)

        @block.sync
        def _(sp):
            def load(b, c):
                for sb_, s in ((Q, "q"), (K, "k")):
                    sp.dma_start(sb_[c % 2][:], S[s][b, :, c, :, :]).then_inc(qk_in[c % 2], 16)

            for n in range(UNITS):
                if n >= 2:
                    sp.wait_ge(scores, 2 * STEPS * (n - 1))
                load(n // NQ, n % NQ)
                if n == 1:
                    sp.dma_start(wo[:], A["wo_t"]).then_inc(w_in, 16)
                    sp.dma_start(bo[:], A["bo"].partition_broadcast(P)).then_inc(w_in, 16)
                    sp.dma_start(wg[:], A["w_gate"]).then_inc(w_in, 16)
                    sp.dma_start(R["W1"][:], A["w1"].rearrange("e d f -> d e f")).then_inc(R["w_in"], 16)
                    sp.dma_start(R["W2"][:].rearrange("p e c d -> p (e c) d"),
                                 A["w2"].rearrange("e (c p) d -> p (e c) d", p=P)).then_inc(R["w_in"], 16)
                    sp.wait_ge(v_zero, 5)
                    for h in range(GR):
                        for e in range(0, NE, 6):
                            sp.dma_start(R["x_rows"][h][e:e + 6].rearrange("e r d -> (e r d)").rearrange(
                                "(p k q) -> p k q", p=P, q=ROWS), zero[:].unsqueeze(1).broadcast_to([P, 6, ROWS])
                                ).then_inc(R["zero_out"], 16)

        @block.scalar
        def _(act):
            def batch(b, first):
                for g in range(G):
                    for pair in range(2):
                        act.wait_ge(scores, b * (2 * G) + (2 * g + pair + 1))
                        if pair == 0 and (g >= 4 or not first):
                            act.wait_ge(av_done, b * G + (g - 3))
                        nc.scalar.activation(E[g % 4][:, 2 * pair:2 * pair + 2, :],
                                             pS[pair][:].rearrange("p (a s) -> p a s", a=2),
                                             ACT.Exp, scale=SCALE).then_inc(exp_done, 1)

            over_batches(act, batch)
            for n in range(2):
                act.wait_ge(var_done, n + 1)
                nc.scalar.activation(r1[:], v128[:], ACT.Sqrt, bias=R["c_eps"], scale=1.0 / D).then_inc(std_done, 1)

        @block.gpsimd
        def _(pool):
            for i in range(2):
                nc.gpsimd.memset(V4[i][:], 0.0).then_inc(v_zero, 1)
            nc.gpsimd.memset(zero[:], 0.0).then_inc(v_zero, 1)
            pool.wait_ge(v_zero, 3)
            for i in range(2):
                nc.gpsimd.memset(V4[i][:, :, :, HD:HD + 1], 1.0).then_inc(v_zero, 1)
            for b in range(B):
                pool.wait_ge(yb_done, b + 1)
                pool.wait_ge(v_staged, NQ * (b + 1))
                nc.gpsimd.tensor_copy(R["Yn"][:, b * TB:(b + 1) * TB, :], YB[:]).then_inc(yn_done, 1)

        @block.vector
        def _(v):
            v.wait_ge(v_zero, 5)

            def stage(n, c):
                nc.vector.tensor_copy(V4[c % 2][:, :, :, 0:HD],
                                      R["V"][:, n, :, :].rearrange("p t (h e) -> p t h e", h=4)
                                      ).then_inc(v_staged, 1)

            c = Chain(v, vs)
            tiles = lambda ap, p: ap[:, p * TB:(p + 1) * TB, :]

            def late(p, i):
                v.wait_ge(late_mm, p * NX + (i + 1))
                bank = pX[LATE[i][1]][:]
                if i in (0, 1):
                    op = nc.vector.tensor_copy(OT[:, i, :], bank)
                if i in (2, 3):
                    op = nc.vector.tensor_tensor(SO[:, 4 * i - 8:4 * i - 4, :], bank.rearrange("p (t d) -> p t d", t=4),
                                                 bo[:].unsqueeze(1).broadcast_to([P, 4, D]), ALU.add)
                if i in (4, 5):
                    op = nc.vector.tensor_copy(YT[:, i - 4, :], bank)
                if i == 6:
                    op = nc.vector.tensor_copy(LG[:], bank[:, 0:TB * NE].rearrange("p (t e) -> p t e", t=TB))
                op.then_inc(late_read, 1)

            def statistics(p, src):
                chained = [nc.vector.bn_stats(st[:, t, :], src(t)) for t in range(TB)]
                for op in chained:
                    c.mark(op)
                c.wait()
                last = finish_stats(nc, c, st[:], mean[:], v128[:], t1[:], t2[:])
                if p < B - 1:
                    c.run(last)
                else:
                    last.then_inc(var_done, 1)

            def output_statistics(p):
                v.wait_ge(late_read, p * NX + 4)
                statistics(p, lambda t: SO[:, t, :])

            def inverse_deviation():
                rsqrt(nc, c, v128[:], r1[:], t1[:], 1.0 / D, EPS)

            def inverse_from_scalar(n):
                v.wait_ge(std_done, n)
                c.run(nc.vector.reciprocal(r1[:], r1[:]))

            def output_normed(p):
                for t in range(TB):
                    c.mark(nc.vector.tensor_scalar(SO[:, t, :], SO[:, t, :], mean[:, t:t + 1], r1[:, t:t + 1],
                                                   ALU.subtract, ALU.mult))
                c.wait()

            def residual(p):
                c.run(nc.vector.tensor_tensor(tiles(X[:], p), tiles(X[:], p), SO[:], ALU.add))
                statistics(p, lambda t: X[:, p * TB + t, :])

            def normed(p):
                for t in range(TB):
                    y = nc.vector.tensor_scalar(YB[:, t, :], X[:, p * TB + t, :],
                                                mean[:, t:t + 1], r1[:, t:t + 1], ALU.subtract, ALU.mult)
                    if t == TB - 1:
                        y.then_inc(yb_done, 1)

            def largest(p):
                v.wait_ge(late_read, p * NX + NX)
                v.wait_ge(yn_done, p + 1)
                for t in range(TB):
                    c.mark(nc.vector.max(top[:, t, :], LG[:, t, :]))
                c.wait()

            def choices(p):
                for t in range(TB):
                    c.mark(nc.vector.max_index(ix[:, t, :], top[:, t, :], LG[:, t, :]))
                c.mark(nc.vector.tensor_tensor(tiles(R["EX"], p)[:, :, 0:NE], LG[:],
                                               top[:, :, 0:1].broadcast_to([P, TB, NE]), ALU.subtract))
                c.mark(nc.vector.tensor_tensor(tiles(R["EX"], p)[:, :, NE:NE + 1], top[:, :, 1:2], top[:, :, 0:1],
                                               ALU.subtract))
                c.wait()
                c.run(nc.vector.tensor_copy(tiles(R["eidx"], p), ix[:, :, 0:2]))

            def batch(b, first, last):
                p = b - 1
                if not first:
                    late(p, 0)
                for hu in range(HU):
                    v.wait_ge(av_done, b * G + TB * (hu + 1))
                    nc.vector.tensor_copy(AS[hu % 2][:], acc[hu % 2][:]).then_inc(acc_read, 1)
                    if hu % 2 == 1 and not (last and hu // 2 + 2 >= NQ):
                        stage(b * NQ + (hu // 2 + 2), hu // 2)
                    if not first:
                        if hu == 0:
                            late(p, 1)
                        if hu == 1:
                            late(p, 2)
                            late(p, 3)
                            output_statistics(p)
                        if hu == 2:
                            output_normed(p)
                        if hu == 3:
                            inverse_deviation()
                        if hu == 5:
                            late(p, 5)
                        if hu == 6:
                            late(p, 6)
                        if hu == 7:
                            choices(p)
                    v.wait_ge(tr_mm, b * HU + (hu + 1))
                    o = pX[hu % 2][:].rearrange("p (t h e) -> p t h e", t=4, h=4)
                    nc.vector.reciprocal(rec[:], o[:, :, :, HD]).then_inc(rec_done, 1)
                    v.wait_ge(rec_done, b * HU + (hu + 1))
                    t0 = 4 * (hu % 2)
                    col = 32 * (hu // 2)
                    nc.vector.tensor_tensor(O[:, t0:t0 + 4, col:col + 32].rearrange("p t (h e) -> p t h e", h=4),
                                            o[:, :, :, 0:HD], rec[:].unsqueeze(3).broadcast_to([P, 4, 4, HD]),
                                            ALU.mult).then_inc(o_done, 1)
                    if not first:
                        if hu == 1:
                            inverse_deviation()
                        if hu == 2:
                            residual(p)
                        if hu == 3:
                            normed(p)
                        if hu == 4:
                            late(p, 4)
                        if hu == 6:
                            largest(p)

            stage(0, 0)
            stage(1, 1)
            v.wait_ge(w_in, 48)
            for b in range(B):
                batch(b, b == 0, b == B - 1)
            p = B - 1
            for i in range(4):
                late(p, i)
            output_statistics(p)
            inverse_from_scalar(1)
            output_normed(p)
            residual(p)
            inverse_from_scalar(2)
            normed(p)
            late(p, 4)
            late(p, 5)
            late(p, 6)
            largest(p)
            choices(p)

        @block.tensor
        def _(pe):
            def score(b, first, g, pair):
                c, half, j = g // STEPS, (g // TB) % 2, g % TB
                if g % STEPS == 0 and pair == 0:
                    pe.wait_ge(qk_in[c % 2], b * 64 + 32 * (c // 2 + 1))
                if g >= 1 or not first:
                    pe.wait_ge(exp_done, b * (2 * G) + (2 * g - 1 + pair))
                for a in range(2):
                    rows = slice(64 * a, 64 * a + 64)
                    last = nc.tensor.matmul(pS[pair][:, a * CH:(a + 1) * CH],
                                            K[c % 2][rows, pair, j * P:(j + 1) * P],
                                            Q[c % 2][rows, pair, half * CH:(half + 1) * CH], start=True, stop=True)
                last.then_inc(scores, 1)

            def av(b, first, g):
                c, hu, j = g // STEPS, g // TB, g % TB
                if g % STEPS == 0:
                    pe.wait_ge(v_staged, b * NQ + (c + 1))
                if j == 0 and (hu >= 2 or not first):
                    pe.wait_ge(acc_read, b * HU + (hu - 1))
                pe.wait_ge(exp_done, b * (2 * G) + (2 * g + 2))
                for h in range(4):
                    last = nc.tensor.matmul(acc[hu % 2][32 * h:32 * h + 32, :], V4[c % 2][:, j, h, :],
                                            E[g % 4][:, h, :], start=j == 0, stop=j == TB - 1)
                last.then_inc(av_done, 1)

            def transposes(b, first, hu):
                pe.wait_ge(acc_read, b * HU + (hu + 1))
                if hu >= 2 or not first:
                    pe.wait_ge(o_done, b * HU + (hu - 1))
                if hu in LATE_BEFORE and not first:
                    pe.wait_ge(late_read, b * NX + (LATE_BEFORE[hu] - NX))
                for t in range(4):
                    last = nc.tensor.transpose(pX[hu % 2][:, t * P:(t + 1) * P],
                                               AS[hu % 2][:, t * P:(t + 1) * P], R["ident"][:])
                last.then_inc(tr_mm, 1)

            def late(p, i):
                bank = pX[LATE[i][1]]
                before = (0, 0, 1, 2, 4, 4, 6)[i]
                if before:
                    pe.wait_ge(late_read, p * NX + before)
                if i in (4, 5):
                    pe.wait_ge(yb_done, p + 1)
                if i < 6:
                    for j in range(4):
                        out, t = bank[:, j * P:(j + 1) * P], 4 * (i % 2) + j
                        if i in (2, 3):
                            last = nc.tensor.matmul(out, OT[:, i % 2, j * P:(j + 1) * P], wo[:], start=True, stop=True)
                        else:
                            last = nc.tensor.transpose(out, (O if i < 2 else YB)[:, t, :], R["ident"][:])
                else:
                    for t in range(TB):
                        last = nc.tensor.matmul(bank[:, t * NE:(t + 1) * NE], YT[:, t // 4, t % 4 * P:(t % 4 + 1) * P],
                                                wg[:], start=True, stop=True)
                last.then_inc(late_mm, 1)

            def batch(b, first):
                for g in range(G):
                    score(b, first, g, 0)
                    if g >= 2 or not first:
                        av(b, first, g - 2)
                    score(b, first, g, 1)
                    if g % TB == 4 and (g > TB or not first):
                        transposes(b, first, g // TB - 1)
                    for i, (step, bank, halves) in enumerate(LATE):
                        if g == step and not first:
                            pe.wait_ge(o_done, b * HU + halves)
                            late(b - 1, i)
                if not first:
                    pe.wait_ge(late_read, b * NX)

            pe.wait_ge(w_in, 48)
            over_batches(pe, batch)
            av(B - 1, False, G - 2)
            av(B - 1, False, G - 1)
            transposes(B - 1, False, HU - 1)
            pe.wait_ge(o_done, B * HU)
            for i in range(NX):
                late(B - 1, i)




NHS = 3
GR = 4
GT = T // GR
NE = 24
CAP = -(-2 * GT * P // NE)
ROWS = 96
EB = 4
NB = NE // EB
BIG = 100000.0


def tile_of(h, i):
    return (i // 2) * TB + 2 * h + i % 2


def scatter_tokens(nc, R, rows, h, done):
    for i in range(GT):
        t = tile_of(h, i)
        for k in range(2):
            nc.gpsimd.indirect_dma_start(rows.rearrange("e r d -> (e r) d"),
                                         bass.IndirectOffsetOnAxis(ap=R["send"][:, t, k:k + 1], axis=0),
                                         R["Yn"][:, t, :], None, bounds_check=NE * ROWS - 1, oob_is_err=False
                                         ).then_inc(done, 16)


def routing(nc, R, A):
    with ExitStack() as ctx:
        sb = lambda n, s, d=F32: ctx.enter_context(nc.sbuf_tensor(n, s, d))
        pb = lambda n: ctx.enter_context(nc.psum_tensor(n, [P, 512], F32))
        sem = lambda n: ctx.enter_context(nc.semaphore(n))
        EX, eidx = R["EX"], R["eidx"]
        iota_i, iota = sb("r_iota_i", [P, NE], I32), sb("r_iota", [P, NE])
        M = sb("r_m", [P, T, 2, NE], BF16)
        PF = sb("r_pf", [P, GR, GT + 1, 2 * NE], BF16)
        before, onesb = sb("r_before", [P, P], BF16), sb("r_onesb", [P, P], BF16)
        LP = sb("r_lp", [P, T, 2, NE])
        p2, valid = sb("r_p2", [P, T, 2]), sb("r_valid", [P, T, 2])
        sl, s2 = sb("r_slot", [P, T, 2]), sb("r_away", [P, T, 2])
        zs, g, gs = sb("r_zs", [P, T]), sb("r_g", [P, T, 2]), sb("r_gs", [P, T])
        pP = [pb("r_pp0"), pb("r_pp1")]
        consts, pf_done, pos_mm, pos_read, ex_done, send_done = (sem("r_" + n) for n in (
            "consts", "pf_done", "pos_mm", "pos_read", "ex_done", "send_done"))
        vs, ps = sem("r_vec"), sem("r_pool")
        block = ctx.enter_context(nc.Block())

        @block.gpsimd
        def _(pool):
            nc.gpsimd.iota(iota_i[:], pattern=[[1, NE]], base=0, channel_multiplier=0).then_inc(ps, 1)
            nc.gpsimd.memset(onesb[:], 1.0).then_inc(ps, 1)
            pool.wait_ge(ps, 2)
            nc.gpsimd.tensor_copy(iota[:], iota_i[:]).then_inc(consts, 1)
            nc.gpsimd.affine_select(out=before[:], in_=onesb[:], compare_op=ALU.is_gt, fill=0.0,
                                    base=0, pattern=[[1, P]], channel_multiplier=-1).then_inc(consts, 1)
            pool.wait_ge(R["zero_out"], 16 * GR * 4)
            pool.wait_ge(send_done, 1)
            scatter_tokens(nc, R, R["x_rows"][0], 0, R["sent"][0])

        @block.scalar
        def _(act):
            nc.scalar.activation(EX, EX, ACT.Exp).then_inc(ex_done, 1)

        @block.vector
        def _(v):
            c = Chain(v, vs)

            v.wait_ge(consts, 2)
            for k in range(2):
                c.mark(nc.vector.tensor_tensor(M[:, :, k, :], iota[:].unsqueeze(1).broadcast_to([P, T, NE]),
                                               eidx[:, :, k:k + 1].broadcast_to([P, T, NE]), ALU.is_equal))
            c.wait()
            Mt = M[:].rearrange("p (b h r) k e -> p b h r (k e)", b=B, h=GR)
            c.run(nc.vector.memset(PF[:, :, 0, :], 0.0))
            for i in range(GT):
                add = nc.vector.tensor_tensor(PF[:, :, i + 1, :], PF[:, :, i, :], Mt[:, i // 2, :, i % 2, :], ALU.add)
                if i < GT - 1:
                    c.run(add)
                else:
                    add.then_inc(pf_done, 1)
            for h in range(GR):
                v.wait_ge(pos_mm, h + 1)
                src = pP[h % 2][:, 0:GT * 2 * NE].rearrange("p (b r k e) -> p b r (k e)", b=B, r=2, k=2)
                dst = LP[:].rearrange("p (b h r) k e -> p b h r (k e)", b=B, h=GR)[:, :, h, :, :]
                nc.vector.tensor_tensor(dst, src, Mt[:, :, h, :, :], ALU.mult).then_inc(pos_read, 1)
            v.wait_ge(pos_read, GR)
            c.run(nc.vector.tensor_reduce(p2[:], LP[:], AX.X, ALU.add))
            c.mark(nc.vector.tensor_scalar(valid[:], p2[:], CAP - 0.5, None, ALU.is_lt))
            c.run(nc.vector.tensor_scalar(p2[:], p2[:], float(CAP), None, ALU.min))
            c.run(nc.vector.scalar_tensor_tensor(sl[:], eidx, float(ROWS), p2[:], ALU.mult, ALU.add))
            c.mark(nc.vector.tensor_copy(R["take"], sl[:]))
            c.run(nc.vector.tensor_scalar(s2[:], valid[:], -BIG, BIG, ALU.mult, ALU.add))
            nc.vector.tensor_tensor(R["send"], sl[:], s2[:], ALU.add).then_inc(send_done, 1)
            v.wait_ge(ex_done, 1)
            c.run(nc.vector.tensor_reduce(zs[:], EX[:, :, 0:NE], AX.X, ALU.add))
            c.run(nc.vector.reciprocal(zs[:], zs[:]))
            c.mark(nc.vector.tensor_copy(g[:, :, 0], zs[:]))
            c.run(nc.vector.tensor_tensor(g[:, :, 1], zs[:], EX[:, :, NE], ALU.mult))
            c.run(nc.vector.tensor_tensor(g[:], g[:], valid[:], ALU.mult))
            c.run(nc.vector.tensor_tensor(gs[:], g[:, :, 0], g[:, :, 1], ALU.add))
            c.run(nc.vector.tensor_scalar(gs[:], gs[:], 1e-9, None, ALU.max))
            c.run(nc.vector.reciprocal(gs[:], gs[:]))
            c.run(nc.vector.tensor_tensor(R["gate"], g[:], gs[:].unsqueeze(2).broadcast_to([P, T, 2]), ALU.mult))
            c.run(nc.vector.tensor_tensor(LP[:], M[:], R["gate"].unsqueeze(3).broadcast_to([P, T, 2, NE]), ALU.mult))
            c.run(nc.vector.tensor_tensor(R["GD"][:], LP[:, :, 0, :], LP[:, :, 1, :], ALU.add))

        @block.tensor
        def _(pe):
            mm = nc.tensor.matmul
            pe.wait_ge(pf_done, 1)
            for h in range(GR):
                if h >= 2:
                    pe.wait_ge(pos_read, h - 1)
                for i in range(GT):
                    o = pP[h % 2][:, i * 2 * NE:(i + 1) * 2 * NE]
                    mm(o, before[:], M[:, tile_of(h, i), :, :].rearrange("p k e -> p (k e)"), start=True, stop=False)
                    mm(o, onesb[:], PF[:, h, i, :], start=False, stop=False)
                    last = mm(o[:, NE:2 * NE], onesb[:], PF[:, h, GT, 0:NE], start=False, stop=True)
                last.then_inc(pos_mm, 1)


def expert_layers(nc, R, A, DR):
    with ExitStack() as ctx:
        sb = lambda n, s, d=F32: ctx.enter_context(nc.sbuf_tensor(n, s, d))
        pb = lambda n: ctx.enter_context(nc.psum_tensor(n, [P, 512], F32))
        sem = lambda n: ctx.enter_context(nc.semaphore(n))
        X, Yn, ident, W1, W2, GD = R["X"], R["Yn"], R["ident"], R["W1"], R["W2"], R["GD"]
        gate, take, send = R["gate"], R["take"], R["send"]
        XS = [sb(f"e_xs{i}", [ROWS, EB, D]) for i in range(3)]
        XT = [sb(f"e_xt{i}", [P, EB * ROWS]) for i in range(2)]
        HS = [sb(f"e_hs{i}", [ROWS, FF]) for i in range(NHS)]
        HL = [sb(f"e_hl{i}", [ROWS, 2, FF]) for i in range(3)]
        GA = [[sb(f"e_g{k}{i}", [P, FF]) for k in range(2)] for i in range(2)]
        TT = sb("e_t", [P, GT, FF])
        HT = [sb(f"e_ht{c}", [P, EB * ROWS]) for c in range(FC)]
        YS = [sb(f"e_ys{i}", [ROWS, EB, D]) for i in range(2)]
        YA = [[sb(f"e_ya{k}{i}", [P, D]) for k in range(2)] for i in range(2)]
        GTT = sb("e_gt", [NE, GT * P])
        b1, b2 = sb("e_b1", [NE, FF]), sb("e_b2", [NE, D])
        lnh, lno = sb("e_lnh", [P, 2, GR, FC]), sb("e_lno", [P, 2, D])
        st = sb("e_st", [P, GT, 6])
        mean, v128, r1, t1, t2 = (sb(f"e_s{i}", [P, GT]) for i in range(5))
        pX, pH, pN = pb("e_px"), [pb("e_ph0"), pb("e_ph1")], [pb("e_pn0"), pb("e_pn1")]
        pY, pG = pb("e_py"), [pb("e_pg0"), pb("e_pg1")]
        w_in = sem("e_w_in")
        (xt_mm, xt_done, h_mm, hs_done, t_bias, gt_mm, gt_done, b2_mm, b2_read, c_read, n_done, hn_mm, ht_done,
         y_mm, ys_done, y_read, o_done) = (sem("e_" + n) for n in (
             "xt_mm", "xt_done", "h_mm", "hs_done", "t_bias", "gt_mm", "gt_done", "b2_mm", "b2_read", "c_read",
             "n_done", "hn_mm", "ht_done", "y_mm", "ys_done", "y_read", "o_done"))
        sent = R["sent"]
        hs_out = [sem(f"e_hs_out{i}") for i in range(NHS)]
        n_sent = [sem(f"e_n_sent{h}") for h in range(GR)]
        ys_out = [sem(f"e_ys_out{i}") for i in range(2)]
        xs_in = [sem(f"e_xs_in{i}") for i in range(3)]
        ga_in = [sem(f"e_ga_in{i}") for i in range(2)]
        hl_in = [sem(f"e_hl_in{i}") for i in range(3)]
        ya_in = [sem(f"e_ya_in{i}") for i in range(2)]
        out_done = sem("e_out_done")
        var_done, std_done = sem("e_var_done"), sem("e_std_done")
        vs = sem("e_vec")
        block = ctx.enter_context(nc.Block())
        XD, HD_, YD = DR["x"], DR["h"], DR["y"]
        ORDER = [("u", 0), ("b", 0), ("u", 1), ("b", 1), ("w", 0), ("u", 2), ("b", 2), ("w", 1), ("u", 3), ("b", 3),
                 ("w", 2), ("w", 3)]
        ring = {}
        for s, h in ORDER:
            if s != "w":
                for j in range(NE if s == "u" else GT):
                    ring[s, h, j] = len(ring)

        def h_wait(pe, n):
            s, h, j = list(ring)[n]
            pe.wait_ge(hs_done if s == "u" else t_bias, h * (NE if s == "u" else GT) + j + 1)

        @block.sync
        def _(sp):
            def x_load(n):
                h, eb = n // NB, n % NB
                if eb == 0:
                    sp.wait_ge(sent[h], 2 * GT * 16)
                if n >= 3:
                    sp.wait_ge(xt_mm, n - 2)
                sp.dma_start(XS[n % 3][:], XD[h][eb * EB:(eb + 1) * EB, :, :].rearrange("e r d -> r e d")
                             ).then_inc(xs_in[n % 3], 16)

            def h_store(m):
                h, e = m // NE, m % NE
                sp.wait_ge(hs_done, m + 1)
                sp.dma_start(HD_[h][e, :, :], HS[m % NHS][:]).then_inc(hs_out[m % NHS], 16)

            def h_load(m):
                h, pr = m // (NE // 2), m % (NE // 2)
                if pr == 0:
                    sp.wait_ge(n_sent[h], 2 * GT * 16)
                if m >= 3:
                    sp.wait_ge(hn_mm, FC * ((m - 3) // 2 + 1))
                sp.dma_start(HL[m % 3][:], HD_[h][2 * pr:2 * pr + 2, :, :].rearrange("e r d -> r e d")
                             ).then_inc(hl_in[m % 3], 16)

            def y_store(n):
                h, eb = n // NB, n % NB
                sp.wait_ge(ys_done, n + 1)
                sp.dma_start(YD[h][eb * EB:(eb + 1) * EB, :, :].rearrange("e r d -> r e d"), YS[n % 2][:]
                             ).then_inc(ys_out[n % 2], 16)

            for s, h in ORDER:
                if s == "u":
                    x_load(h * NB)
                    x_load(h * NB + 1)
                    if h == 0:
                        sp.dma_start(b1[:], A["b1"]).then_inc(w_in, 16)
                        sp.dma_start(b2[:], A["b2"]).then_inc(w_in, 16)
                        sp.dma_start(lnh[:], A["ln_hid"]).then_inc(w_in, 16)
                        sp.dma_start(lno[:], A["ln_out"].partition_broadcast(P)).then_inc(w_in, 16)
                    for eb in range(NB):
                        if eb + 2 < NB:
                            x_load(h * NB + eb + 2)
                        for e in range(EB):
                            h_store(h * NE + eb * EB + e)
                if s == "w":
                    h_load(h * 2 * NB)
                    h_load(h * 2 * NB + 1)
                    h_load(h * 2 * NB + 2)
                    for eb in range(NB):
                        for j in range(3 + 2 * eb, min(5 + 2 * eb, 2 * NB)):
                            h_load(h * 2 * NB + j)
                        y_store(h * NB + eb)
            for h in range(GR):
                sp.wait_ge(o_done, h + 1)
                for b in range(B):
                    t = b * TB + 2 * h
                    sp.dma_start(DR["out"][t * P:(t + 2) * P, :].rearrange("(t p) d -> p t d", p=P),
                                 X[:, t:t + 2, :]).then_inc(out_done, 16)
            sp.wait_ge(out_done, 16 * GR * B)

        @block.gpsimd
        def _(pool):
            idx = lambda ap, t, k: bass.IndirectOffsetOnAxis(ap=ap[:, t, k:k + 1], axis=0)
            flat = lambda ap, h: ap[h].rearrange("e r d -> (e r) d")
            last_row = NE * ROWS - 1

            def scatter_x(h):
                scatter_tokens(nc, R, XD[h], h, sent[h])

            def gather_h(h):
                for i in range(NHS):
                    pool.wait_ge(hs_out[i], (h + 1) * NE // NHS * 16)
                for i in range(GT):
                    t, n = tile_of(h, i), h * GT + i
                    if n >= 2:
                        pool.wait_ge(c_read, n - 1)
                    for k in range(2):
                        nc.gpsimd.indirect_dma_start(GA[n % 2][k][:], None, flat(HD_, h), idx(take, t, k)
                                                     ).then_inc(ga_in[n % 2], 16)

            def scatter_n(h):
                for i in range(GT):
                    t = tile_of(h, i)
                    pool.wait_ge(n_done, h * GT + i + 1)
                    for k in range(2):
                        nc.gpsimd.indirect_dma_start(flat(HD_, h), idx(send, t, k), TT[:, i, :], None,
                                                     bounds_check=last_row, oob_is_err=False).then_inc(n_sent[h], 16)

            def gather_y(h):
                for i in range(2):
                    pool.wait_ge(ys_out[i], (h + 1) * NB // 2 * 16)
                for i in range(GT):
                    t, n = tile_of(h, i), h * GT + i
                    if n >= 2:
                        pool.wait_ge(y_read, n - 1)
                    for k in range(2):
                        nc.gpsimd.indirect_dma_start(YA[n % 2][k][:], None, flat(YD, h), idx(take, t, k)
                                                     ).then_inc(ya_in[n % 2], 16)

            for stage, h in ((scatter_x, 1), (gather_h, 0), (scatter_n, 0), (scatter_x, 2), (gather_h, 1),
                             (scatter_n, 1), (gather_y, 0), (scatter_x, 3), (gather_h, 2), (scatter_n, 2),
                             (gather_y, 1), (gather_h, 3), (scatter_n, 3), (gather_y, 2), (gather_y, 3)):
                stage(h)

        @block.tensor
        def _(pe):
            mm = nc.tensor.matmul
            pe.wait_ge(R["w_in"], 32)

            def x_transposes(n):
                pe.wait_ge(xs_in[n % 3], 16 * (n // 3 + 1))
                if n >= 1:
                    pe.wait_ge(xt_done, n)
                for e in range(EB):
                    tr = nc.tensor.transpose(pX[:, e * ROWS:(e + 1) * ROWS], XS[n % 3][:, e, :], ident[0:ROWS, 0:ROWS])
                tr.then_inc(xt_mm, 1)

            def h_free(key):
                n = ring[key]
                if n >= 2:
                    h_wait(pe, n - 2)
                return pH[n % 2]

            def y_block(n):
                h, eb = n // NB, n % NB
                for c in range(FC):
                    m = FC * n + c
                    if m >= 2:
                        pe.wait_ge(ht_done, m - 1)
                    for e in range(EB):
                        l = 2 * n + e // 2
                        if c == 0 and e % 2 == 0:
                            pe.wait_ge(hl_in[l % 3], 16 * (l // 3 + 1))
                        tr = nc.tensor.transpose(pN[m % 2][:, e * ROWS:(e + 1) * ROWS],
                                                 HL[l % 3][:, e % 2, c * P:(c + 1) * P], ident[0:ROWS, 0:ROWS])
                    tr.then_inc(hn_mm, 1)
                if n >= 1:
                    pe.wait_ge(ys_done, n)
                for c in range(FC):
                    pe.wait_ge(ht_done, FC * n + c + 1)
                    for e in range(EB):
                        last = mm(pY[0:ROWS, e * D:(e + 1) * D], HT[c][:, e * ROWS:(e + 1) * ROWS],
                                  W2[:, eb * EB + e, c, :], start=c == 0 and e == 0, stop=c == FC - 1,
                                  skip_group_check=True)
                    last.then_inc(y_mm, 1)

            for s, h in ORDER:
                if s == "u":
                    x_transposes(h * NB)
                    for eb in range(NB):
                        n = h * NB + eb
                        if eb + 1 < NB:
                            x_transposes(n + 1)
                        pe.wait_ge(xt_done, n + 1)
                        for e in range(EB):
                            mm(h_free(("u", h, eb * EB + e))[0:ROWS, :], XT[n % 2][:, e * ROWS:(e + 1) * ROWS],
                               W1[:, eb * EB + e, :], start=True, stop=True).then_inc(h_mm, 1)
                if s == "b":
                    if h == 0:
                        pe.wait_ge(w_in, 64)
                    for half in range(2):
                        if h >= 1:
                            pe.wait_ge(b2_read, 2 * h)
                        for j in range(4):
                            tr = nc.tensor.transpose(pG[half][0:NE, j * P:(j + 1) * P],
                                                     GD[:, tile_of(h, 4 * half + j), :], ident[:])
                        tr.then_inc(gt_mm, 1)
                    pe.wait_ge(gt_done, 2 * h + 2)
                    for half in range(2):
                        for j in range(4):
                            i = 4 * half + j
                            last = mm(pG[half][:, j * P:(j + 1) * P], GTT[:, i * P:(i + 1) * P], b2[:],
                                      start=True, stop=True)
                        last.then_inc(b2_mm, 1)
                    for i in range(GT):
                        mm(h_free(("b", h, i))[:], GTT[:, i * P:(i + 1) * P], b1[:],
                           start=True, stop=True).then_inc(h_mm, 1)
                if s == "w":
                    for eb in range(NB):
                        y_block(h * NB + eb)

        @block.scalar
        def _(act):
            def xt(n):
                act.wait_ge(xt_mm, n + 1)
                if n >= 2:
                    act.wait_ge(h_mm, ring["u", (n - 2) // NB, (n - 2) % NB * EB + EB - 1] + 1)
                nc.scalar.copy(XT[n % 2][:], pX[:, 0:EB * ROWS]).then_inc(xt_done, 1)

            for s, h in ORDER:
                if s == "u":
                    xt(h * NB)
                    for eb in range(NB):
                        if eb + 1 < NB:
                            xt(h * NB + eb + 1)
                        for e in range(EB):
                            m = h * NE + eb * EB + e
                            r = ring["u", h, eb * EB + e]
                            act.wait_ge(h_mm, r + 1)
                            if m >= NHS:
                                act.wait_ge(hs_out[m % NHS], 16 * (m // NHS))
                            nc.scalar.copy(HS[m % NHS][:], pH[r % 2][0:ROWS, :]).then_inc(hs_done, 1)
                if s == "b":
                    for half in range(2):
                        act.wait_ge(gt_mm, 2 * h + half + 1)
                        nc.scalar.copy(GTT[:, half * CH:(half + 1) * CH], pG[half][0:NE, :]).then_inc(gt_done, 1)
                    if h >= 1:
                        act.wait_ge(n_sent[h - 1], 2 * GT * 16)
                    for i in range(GT):
                        r = ring["b", h, i]
                        act.wait_ge(h_mm, r + 1)
                        nc.scalar.copy(TT[:, i, :], pH[r % 2][:]).then_inc(t_bias, 1)
                if s == "w":
                    if h == 0:
                        act.wait_ge(w_in, 64)
                    for eb in range(NB):
                        n = h * NB + eb
                        for c in range(FC):
                            m = FC * n + c
                            act.wait_ge(hn_mm, m + 1)
                            if n >= 1:
                                act.wait_ge(y_mm, FC * (n - 1) + c + 1)
                            nc.scalar.activation(HT[c][:], pN[m % 2][:, 0:EB * ROWS], ACT.Relu,
                                                 bias=lnh[:, 1, h, c:c + 1], scale=lnh[:, 0, h, c:c + 1]
                                                 ).then_inc(ht_done, 1)
                        act.wait_ge(y_mm, FC * n + FC)
                        if n >= 2:
                            act.wait_ge(ys_out[n % 2], 16 * (n // 2))
                        nc.scalar.copy(YS[n % 2][:], pY[0:ROWS, :].rearrange("p (e d) -> p e d", e=EB)
                                       ).then_inc(ys_done, 1)
            for n, eps in enumerate((R["c_ln_eps"], R["c_eps"])):
                act.wait_ge(var_done, n + 1)
                nc.scalar.activation(r1[:], v128[:], ACT.Sqrt, bias=eps, scale=1.0 / D).then_inc(std_done, 1)

        @block.vector
        def _(v):
            c = Chain(v, vs)
            group = lambda ap, h: ap.rearrange("p (b h r) d -> p b h r d", b=B, h=GR)[:, :, h, :, :]

            def combine(h):
                v.wait_ge(sent[h], 2 * GT * 16)
                for half in range(2):
                    v.wait_ge(b2_mm, 2 * h + half + 1)
                    y = Yn.rearrange("p (b h r) d -> p b h (r d)", b=B, h=GR)[:, 2 * half:2 * half + 2, h, :]
                    nc.vector.tensor_tensor(y, y, pG[half][:].rearrange("p (b q) -> p b q", b=2),
                                            ALU.add).then_inc(b2_read, 1)
                for i in range(GT):
                    t, n = tile_of(h, i), h * GT + i
                    v.wait_ge(t_bias, n + 1)
                    v.wait_ge(ga_in[n % 2], 32 * (n // 2 + 1))
                    c.run(nc.vector.scalar_tensor_tensor(TT[:, i, :], GA[n % 2][0][:], gate[:, t, 0:1], TT[:, i, :],
                                                         ALU.mult, ALU.add))
                    nc.vector.scalar_tensor_tensor(TT[:, i, :], GA[n % 2][1][:], gate[:, t, 1:2], TT[:, i, :],
                                                   ALU.mult, ALU.add).then_inc(c_read, 1)
                    v.wait_ge(c_read, n + 1)
                    c.mark(nc.vector.bn_stats(st[:, i, :], TT[:, i, :]))
                c.wait()
                c.run(finish_stats(nc, c, st[:], mean[:], v128[:], t1[:], t2[:], FF))
                rsqrt(nc, c, v128[:], r1[:], t1[:], 1.0 / FF, LN_EPS)
                for i in range(GT):
                    nc.vector.tensor_scalar(TT[:, i, :], TT[:, i, :], mean[:, i:i + 1], r1[:, i:i + 1],
                                            ALU.subtract, ALU.mult).then_inc(n_done, 1)

            def normalise(h, eps):
                for i in range(GT):
                    c.mark(nc.vector.bn_stats(st[:, i, :], Yn[:, tile_of(h, i), :]))
                c.wait()
                last = finish_stats(nc, c, st[:], mean[:], v128[:], t1[:], t2[:], D)
                if h < GR - 1:
                    c.run(last)
                    rsqrt(nc, c, v128[:], r1[:], t1[:], 1.0 / D, eps)
                else:
                    last.then_inc(var_done, 1)
                    v.wait_ge(std_done, 1 if eps == LN_EPS else 2)
                    c.run(nc.vector.reciprocal(r1[:], r1[:]))
                for i in range(GT):
                    y = Yn[:, tile_of(h, i), :]
                    c.mark(nc.vector.tensor_scalar(y, y, mean[:, i:i + 1], r1[:, i:i + 1], ALU.subtract, ALU.mult))
                c.wait()

            def output(h):
                for i in range(GT):
                    t, n = tile_of(h, i), h * GT + i
                    v.wait_ge(ya_in[n % 2], 32 * (n // 2 + 1))
                    c.run(nc.vector.scalar_tensor_tensor(Yn[:, t, :], YA[n % 2][0][:], gate[:, t, 0:1], Yn[:, t, :],
                                                         ALU.mult, ALU.add))
                    nc.vector.scalar_tensor_tensor(Yn[:, t, :], YA[n % 2][1][:], gate[:, t, 1:2], Yn[:, t, :],
                                                   ALU.mult, ALU.add).then_inc(y_read, 1)
                v.wait_ge(y_read, (h + 1) * GT)
                normalise(h, LN_EPS)
                for k, op in ((0, ALU.mult), (1, ALU.add)):
                    for b in range(B):
                        y = Yn[:, b * TB + 2 * h:b * TB + 2 * h + 2, :]
                        c.mark(nc.vector.tensor_tensor(y, y, lno[:, k:k + 1, :].broadcast_to([P, 2, D]), op))
                    c.wait()
                normalise(h, EPS)
                x = group(X[:], h).rearrange("p b r d -> p b (r d)")
                nc.vector.tensor_tensor(x, x, group(Yn, h).rearrange("p b r d -> p b (r d)"), ALU.add
                                        ).then_inc(o_done, 1)

            v.wait_ge(w_in, 64)
            for stage, h in ((combine, 0), (combine, 1), (output, 0), (combine, 2), (output, 1), (combine, 3),
                             (output, 2), (output, 3)):
                stage(h)


def experts(nc, R, A, out):
    with ExitStack() as ctx:
        sb = lambda n, s, d=F32: ctx.enter_context(nc.sbuf_tensor(n, s, d))
        R["sent"] = [ctx.enter_context(nc.semaphore(f"sent{h}")) for h in range(GR)]
        R["GD"] = sb("gates_dense", [P, T, NE])
        R["gate"] = sb("gate", [P, T, 2])[:]
        R["take"], R["send"] = sb("take", [P, T, 2], I32)[:], sb("send", [P, T, 2], I32)[:]
        DR = {"x": R["x_rows"], "out": out,
              "h": [nc.dram_tensor(f"h_rows{h}", (NE, ROWS, FF), F32, kind="Internal").ap() for h in range(GR)],
              "y": [nc.dram_tensor(f"y_rows{h}", (NE, ROWS, D), F32, kind="Internal").ap() for h in range(GR)]}
        routing(nc, R, A)
        expert_layers(nc, R, A, DR)



def build(nc, A, out):
    with ExitStack() as ctx:
        sb = lambda n, s, d=F32: ctx.enter_context(nc.sbuf_tensor(n, s, d))
        consts = sb("consts", [P, 8])
        R = {
            "X": sb("x_res", [P, T, D]), "ident": sb("ident", [P, P]), "ones": sb("ones", [P, P]),
            "c_eps": consts[:, 0:1], "c_eps2": consts[:, 1:2], "c_ln_eps": consts[:, 2:3],
        }
        with nc.sbuf_tensor("up_t", [P, FF], F32) as R["up_t"], nc.sbuf_tensor("down_t", [P, FF], F32) as R["down_t"]:
            first_attention(nc, R, A)
            feed_forward(nc, R, A)
        flag = sb("flag", [1, 8], I32)
        R["flag"] = flag[0:1, 0:1]
        R["V"] = sb("v_all", [P, UNITS, TB, 32])
        S = {n: nc.dram_tensor(f"stack_{n}", (B, P, NQ, 2, L), BF16, kind="Internal").ap() for n in "qk"}
        second_projections(nc, R, A, S)
        exact_maxima(nc, R, S)
        R["w_in"], R["zero_out"] = (ctx.enter_context(nc.semaphore(n)) for n in ("experts_in", "zero_out"))
        R["W1"], R["W2"] = sb("w_1", [P, NE, FF]), sb("w_2", [P, NE, FC, D])
        R["x_rows"] = [nc.dram_tensor(f"x_rows{h}", (NE, ROWS, D), F32, kind="Internal").ap() for h in range(GR)]
        R["Yn"] = R["V"][:].rearrange("p n t e -> p (n t e)").rearrange("p (t d) -> p t d", d=D)
        R["EX"], R["eidx"] = sb("gate_exponents", [P, T, NE + 1])[:], sb("experts_chosen", [P, T, 2])[:]
        second_scores(nc, R, A, S)
        experts(nc, R, A, out)


def layout(inputs):
    a = {k: np.asarray(v) for k, v in inputs.items()}
    f = lambda z: np.ascontiguousarray(z, dtype=np.float32)
    w, bq = a["L0_attn_qkv_w"], a["L0_attn_qkv_b"]
    got = {
        "x": f(a["L0_attn_x"].reshape(B * L, D)),
        "wq_t": f(w[0:D].T), "wk_t": f(w[D:2 * D].T), "wv": f(w[2 * D:]), "wv_t": f(w[2 * D:].T),
        "proj_t": f(a["L0_attn_proj_w"].T),
        "norm_w": f(a["L0_attn_norm_w"][:, None]), "norm_b": f(a["L0_attn_norm_b"][:, None]),
        "bv": f(bq[2 * D:, None]),
        "rows": f(np.stack([bq[0:D], bq[D:2 * D], a["L0_attn_proj_b"]])[None]),
        "w_up": f(a["L0_ffn_w_up"].T),
        "w_down": f(a["L0_ffn_w_down"].T.reshape(FC, P, D).transpose(1, 0, 2).reshape(P, FF)),
    }
    a2, dim, n, pair = np.meshgrid(range(2), range(8), range(4), range(2), indexing="ij")
    head = (4 * n + 2 * pair + a2).ravel()
    dim = dim.ravel()
    rows_a = 8 * head + 2 * (dim % 4) + dim // 4
    rows_b = 8 * head + 2 * (dim % 4) + 1 - dim // 4
    order = [("Wq", "bq", rows_a), ("Wq", "bq", rows_b), ("Wk", "bk", rows_a), ("Wk", "bk", rows_b)]
    got["w_ab"] = f(np.stack([a["L1_attn_" + w][r].T for w, _, r in order], axis=1))
    got["b_ab"] = f(np.stack([a["L1_attn_" + c][r] for _, c, r in order], axis=1))
    inv = (np.float32(1) / np.power(np.float32(10000), np.arange(0, HD, 2, dtype=np.float32) / np.float32(HD)))
    angle = np.outer(np.arange(L, dtype=np.float32), inv).astype(np.float32)
    sign = np.where(dim < 4, -1, 1).astype(np.float32)[:, None]
    got["cos_sin"] = f(np.stack([np.cos(angle)[:, dim % 4].T, sign * np.sin(angle)[:, dim % 4].T], axis=1))
    got["head_sum"] = ((8 * a2 + 2 * n + pair).reshape(P, 1) == np.arange(HEADS)).astype(mybir.dt.np(BF16))
    got["ones_row"] = np.ones((3, 2 * L), mybir.dt.np(BF16))
    got["wv1_t"] = f(a["L1_attn_Wv"].T)
    got["bv1"] = f(a["L1_attn_bv"])
    got["wo_t"] = f(a["L1_attn_Wo"].T)
    got["bo"] = f(a["L1_attn_bo"])
    got["w_gate"] = f(a["L1_ffn_Wg"])
    got["w1"] = f(a["L1_ffn_W1"])
    got["w2"] = f(a["L1_ffn_W2"])
    got["b1"], got["b2"] = f(a["L1_ffn_b1"]), f(a["L1_ffn_b2"])
    ln = np.stack([a["L1_ffn_ln_hid_w"], a["L1_ffn_ln_hid_b"]])
    got["ln_hid"] = f(ln.reshape(2, GR, FC, P).transpose(3, 0, 1, 2))
    got["ln_out"] = f(np.stack([a["L1_ffn_ln_out_w"], a["L1_ffn_ln_out_b"]]))
    return got


def kernel(**inputs):
    import concourse.bacc as bacc
    from concourse.bass_utils import run_bass_kernel_spmd as run

    nc = bacc.Bacc("TRN2", target_bir_lowering=False, num_devices=1)
    arrays = layout(inputs)
    A = {k: nc.dram_tensor(f"in_{k}", z.shape, mybir.dt.from_np(z.dtype), kind="ExternalInput").ap()
         for k, z in arrays.items()}
    out = nc.dram_tensor("out_x", (B * L, D), F32, kind="ExternalOutput").ap()
    build(nc, A, out)
    r = run(nc, [{f"in_{k}": z for k, z in arrays.items()}], core_ids=[0])
    return r.results[0]["out_x"].reshape(B, L, D)
```
